# Optimizing a Trainium2 kernel written in Bass

```python
import numpy as np
import jax
import jax.numpy as jnp

def _softmax(x, axis=-1):
    return jax.nn.softmax(x, axis=axis)

def _gelu(x):
    return jax.nn.gelu(x, approximate=True)

def _silu(x):
    return jax.nn.silu(x)

def _sigmoid(x):
    return jax.nn.sigmoid(x)

def _layernorm(x, axis=-1, eps=1e-05):
    m = jnp.mean(x, axis=axis, keepdims=True)
    v = jnp.var(x, axis=axis, keepdims=True)
    return (x - m) / jnp.sqrt(v + eps)

def _scatter_add(tgt, idx, src, axis=0):
    return tgt.at[idx].add(src)

def _segment_sum(src, seg, n):
    return jax.ops.segment_sum(src, seg, n)
kernel_name = 'mk_flamingo_gated_d1_seqx_r2_455e0b'

def setup_inputs(seed: int=0):
    np.random.seed(seed)
    _w = jnp.asarray

    def _rec_inputs():
        import jax
        import jax.numpy as jnp
        _rk = jax.random.key(seed)
        x = -0.0002928 + 1 * jax.random.normal(jax.random.fold_in(_rk, 1), (16, 100, 512), jnp.float32)
        _lenS = 100 - jax.random.randint(jax.random.fold_in(_rk, 7), (16,), 0, max(1, 100 // 4) + 1, jnp.int32)
        _lenS2 = 722 - jax.random.randint(jax.random.fold_in(_rk, 8), (16,), 0, max(1, 722 // 4) + 1, jnp.int32)
        _ctx_1024P = jax.random.normal(jax.random.fold_in(_rk, 11), (16, 16, 512), jnp.float32)
        _ctx_1024c = jax.random.dirichlet(jax.random.fold_in(_rk, 511), 0.3 * jnp.ones((16,), jnp.float32), (16, 722))
        _ctx_1024t = jnp.einsum('bsk,bkd->bsd', _ctx_1024c, _ctx_1024P)
        _ctx_1024t = _ctx_1024t * jax.lax.rsqrt(jnp.mean(jnp.square(_ctx_1024t)) + 1e-12) * 0.953939
        ctx_1024 = -1.39393e-06 + 0.999914 * (_ctx_1024t + 0.3 * jax.random.normal(jax.random.fold_in(_rk, 611), (16, 722, 512), jnp.float32))
        _validS = jnp.arange(100)[None, :] < _lenS[:, None]
        _validS2 = jnp.arange(722)[None, :] < _lenS2[:, None]
        _causal = jnp.tril(jnp.ones((100, 100), dtype=bool))
        mask_Bx1x1xS2_bf0 = jnp.logical_not(jnp.ones((16, 1, 1, 722), dtype=bool))
        _g = jax.random.normal(jax.random.fold_in(_rk, 9001), (2, 1), jnp.float32)
        _g = jnp.sign(_g) * jnp.maximum(jnp.abs(_g), 1.0) + (_g == 0) * 1.0
        g_xattn = _g[0]
        g_ffn = _g[1]
        return (x, ctx_1024, mask_Bx1x1xS2_bf0, g_xattn, g_ffn)
    x, ctx_1024, mask_Bx1x1xS2_bf0, g_xattn, g_ffn = _rec_inputs()

    def _L0_xattn_setup():
        import jax, jax.numpy as jnp
        import numpy as np
        D_MODEL = 512
        NUM_HEADS = 16
        D_K = D_MODEL // NUM_HEADS
        key = jax.random.key(seed)
        ks = jax.random.split(key, 12)
        B, L = (2, 1024)
        s = 1.0 / np.sqrt(D_MODEL)
        inp = {'q': jax.random.normal(ks[0], (B, L, D_MODEL), jnp.float32), 'k': jax.random.normal(ks[1], (B, L, D_MODEL), jnp.float32), 'v': jax.random.normal(ks[2], (B, L, D_MODEL), jnp.float32), 'mask': jnp.zeros((B, 1, 1, L), dtype=bool), 'W_q': jax.random.normal(ks[3], (D_MODEL, D_MODEL), jnp.float32) * s, 'b_q': jnp.zeros((D_MODEL,), jnp.float32), 'W_k': jax.random.normal(ks[4], (D_MODEL, D_MODEL), jnp.float32) * s, 'b_k': jnp.zeros((D_MODEL,), jnp.float32), 'W_v': jax.random.normal(ks[5], (D_MODEL, D_MODEL), jnp.float32) * s, 'b_v': jnp.zeros((D_MODEL,), jnp.float32), 'W_o': jax.random.normal(ks[6], (D_MODEL, D_MODEL), jnp.float32) * s, 'b_o': jnp.zeros((D_MODEL,), jnp.float32)}
        return inp
    _L0_xattn_all = _L0_xattn_setup()
    _L0_xattn_in = {k: v for k, v in _L0_xattn_all.items() if k in ('W_q', 'b_q', 'W_k', 'b_k', 'W_v', 'b_v', 'W_o', 'b_o')}
    del _L0_xattn_all

    def _L0_ffn_setup():
        import jax, jax.numpy as jnp
        import numpy as np
        from jax import lax
        D = 512
        H = 2048
        E = 8
        TOPK = 2
        key = jax.random.key(seed)
        ks = jax.random.split(key, 7)
        s = 0.02
        return {'x': jax.random.normal(ks[0], (2, 1024, D), dtype=jnp.float32), 'W1': jax.random.normal(ks[1], (E, D, H), dtype=jnp.float32) * s, 'b1': jnp.zeros((E, H), dtype=jnp.float32), 'W2': jax.random.normal(ks[2], (E, H, D), dtype=jnp.float32) * s, 'b2': jnp.zeros((E, D), dtype=jnp.float32), 'Wr': jax.random.normal(ks[3], (D, E), dtype=jnp.float32) * s, 'br': jnp.zeros((E,), dtype=jnp.float32)}
    _L0_ffn_all = _L0_ffn_setup()
    _L0_ffn_in = {k: v for k, v in _L0_ffn_all.items() if k in ('W1', 'b1', 'W2', 'b2', 'Wr', 'br')}
    del _L0_ffn_all
    return {'x': x, 'ctx_1024': ctx_1024, 'mask_Bx1x1xS2_bf0': mask_Bx1x1xS2_bf0, 'g_xattn': g_xattn, 'g_ffn': g_ffn, 'L0_xattn_W_q': _L0_xattn_in['W_q'], 'L0_xattn_b_q': _L0_xattn_in['b_q'], 'L0_xattn_W_k': _L0_xattn_in['W_k'], 'L0_xattn_b_k': _L0_xattn_in['b_k'], 'L0_xattn_W_v': _L0_xattn_in['W_v'], 'L0_xattn_b_v': _L0_xattn_in['b_v'], 'L0_xattn_W_o': _L0_xattn_in['W_o'], 'L0_xattn_b_o': _L0_xattn_in['b_o'], 'L0_ffn_W1': _L0_ffn_in['W1'], 'L0_ffn_b1': _L0_ffn_in['b1'], 'L0_ffn_W2': _L0_ffn_in['W2'], 'L0_ffn_b2': _L0_ffn_in['b2'], 'L0_ffn_Wr': _L0_ffn_in['Wr'], 'L0_ffn_br': _L0_ffn_in['br']}

def reference(x, ctx_1024, mask_Bx1x1xS2_bf0, g_xattn, g_ffn, L0_xattn_W_q, L0_xattn_b_q, L0_xattn_W_k, L0_xattn_b_k, L0_xattn_W_v, L0_xattn_b_v, L0_xattn_W_o, L0_xattn_b_o, L0_ffn_W1, L0_ffn_b1, L0_ffn_W2, L0_ffn_b2, L0_ffn_Wr, L0_ffn_br):
    import jax
    import jax.numpy as jnp

    def _L0_xattn_ref(q, k, v, mask, W_q, b_q, W_k, b_k, W_v, b_v, W_o, b_o):
        import jax, jax.numpy as jnp
        import numpy as np
        D_MODEL = 512
        NUM_HEADS = 16
        D_K = D_MODEL // NUM_HEADS
        B, Lq, _ = q.shape
        Lk = k.shape[1]
        scale = jnp.sqrt(jnp.asarray(D_K, q.dtype))
        Q = (q @ W_q.T + b_q).reshape(B, Lq, NUM_HEADS, D_K).transpose(0, 2, 1, 3)
        K = (k @ W_k.T + b_k).reshape(B, Lk, NUM_HEADS, D_K).transpose(0, 2, 1, 3)
        V = (v @ W_v.T + b_v).reshape(B, Lk, NUM_HEADS, D_K).transpose(0, 2, 1, 3)
        scores = jnp.einsum('bhqd,bhkd->bhqk', Q, K) / scale
        scores = jnp.where(mask, -jnp.inf, scores)
        attn = jax.nn.softmax(scores, axis=-1)
        out = jnp.einsum('bhqk,bhkd->bhqd', attn, V)
        out = out.transpose(0, 2, 1, 3).reshape(B, Lq, D_MODEL)
        return out @ W_o.T + b_o

    def _L0_ffn_ref(x, W1, b1, W2, b2, Wr, br):
        import jax, jax.numpy as jnp
        import numpy as np
        from jax import lax
        D = 512
        H = 2048
        E = 8
        TOPK = 2
        B, S, _ = x.shape
        xf = x.reshape(-1, D)
        logits = xf @ Wr + br
        topv, _ = lax.top_k(logits, TOPK)
        thresh = topv[:, TOPK - 1:TOPK]
        masked = jnp.where(logits >= thresh, logits, -jnp.inf)
        weights = jax.nn.softmax(masked, axis=-1)
        h = jax.nn.gelu(jnp.einsum('td,edh->eth', xf, W1) + b1[:, None, :], approximate=False)
        expert_out = jnp.einsum('eth,ehd->etd', h, W2) + b2[:, None, :]
        out = jnp.einsum('etd,te->td', expert_out, weights)
        return out.reshape(B, S, D)
    x = x + jnp.tanh(g_xattn[0]) * _L0_xattn_ref(_layernorm(x, axis=-1), ctx_1024, ctx_1024, mask_Bx1x1xS2_bf0, L0_xattn_W_q, L0_xattn_b_q, L0_xattn_W_k, L0_xattn_b_k, L0_xattn_W_v, L0_xattn_b_v, L0_xattn_W_o, L0_xattn_b_o)
    x = x + jnp.tanh(g_ffn[0]) * _L0_ffn_ref(_layernorm(x, axis=-1), L0_ffn_W1, L0_ffn_b1, L0_ffn_W2, L0_ffn_b2, L0_ffn_Wr, L0_ffn_br)
    return x

_drawn_inputs = setup_inputs


def setup_inputs(seed=0):
    import zlib

    import numpy as np

    out = dict(_drawn_inputs(seed))
    spreads = {'L0_xattn_b_q': (0.0, 0.338),
     'L0_xattn_b_k': (0.0, 0.8),
     'L0_xattn_b_v': (0.0, 0.1),
     'L0_xattn_b_o': (0.0, 0.1),
     'L0_ffn_b1': (0.0, 0.1),
     'L0_ffn_b2': (0.0, 0.1),
     'L0_ffn_br': (0.0, 0.1)}
    factors = {}
    for name, (base, spread) in spreads.items():
        noise = np.random.default_rng([zlib.crc32(name.encode()), seed]).standard_normal(out[name].shape)
        drawn = base * np.exp(spread * noise) if base else spread * noise
        out[name] = jnp.asarray(drawn.astype(out[name].dtype))
    for name, factor in factors.items():
        out[name] = (out[name] * factor).astype(out[name].dtype)
    return out
```

```python
from contextlib import ExitStack

import concourse.bass as bass
from concourse import mybir

B, LQ, D = 16, 100, 512
S = 722
H, DK = 16, 32
E, HID = 8, 2048
EPS = 1e-5
SCALE = float(DK) ** -0.5

P = 128
DC = D // P
KT = 122
NT = 6
SP_ = KT * NT
HALF = SP_ // 2
HT = NT // 2
REAL = (HALF, S - HALF)
GH = P // DK
NG = H // GH
NQ = GH * LQ
UK = DC
UH = UK + HT
SLOTS = 512
ROUNDS = 4
ROWS = SLOTS * ROUNDS
NS = SLOTS // P
NJ = HID // P
RAW = 4
RING = 4
MASKED = -3.0e38
OOB = float(1 << 20)

ALU = mybir.AluOpType
ACT = mybir.ActivationFunctionType
AX = mybir.AxisListType
F32 = mybir.dt.float32
F32R = mybir.dt.float32r
BF16 = mybir.dt.bfloat16
I32 = mybir.dt.int32
U8 = mybir.dt.uint8

T_PRO = ["xT", "Q", "QT", "bc3"]
T_0 = ["xT", "bc0", "Q", "bc1", "QT", "bc2", "bc3"]
T_MID = ["op", "xT", "bc0", "Q", "rT", "bc1", "rm", "QT", "bc2", "pos", "bc3"]
T_LAST = ["op", "bc0", "rT", "bc1", "rm", "bc2", "pos"]
T_EPI = ["op", "rT", "rm", "pos"]


def t_index(b, kind, name):
    if kind == "pro":
        return T_PRO.index(name)
    if kind == "first":
        return len(T_PRO) + T_0.index(name)
    if kind == "epi":
        return len(T_PRO) + len(T_0) + (B - 2) * len(T_MID) + len(T_LAST) + T_EPI.index(name)
    order = T_MID if kind == "mid" else T_LAST
    return len(T_PRO) + len(T_0) - len(T_MID) + len(T_MID) * b + order.index(name)


def f32(ap):
    return ap.bitcast(F32)


def wait(eng, sem, value):
    if isinstance(value, int) and value <= 0:
        return
    eng.wait_ge(sem, value)


def alone(eng, passed):
    eng.sem_inc(passed, 1)


class Chain:

    def __init__(self, eng, sem, base, passed=None):
        self.eng, self.sem, self.base, self.n, self.passed = eng, sem, base, 0, passed

    def then(self, ins):
        ins.then_inc(self.sem, 1)
        self.n += 1

    def link(self, ins):
        self.then(ins)
        self.eng.wait_ge(self.sem, self.base + self.n)
        if self.passed is not None:
            alone(self.eng, self.passed)


def attention_phase(nc, A):
    with ExitStack() as ctx:
        def sb(name, shape, dt=F32):
            return ctx.enter_context(nc.sbuf_tensor(name, shape, dt))

        def sem(name):
            return ctx.enter_context(nc.semaphore(name))

        wkh, wkl = sb("wkh", [P, DC, D], F32R), sb("wkl", [P, DC, D], F32R)
        wvh, wvl = sb("wvh", [P, DC, D], F32R), sb("wvl", [P, DC, D], F32R)
        wqh, wql = sb("wqh", [P, DC, D], F32R), sb("wql", [P, DC, D], F32R)
        wo = sb("wo", [P, DC, D])
        kh = [sb(f"kh{i}", [P, NG, SP_], F32R) for i in range(2)]
        kl = [sb(f"kl{i}", [P, NG, SP_], F32R) for i in range(2)]
        vv = [sb(f"vv{i}", [KT, NT, D]) for i in range(2)]
        craw = sb("craw", [P, DC, HALF])
        ch = [sb(f"ch{i}", [P, DC, HALF], F32R) for i in range(2)]
        cl = [sb(f"cl{i}", [P, DC, HALF], F32R) for i in range(2)]
        prob = sb("prob", [P, NT, NQ])
        acc = sb("acc", [KT, 2, NQ])
        shift = sb("shift", [KT, NQ])
        diag = sb("diag", [LQ, GH, LQ], F32R)
        mx = sb("mx", [LQ, GH])
        junk = sb("junk", [LQ, 2, HALF], BF16)
        qbh, qbl = sb("qbh", [P, GH, LQ], F32R), sb("qbl", [P, GH, LQ], F32R)
        qt = sb("qt", [P, NG, LQ])
        qth, qtl = sb("qth", [P, NG, LQ], F32R), sb("qtl", [P, NG, LQ], F32R)
        qs = sb("qs", [LQ, D])
        xn = sb("xn", [LQ, D])
        xth, xtl = sb("xth", [P, DC, LQ], F32R), sb("xtl", [P, DC, LQ], F32R)
        rden = sb("rden", [P, LQ])
        ot = sb("ot", [P, NG, LQ])
        x1 = sb("x1", [LQ, D])
        xn2 = sb("xn2", [LQ, D])
        x2t = qt
        mrow8 = sb("mrow8", [LQ, SP_], U8)
        mrow = [sb(f"mrow{i}", [LQ, 2, HALF], BF16) for i in range(2)]
        mkey8 = sb("mkey8", [KT, B * NT], U8)
        mkey = sb("mkey", [KT, B * NT])
        ident, tri = sb("ident", [P, P]), sb("tri", [LQ, LQ])
        blockm = sb("blockm", [P, GH, LQ])
        rankc = sb("rankc", [LQ, E, E])
        rankv = sb("rankv", [LQ, E])
        rowbase = sb("rowbase", [LQ, E])
        ones = sb("ones", [P, P])
        onesr = sb("onesr", [LQ, P], F32R)
        gbo = sb("gbo", [LQ, D])
        bq, bk, bv = sb("bq", [P, NG]), sb("bk", [P, NG]), sb("bv", [P, NG])
        wr = sb("wr", [P, DC, E])
        br = sb("br", [LQ, E])
        gx = sb("gx", [P, 2])
        tg = sb("tg", [P, 2])
        st = sb("st", [LQ, 6])
        mv = sb("mv", [LQ, 2])
        rstd, rs2 = sb("rstd", [LQ, 1]), sb("rs2", [LQ, 1])
        mhalf = sb("mhalf", [LQ, 1])
        st2 = sb("st2", [LQ, 6])
        mv2 = sb("mv2", [LQ, 2])
        lg, m8, nm1 = sb("lg", [LQ, E]), sb("m8", [LQ, 8]), sb("nm1", [LQ, 1])
        ex, sel, cum = sb("ex", [LQ, E]), sb("sel", [LQ, E]), sb("cum", [LQ, E])
        zero8 = sb("zero8", [LQ, E])
        we, wsum, wgt = sb("we", [LQ, E]), sb("wsum", [LQ, 1]), sb("wgt", [LQ, E])
        seen, slot = sb("seen", [LQ, E]), sb("slot", [LQ, E])
        sk, skv = sb("sk", [LQ, E, E]), sb("skv", [LQ, E, E])
        idf, gone = sb("idf", [LQ, E]), sb("gone", [LQ, E])
        idx = sb("idx", [LQ, 2], I32)
        act32, base32 = sb("act32", [1, E * ROUNDS]), sb("base32", [1, E * ROUNDS])
        thr32, zero32 = sb("thr32", [1, E * ROUNDS]), sb("zero32", [1, E * ROUNDS])
        unit32 = sb("unit32", [1, E * ROUNDS])
        cnt32 = sb("cnt32", [1, E * ROUNDS])

        pa = [ctx.enter_context(nc.psum_tensor(f"pa{i}", [P, 512], F32)) for i in range(2)]
        psc = [ctx.enter_context(nc.psum_tensor(f"psc{i}", [P, 512], F32)) for i in range(2)]
        pm = ctx.enter_context(nc.psum_tensor("pm", [P, 2, 512], F32))
        po = ctx.enter_context(nc.psum_tensor("po", [P, 512], F32))
        pt = ctx.enter_context(nc.psum_tensor("pt", [P, 512], F32))

        def s_bank(t):
            return pm[0:KT, t - 2, 0:NQ] if t in (2, 3) else psc[t % 2][0:KT, 0:NQ]

        w_in = [sem(f"w_in_{n}") for n in "kvqo"]
        const_in, c_in, x_in = sem("const_in"), sem("c_in"), sem("x_in")
        m_in, xres_in = sem("m_in"), sem("xres_in")
        row_out, x1_out, xn2_out, zero_out = sem("row_out"), sem("x1_out"), sem("xn2_out"), sem("zero_out")
        w_hi, w_lo = sem("w_hi"), sem("w_lo")
        setup_act, setup_dve, setup_pool = sem("setup_act"), sem("setup_dve"), sem("setup_pool")
        c_hi, c_lo = sem("c_hi"), sem("c_lo")
        proj_ready, k_hi, k_lo, v_copy = sem("proj_ready"), sem("k_hi"), sem("k_lo"), sem("v_copy")
        s_ready, s_used, p_ready = sem("s_ready"), sem("s_used"), sem("p_ready")
        max_ready, max_used, diag_ready, shift_ready = sem("max_ready"), sem("max_used"), sem("diag_ready"), sem("shift_ready")
        qb_hi, qb_ready, sum_step, pv_done, norm_step = sem("qb_hi"), sem("qb_ready"), sem("sum_step"), sem("pv_done"), sem("norm_step")
        t_ready = sem("t_ready")
        ln1_step, ln1_pow, xt_hi, xt_lo, qs_ready, qt_step = sem("ln1_step"), sem("ln1_pow"), sem("xt_hi"), sem("xt_lo"), sem("qs_ready"), sem("qt_step")
        m_used, xres_ready, x1_ready, ln2_step, ln2_pow = sem("m_used"), sem("xres_ready"), sem("x1_ready"), sem("ln2_step"), sem("ln2_pow")
        x2t_ready, gate_step, gate_exp, pos_step, idx_ready = sem("x2t_ready"), sem("gate_step"), sem("gate_exp"), sem("pos_step"), sem("idx_ready")

        NCONST = 17
        N_LN1, N_LN2, N_GATE, N_POS, N_NORM, N_QT, N_SUM = 3, 3, 7, 9, 3, 3, 3
        block = ctx.enter_context(nc.Block())

        @block.sync
        def _(sp):
            flat = prob[:, :, :].rearrange("p t n -> p (t n)")

            def load_w(n, name):
                wait(sp, w_lo, n)
                sp.dma_start(flat[:, 0:DC * D], A[name].rearrange("p c n -> p (c n)")).then_inc(w_in[n], 16)

            def load_ctx(b, half):
                wait(sp, c_lo, 2 * b + half)
                alone(sp, A["passed"])
                sp.dma_start(craw[:, :, 0:REAL[half]],
                             A["ctx"][bass.ds(b, 1), :, :, half * HALF:half * HALF + REAL[half]]
                             .rearrange("b p c n -> (b p) c n")).then_inc(c_in, 16)

            def load_x(b):
                wait(sp, xt_hi, b)
                alone(sp, A["passed"])
                sp.dma_start(xn[:, :], A["x"][bass.ds(b, 1)].rearrange("b l d -> (b l) d")).then_inc(x_in, 16)

            def load_mask(b):
                wait(sp, m_used, b)
                alone(sp, A["passed"])
                sp.dma_start(mrow8[:, :], A["mrow"][bass.ds(b, 1), :].rearrange("b s -> (b s)")
                             .partition_broadcast(LQ)).then_inc(m_in, 16)

            def load_res(b):
                wait(sp, x1_out, 16 * b)
                alone(sp, A["passed"])
                wait(sp, ln2_step, N_LN2 * b)
                alone(sp, A["passed"])
                sp.dma_start(x1[:, :], A["x"][bass.ds(b, 1)].rearrange("b l d -> (b l) d")).then_inc(xres_in, 16)

            def clear_slots(b):
                wait(sp, zero_out, 16 * b)
                alone(sp, A["passed"])
                sp.dma_start(A["slots"].rearrange("(e n p) d -> n p e d", e=E, p=P)[bass.ds(b, 1)]
                             .rearrange("n p e d -> (n p) e d"),
                             A["zero"][:, :].unsqueeze(1).broadcast_to([P, E, D])).then_inc(zero_out, 16)

            def batch(b):
                load_ctx(b, 0)
                load_x(b)
                load_mask(b)
                load_ctx(b, 1)
                clear_slots(b)

            load_w(0, "wk")
            sp.dma_start(craw[:, :, 0:REAL[0]], A["ctx"][0, :, :, 0:REAL[0]]).then_inc(c_in, 16)
            for dst, src in ((ident, A["ident"]), (tri, A["tri"]), (blockm, A["blockm"]), (rankc, A["rankc"]),
                             (rankv, A["rankv"]), (rowbase, A["rowbase"]), (bq, A["bq"]), (bk, A["bk"]), (bv, A["bv"]),
                             (wr, A["wr"]), (mkey8, A["mkey"]), (thr32, A["thr32"]), (unit32, A["unit32"])):
                sp.dma_start(dst[:], src).then_inc(const_in, 16)
            sp.dma_start(br[:, :], A["br"].partition_broadcast(LQ)).then_inc(const_in, 16)
            sp.dma_start(gbo[:, :], A["bo"].partition_broadcast(LQ)).then_inc(const_in, 16)
            sp.dma_start(gx[:, 0:1], A["gx"].partition_broadcast(P)).then_inc(const_in, 16)
            sp.dma_start(gx[:, 1:2], A["gf"].partition_broadcast(P)).then_inc(const_in, 16)
            load_x(0)
            load_mask(0)
            load_w(1, "wv")
            load_w(2, "wq")
            load_ctx(0, 1)
            sp.dma_start(wo[:, :, :], A["wo"]).then_inc(w_in[3], 16)
            load_res(0)
            sp.wait_ge(setup_pool, 2)
            clear_slots(0)
            batch(1)
            with sp.Fori(2, B) as b:
                batch(b)
                load_res(b - 1)
            load_res(B - 1)

        def pe_units(pe, nxt, half):
            hh = 2 * nxt + half

            def bank(k):
                return pa[(UH * half + k) % 2]

            def unit(k):
                if k == 0:
                    wait(pe, v_copy, HT * hh - 1)
                elif k == 1:
                    wait(pe, v_copy, HT * hh)
                elif k < UK + 2:
                    wait(pe, k_lo, UK * hh + k - 1)
                else:
                    wait(pe, v_copy, HT * hh + k - UK - 1)
                if k == 0:
                    wait(pe, c_lo, hh + 1)
                if k < UK:
                    o = bank(k)[:, 0:HALF]
                    n = 0
                    for c in range(DC):
                        wh, wl = wkh[:, c, k * P:(k + 1) * P], wkl[:, c, k * P:(k + 1) * P]
                        for w, x in ((wh, ch[half]), (wh, cl[half]), (wl, ch[half])):
                            last = pe.matmul(o, w, x[:, c, :], start=(n == 0), stop=(n == 3 * DC - 1))
                            n += 1
                else:
                    t = k - UK
                    o = bank(k)[0:KT, 0:D]
                    n = 0
                    for c in range(DC):
                        xh, xl = ch[half][:, c, t * KT:(t + 1) * KT], cl[half][:, c, t * KT:(t + 1) * KT]
                        for x, w in ((xh, wvh), (xl, wvh), (xh, wvl)):
                            last = pe.matmul(o, x, w[:, c, :], start=(n == 0), stop=(n == 3 * DC - 1))
                            n += 1
                last.then_inc(proj_ready, 1)
            return unit

        @block.tensor
        def _(pe):
            def t_use(b, kind, name):
                order = {"pro": T_PRO, "first": T_0, "mid": T_MID, "last": T_LAST, "epi": T_EPI}[kind]
                at = order.index(name)
                if kind == "pro":
                    b = -1
                    if at == 0:
                        return
                if at:
                    before = order[at - 1]
                elif kind == "epi":
                    before, b = "pos", b - 1
                else:
                    before, b = "bc3", b - 1
                read_by = {"xT": (xt_lo, b + 2), "Q": (qs_ready, b + 2), "QT": (qt_step, N_QT * (b + 1) + 1),
                           "op": (x1_ready, b), "rT": (x2t_ready, b), "rm": (gate_step, N_GATE * (b - 1) + 1),
                           "pos": (pos_step, N_POS * (b - 1) + 2)}
                if before in read_by:
                    pe.wait_ge(*read_by[before])
                else:
                    pe.wait_ge(shift_ready, NG * b + int(before[2]) + 2)

            def x_transposes(b, kind, nxt):
                wait(pe, ln1_step, N_LN1 * (nxt + 1))
                t_use(b, kind, "xT")
                for c in range(DC):
                    last = pe.transpose(pt[:, c * LQ:(c + 1) * LQ], xn[:, c * P:(c + 1) * P], ident[0:LQ, 0:LQ])
                last.then_inc(t_ready, 1)

            def q_product(b, kind, nxt):
                wait(pe, xt_lo, nxt + 1)
                if kind == "pro":
                    wait(pe, w_lo, 3)
                t_use(b, kind, "Q")
                n = 0
                for c in range(DC):
                    for x, w in ((xth, wqh), (xth, wql), (xtl, wqh)):
                        last = pe.matmul(pt[0:LQ, 0:D], x[:, c, :], w[:, c, :], start=(n == 0), stop=(n == 3 * DC - 1))
                        n += 1
                last.then_inc(t_ready, 1)

            def q_transposes(b, kind, nxt):
                wait(pe, qs_ready, nxt + 1)
                t_use(b, kind, "QT")
                for c in range(DC):
                    last = pe.transpose(pt[:, c * LQ:(c + 1) * LQ], qs[:, c * P:(c + 1) * P], ident[0:LQ, 0:LQ])
                last.then_inc(t_ready, 1)

            def max_head(G, kpar, c, h, nxt=None):
                if h == 0:
                    wait(pe, qb_hi, G + 1)
                    if nxt is not None:
                        wait(pe, k_lo, 2 * UK * (nxt + 1))
                    wait(pe, s_used, NT * (G - 1) + 4)
                wait(pe, max_used, GH * G + h)
                for i in range(2):
                    last = pe.matmul(pm[0:LQ, i, 0:HALF], qbh[:, h, :], kh[kpar][:, c, i * HALF:(i + 1) * HALF],
                                     start=True, stop=True)
                last.then_inc(max_ready, 1)

            def broadcast_shift(b, kind, name, G):
                wait(pe, diag_ready, G + 1)
                t_use(b, kind, name)
                pe.matmul(pt[:, 0:NQ], onesr[:, :], diag[:, :, :].rearrange("p h q -> p (h q)"),
                          start=True, stop=True).then_inc(t_ready, 1)

            def scores(b, kind, g, par):
                G = NG * b + g
                wait(pe, qb_ready, G + 1)
                q_h = qbh[:, :, :].rearrange("p h q -> p (h q)")
                q_l = qbl[:, :, :].rearrange("p h q -> p (h q)")
                for t in range(NT):
                    if t in (0, 1):
                        wait(pe, s_used, NT * G + t - 1)
                    elif t in (2, 3):
                        wait(pe, max_used, GH * (G + 1))
                    else:
                        wait(pe, s_used, NT * G + t - 3)
                    if t == 2:
                        if g:
                            broadcast_shift(b, kind, f"bc{g - 1}", G)
                        else:
                            before = {"first": "pro", "mid": "first" if isinstance(b, int) and b == 1 else "mid"}
                            broadcast_shift(b - 1, before.get(kind, "mid"), "bc3", G)
                    k_h, k_l = kh[par][:, g, t * KT:(t + 1) * KT], kl[par][:, g, t * KT:(t + 1) * KT]
                    o = s_bank(t)
                    pe.matmul(o, k_h, q_h, start=True, stop=False)
                    pe.matmul(o, k_h, q_l, start=False, stop=False)
                    pe.matmul(o, k_l, q_h, start=False, stop=True).then_inc(s_ready, 1)

            def weigh_values(b, G, par, c, part):
                if part == 0:
                    if c == 0:
                        wait(pe, v_copy, 2 * HT * (b + 1))
                    wait(pe, norm_step, N_NORM * G)
                wait(pe, p_ready, NT * G + HT * (part + 1))
                for t in range(part * HT, (part + 1) * HT):
                    for h in range(GH):
                        pe.matmul(po[h * DK:(h + 1) * DK, 0:LQ],
                                  vv[par][:, t, c * P + h * DK:c * P + (h + 1) * DK],
                                  prob[0:KT, t, h * LQ:(h + 1) * LQ], start=(t == 0), stop=(t == NT - 1),
                                  tile_position=(0, h * DK))

            def sum_probs(G):
                wait(pe, sum_step, N_SUM * (G + 1))
                for h in range(GH):
                    last = pe.matmul(po[h * DK:(h + 1) * DK, P:P + LQ], ones[0:KT, 0:DK],
                                     acc[:, 0, h * LQ:(h + 1) * LQ], start=True, stop=True,
                                     tile_position=(0, h * DK))
                last.then_inc(pv_done, 1)

            def out_product(b, kind, prev):
                wait(pe, norm_step, N_NORM * NG * (prev + 1))
                t_use(b, kind, "op")
                for c in range(DC):
                    last = pe.matmul(pt[0:LQ, 0:D], ot[:, c, :], wo[:, c, :], start=(c == 0), stop=(c == DC - 1))
                last.then_inc(t_ready, 1)

            def gate_transposes(b, kind, prev):
                wait(pe, ln2_step, N_LN2 * (prev + 1))
                t_use(b, kind, "rT")
                for c in range(DC):
                    last = pe.transpose(pt[:, c * LQ:(c + 1) * LQ], xn2[:, c * P:(c + 1) * P], ident[0:LQ, 0:LQ])
                last.then_inc(t_ready, 1)

            def gate_product(b, kind, prev):
                wait(pe, x2t_ready, prev + 1)
                t_use(b, kind, "rm")
                for c in range(DC):
                    last = pe.matmul(pt[0:LQ, 0:E], x2t[:, c, :], wr[:, c, :], start=(c == 0), stop=(c == DC - 1))
                last.then_inc(t_ready, 1)

            def positions(b, kind, prev):
                wait(pe, gate_step, N_GATE * prev + 3)
                t_use(b, kind, "pos")
                pe.matmul(pt[0:LQ, 0:E], tri[:, :], sel[:, :], start=True, stop=True)
                pe.matmul(pt[0:LQ, E:2 * E], ones[0:LQ, 0:LQ], sel[:, :], start=True, stop=True).then_inc(t_ready, 1)

            def iteration(b, kind, par):
                more, prev = kind != "last", kind != "first"
                for g in range(NG):
                    G = NG * b + g
                    scores(b, kind, g, par)
                    unit = pe_units(pe, b + 1, g // 2) if more else None
                    ks = list(range(UK)) if g % 2 == 0 else list(range(UK, UH))
                    for i in range(GH):
                        if more and i < len(ks):
                            unit(ks[i])
                        if i == GH - 1:
                            weigh_values(b, G, par, g, 0)
                        if g < NG - 1:
                            max_head(G + 1, par, g + 1, i)
                        elif more:
                            max_head(G + 1, 1 - par, 0, i, nxt=b + 1)
                        if g == 0 and i == 0 and prev:
                            out_product(b, kind, b - 1)
                        if g == 0 and i == 1 and more:
                            x_transposes(b, kind, b + 1)
                        if g == 1 and i == 0 and more:
                            q_product(b, kind, b + 1)
                        if g == 1 and i == 1 and prev:
                            gate_transposes(b, kind, b - 1)
                        if g == 2 and i == 0 and prev:
                            gate_product(b, kind, b - 1)
                        if g == 2 and i == 1 and more:
                            q_transposes(b, kind, b + 1)
                        if g == 3 and i == 0 and prev:
                            positions(b, kind, b - 1)
                    weigh_values(b, G, par, g, 1)
                    sum_probs(G)

            pe.wait_ge(w_lo, 1)
            pe.wait_ge(const_in, 16 * NCONST)
            pe.wait_ge(setup_dve, 1)
            first = pe_units(pe, 0, 0)
            for k in range(UK):
                first(k)
            x_transposes(0, "pro", 0)
            pe.wait_ge(w_lo, 2)
            for k in range(UK, UH):
                first(k)
            q_product(0, "pro", 0)
            second = pe_units(pe, 0, 1)
            for k in range(UK):
                second(k)
            q_transposes(0, "pro", 0)
            for k in range(UK, UH):
                second(k)
            for h in range(GH):
                max_head(0, 0, 0, h, nxt=0)
            iteration(0, "first", 0)
            pe.wait_ge(w_in[3], 16)
            iteration(1, "mid", 1)
            with pe.Fori(1, B // 2 - 1) as i:
                iteration(2 * i, "mid", 0)
                iteration(2 * i + 1, "mid", 1)
            iteration(B - 2, "mid", 0)
            iteration(B - 1, "last", 1)
            out_product(B, "epi", B - 1)
            gate_transposes(B, "epi", B - 1)
            gate_product(B, "epi", B - 1)
            positions(B, "epi", B - 1)

        @block.scalar
        def _(act):
            raww = prob[:, :, :].rearrange("p t n -> p (t n)")[:, 0:DC * D]

            def split_weight(n, hi):
                act.wait_ge(w_in[n], 16)
                act.activation(hi[:, :, :].rearrange("p c n -> p (c n)"), raww, ACT.Copy).then_inc(w_hi, 1)

            def split_ctx(b, half):
                hh = 2 * b + half
                act.wait_ge(c_in, 16 * (hh + 1))
                wait(act, proj_ready, UH * (hh - 1))
                act.activation(ch[half][:, :, :], craw[:, :, :], ACT.Copy).then_inc(c_hi, 1)

            def unit(b, half, k, par):
                hh = 2 * b + half
                act.wait_ge(proj_ready, UH * hh + k + 1)
                src = pa[(UH * half + k) % 2]
                if k < UK:
                    wait(act, s_ready, NT * NG * (b - 1))
                    act.activation(kh[par][:, k, half * HALF:(half + 1) * HALF], src[:, 0:HALF], ACT.Identity,
                                   bias=bk[:, k:k + 1]).then_inc(k_hi, 1)
                else:
                    wait(act, pv_done, NG * (b - 1))
                    act.activation(vv[par][:, half * HT + k - UK, :], src[0:KT, 0:D], ACT.Copy).then_inc(v_copy, 1)

            def x_hi(b, kind, nxt):
                act.wait_ge(t_ready, t_index(b, kind, "xT") + 1)
                act.activation(xth[:, :, :].rearrange("p c q -> p (c q)"), pt[:, 0:DC * LQ], ACT.Copy).then_inc(xt_hi, 1)

            def q_copy(b, kind):
                act.wait_ge(t_ready, t_index(b, kind, "Q") + 1)
                act.activation(qs[:, :], pt[0:LQ, 0:D], ACT.Copy).then_inc(qs_ready, 1)

            def gate_copy(b, kind, prev):
                act.wait_ge(t_ready, t_index(b, kind, "rT") + 1)
                act.activation(x2t[:, :, :].rearrange("p c q -> p (c q)"), pt[:, 0:DC * LQ], ACT.Copy).then_inc(x2t_ready, 1)

            def shift_copy(b, kind, name, G):
                act.wait_ge(t_ready, t_index(b, kind, name) + 1)
                wait(act, s_used, NT * G)
                act.activation(shift[:, :], pt[0:KT, 0:NQ], ACT.Copy).then_inc(shift_ready, 1)

            def exps(b, G):
                for t in range(NT):
                    act.wait_ge(s_used, NT * G + t + 1)
                    alone(act, A["passed"])
                    act.activation(prob[0:KT, t, :], prob[0:KT, t, :], ACT.Exp,
                                   bias=mkey[:, bass.ds(NT * b + t, 1)], scale=SCALE).then_inc(p_ready, 1)

            def gate_exps(prev):
                act.wait_ge(gate_step, N_GATE * prev + 3)
                act.activation(ex[:, :], lg[:, :], ACT.Exp, bias=nm1[:, :]).then_inc(gate_exp, 1)

            def iteration(b, kind, par):
                more, prev = kind != "last", kind != "first"
                for g in range(NG):
                    G = NG * b + g
                    exps(b, G)
                    ks = list(range(UK)) if g % 2 == 0 else list(range(UK, UH))
                    for i in range(GH):
                        if more and i < len(ks):
                            unit(b + 1, g // 2, ks[i], 1 - par)
                        if i == 1 and more and g == 0:
                            x_hi(b, kind, b + 1)
                        if i == 0 and more and g == 1:
                            q_copy(b, kind)
                        if i == 0 and prev and g == 3:
                            gate_exps(b - 1)
                        if i == 1 and prev and g == 1:
                            gate_copy(b, kind, b - 1)
                    if more and g == 0:
                        split_ctx(b + 1, 1)
                    if more and g == 2 and not (isinstance(b, int) and b == B - 2):
                        split_ctx(b + 2, 0)
                    if g < NG - 1 or more:
                        shift_copy(b, kind, f"bc{g}", G + 1)

            split_weight(0, wkh)
            split_ctx(0, 0)
            act.wait_ge(const_in, 16 * NCONST)
            act.activation(tg[:, :], gx[:, :], ACT.Tanh).then_inc(setup_act, 1)
            split_weight(1, wvh)
            for k in range(UK):
                unit(0, 0, k, 0)
            x_hi(0, "pro", 0)
            split_weight(2, wqh)
            split_ctx(0, 1)
            for k in range(UK, UH):
                unit(0, 0, k, 0)
            q_copy(0, "pro")
            split_ctx(1, 0)
            for k in range(UH):
                unit(0, 1, k, 0)
            shift_copy(0, "pro", "bc3", 0)
            iteration(0, "first", 0)
            iteration(1, "mid", 1)
            with act.Fori(1, B // 2 - 1) as i:
                iteration(2 * i, "mid", 0)
                iteration(2 * i + 1, "mid", 1)
            iteration(B - 2, "mid", 0)
            iteration(B - 1, "last", 1)
            gate_copy(B, "epi", B - 1)
            gate_exps(B - 1)

        @block.vector
        def _(dve):
            raww = prob[:, :, :].rearrange("p t n -> p (t n)")[:, 0:DC * D]

            def split_weight(n, hi, lo):
                dve.wait_ge(w_hi, n + 1)
                dve.tensor_tensor(lo[:, :, :].rearrange("p c n -> p (c n)"), raww,
                                  f32(hi[:, :, :]).rearrange("p c n -> p (c n)"), ALU.subtract).then_inc(w_lo, 1)

            def shifted(G):
                dve.wait_ge(shift_ready, G + 1)
                wait(dve, pv_done, G)
                for t in range(NT):
                    dve.wait_ge(s_ready, NT * G + t + 1)
                    dve.tensor_tensor(prob[0:KT, t, :], s_bank(t), shift[:, :],
                                      ALU.subtract).then_inc(s_used, 1)

            def key_lo(b, half, k, par):
                hh = 2 * b + half
                dve.wait_ge(k_hi, UK * hh + k + 1)
                at = slice(half * HALF, (half + 1) * HALF)
                dve.scalar_tensor_tensor(out=kl[par][:, k, at], in0=pa[(UH * half + k) % 2][:, 0:HALF],
                                         scalar=bk[:, k:k + 1], in1=f32(kh[par][:, k, at]),
                                         op0=ALU.add, op1=ALU.subtract).then_inc(k_lo, 1)

            def head_max(G, h, mpar):
                dve.wait_ge(max_ready, GH * G + h + 1)
                alone(dve, A["passed"])
                dve.tensor_tensor_reduce(junk[:, :, :], pm[0:LQ, :, 0:HALF], mrow[mpar][:, :, :], 1.0, MASKED,
                                         ALU.add, ALU.max, mx[:, h:h + 1]).then_inc(max_used, 1)

            def diagonals(G):
                dve.wait_ge(max_used, GH * (G + 1))
                dve.tensor_tensor(diag[:, :, :], ident[0:LQ, 0:LQ].unsqueeze(1).broadcast_to([LQ, GH, LQ]),
                                  mx[:, :].unsqueeze(2).broadcast_to([LQ, GH, LQ]), ALU.mult).then_inc(diag_ready, 1)

            def normalise(G, c):
                dve.wait_ge(pv_done, G + 1)
                s = Chain(dve, norm_step, N_NORM * G)
                s.link(dve.reciprocal(rden[:, :], po[:, P:P + LQ]))
                s.link(dve.tensor_tensor(rden[:, :], po[:, 0:LQ], rden[:, :], ALU.mult))
                s.link(dve.tensor_scalar(ot[:, c, :], rden[:, :], bv[:, c:c + 1], None, ALU.add))

            def ln1_stats(b):
                dve.wait_ge(x_in, 16 * (b + 1))
                s = Chain(dve, ln1_step, N_LN1 * b, A["passed"])
                s.link(dve.bn_stats(st[:, :], xn[:, :]))
                s.link(dve.bn_aggr(mv[:, :], st[:, :]))

            def ln1_apply(b):
                dve.wait_ge(ln1_pow, 2 * (b + 1))
                dve.tensor_scalar(xn[:, :], xn[:, :], mv[:, 0:1], rstd[:, :], ALU.subtract, ALU.mult).then_inc(ln1_step, 1)

            def x_lo(b, kind, nxt):
                dve.wait_ge(xt_hi, nxt + 1)
                dve.tensor_tensor(xtl[:, :, :].rearrange("p c q -> p (c q)"), pt[:, 0:DC * LQ],
                                  f32(xth[:, :, :]).rearrange("p c q -> p (c q)"), ALU.subtract).then_inc(xt_lo, 1)

            def q_split(b, kind, nxt):
                dve.wait_ge(t_ready, t_index(b, kind, "QT") + 1)
                wait(dve, qb_ready, NG * nxt)
                s = Chain(dve, qt_step, N_QT * nxt)
                s.link(dve.tensor_tensor(qt[:, :, :], pt[:, 0:NQ].rearrange("p (c q) -> p c q", c=NG),
                                         bq[:, :].unsqueeze(2).broadcast_to([P, NG, LQ]), ALU.add)
                       )
                s.link(dve.tensor_copy(qth[:, :, :], qt[:, :, :]))
                s.link(dve.tensor_tensor(qtl[:, :, :], qt[:, :, :], f32(qth[:, :, :]), ALU.subtract))

            def mask_row(b, par):
                dve.wait_ge(m_in, 16 * (b + 1))
                dve.tensor_scalar(mrow[par][:, :, :].rearrange("p a n -> p (a n)"), mrow8[:, :], MASKED, None,
                                  ALU.mult).then_inc(m_used, 1)
                dve.wait_ge(m_used, b + 1)

            def residual(b, kind, prev):
                dve.wait_ge(t_ready, t_index(b, kind, "op") + 1)
                dve.wait_ge(xres_ready, prev + 1)
                dve.scalar_tensor_tensor(out=x1[:, :], in0=pt[0:LQ, 0:D], scalar=tg[0:LQ, 0:1], in1=x1[:, :],
                                         op0=ALU.mult, op1=ALU.add).then_inc(x1_ready, 1)
                dve.wait_ge(x1_ready, prev + 1)
                s = Chain(dve, ln2_step, N_LN2 * prev, A["passed"])
                s.link(dve.bn_stats(st2[:, :], x1[:, :]))
                s.link(dve.bn_aggr(mv2[:, :], st2[:, :]))

            def ln2_apply(prev):
                dve.wait_ge(ln2_pow, 2 * (prev + 1))
                wait(dve, xn2_out, 16 * prev)
                wait(dve, row_out, 32 * prev)
                dve.tensor_scalar(xn2[:, :], x1[:, :], mv2[:, 0:1], rs2[:, :], ALU.subtract, ALU.mult).then_inc(ln2_step, 1)

            def gate(b, kind, prev):
                dve.wait_ge(t_ready, t_index(b, kind, "rm") + 1)
                s = Chain(dve, gate_step, N_GATE * prev, A["passed"])
                s.link(dve.tensor_tensor(lg[:, :], pt[0:LQ, 0:E], br[:, :], ALU.add))
                s.link(dve.max(m8[:, :], lg[:, :]))
                dve.tensor_scalar(nm1[:, :], m8[:, 0:1], -1.0, None, ALU.mult)
                s.link(dve.tensor_scalar(sel[:, :], lg[:, :], m8[:, 1:2], None, ALU.is_ge))

            def gate_weights(prev):
                dve.wait_ge(gate_exp, prev + 1)
                s = Chain(dve, gate_step, N_GATE * prev + 3)
                s.link(dve.tensor_tensor_reduce(we[:, :], ex[:, :], sel[:, :], 1.0, 0.0, ALU.mult, ALU.add, wsum[:, :]))
                s.link(dve.reciprocal(wsum[:, :], wsum[:, :]))
                s.link(dve.tensor_scalar(wgt[:, :], we[:, :], wsum[:, :], tg[0:LQ, 1:2], ALU.mult, ALU.mult))
                s.link(dve.tensor_tensor_scan(cum[:, :], sel[:, :], zero8[:, :], 0.0, ALU.add, ALU.add))

            def choices(b, kind, prev):
                dve.wait_ge(t_ready, t_index(b, kind, "pos") + 1)
                s = Chain(dve, pos_step, N_POS * prev)
                s.link(dve.tensor_tensor(slot[:, :], pt[0:LQ, 0:E], seen[:, :], ALU.add))
                s.link(dve.tensor_tensor(seen[:, :], pt[0:LQ, E:2 * E], seen[:, :], ALU.add))
                s.link(dve.tensor_tensor(slot[:, :], slot[:, :], rowbase[:, :], ALU.add))
                s.link(dve.tensor_tensor(sk[:, :, :], rankc[:, :, :], cum[:, :].unsqueeze(1).broadcast_to([LQ, E, E]),
                                         ALU.is_equal))
                s.link(dve.tensor_tensor(sk[:, :, :], sk[:, :, :], sel[:, :].unsqueeze(1).broadcast_to([LQ, E, E]),
                                         ALU.mult))
                return s

            def slots_of(s, prev):
                s.link(dve.tensor_tensor(skv[:, :, :], sk[:, :, :], slot[:, :].unsqueeze(1).broadcast_to([LQ, E, E]),
                                         ALU.mult))
                s.link(dve.tensor_reduce(idf[:, :], skv[:, :, :], AX.X, ALU.add))
                s.link(dve.tensor_scalar(gone[:, :], rankv[:, :], cum[:, E - 1:E], OOB, ALU.is_gt, ALU.mult))
                s.link(dve.tensor_tensor(idf[:, :], idf[:, :], gone[:, :], ALU.add))
                dve.tensor_tensor(skv[:, :, :], sk[:, :, :], wgt[:, :].unsqueeze(1).broadcast_to([LQ, E, E]),
                                  ALU.mult).then_inc(idx_ready, 1)
                dve.wait_ge(idx_ready, 4 * prev + 1)
                dve.tensor_reduce(A["w_all"][:, bass.ds(E * prev, E)], skv[:, :, :], AX.X, ALU.add).then_inc(idx_ready, 1)
                dve.tensor_copy(A["i_all"][:, bass.ds(E * prev, E)], idf[:, :]).then_inc(idx_ready, 1)
                wait(dve, row_out, 32 * prev)
                dve.tensor_copy(idx[:, :], idf[:, 0:2]).then_inc(idx_ready, 1)
                dve.wait_ge(idx_ready, 4 * prev + 4)

            def iteration(b, kind, par):
                more, prev = kind != "last", kind != "first"
                skip = not more or isinstance(b, int) and b == B - 2
                for g in range(NG):
                    G = NG * b + g
                    shifted(G)
                    if g or prev:
                        normalise(G - 1, (g - 1) % NG)
                    if g == 1 and prev:
                        ln2_apply(b - 1)
                    if g == 3 and not skip:
                        ln1_apply(b + 2)
                    for i in range(GH):
                        if more and g % 2 == 0:
                            key_lo(b + 1, g // 2, i, 1 - par)
                        if g < NG - 1:
                            head_max(G + 1, i, par)
                        elif more:
                            head_max(G + 1, i, 1 - par)
                        if g == 0 and i == 0 and prev:
                            residual(b, kind, b - 1)
                        if g == 0 and i == 1 and more:
                            x_lo(b, kind, b + 1)
                        if g == 1 and i == 2 and more:
                            mask_row(b + 1, 1 - par)
                        if g == 2 and i == 0 and prev:
                            gate(b, kind, b - 1)
                        if g == 2 and i == 1 and more:
                            q_split(b, kind, b + 1)
                        if g == 2 and i == 2 and not skip:
                            ln1_stats(b + 2)
                        if g == 3 and i == 0 and prev:
                            gate_weights(b - 1)
                        if g == 3 and i == 1 and prev:
                            chosen = choices(b, kind, b - 1)
                        if g == 3 and i == 2 and prev:
                            slots_of(chosen, b - 1)
                    if g < NG - 1 or more:
                        diagonals(G + 1)

            split_weight(0, wkh, wkl)
            dve.memset(ones[:, :], 1.0).then_inc(setup_dve, 1)
            dve.memset(zero8[:, :], 0.0)
            dve.memset(seen[:, :], 0.0)
            dve.memset(zero32[:, :], 0.0)
            dve.wait_ge(setup_dve, 1)
            dve.tensor_copy(onesr[:, :], ones[0:LQ, :]).then_inc(setup_dve, 1)
            split_weight(1, wvh, wvl)
            dve.wait_ge(const_in, 16 * NCONST)
            dve.tensor_scalar(mkey[:, :], mkey8[:, :], MASKED, None, ALU.mult).then_inc(setup_dve, 1)
            dve.wait_ge(setup_act, 1)
            dve.tensor_scalar(gbo[:, :], gbo[:, :], tg[0:LQ, 0:1], None, ALU.mult).then_inc(setup_dve, 1)
            ln1_stats(0)
            ln1_apply(0)
            mask_row(0, 0)
            for k in range(UK):
                key_lo(0, 0, k, 0)
            x_lo(0, "pro", 0)
            split_weight(2, wqh, wql)
            for k in range(UK):
                key_lo(0, 1, k, 0)
            q_split(0, "pro", 0)
            ln1_stats(1)
            ln1_apply(1)
            for h in range(GH):
                head_max(0, h, 0)
            diagonals(0)
            dve.wait_ge(setup_dve, 4)
            iteration(0, "first", 0)
            iteration(1, "mid", 1)
            with dve.Fori(1, B // 2 - 1) as i:
                iteration(2 * i, "mid", 0)
                iteration(2 * i + 1, "mid", 1)
            iteration(B - 2, "mid", 0)
            iteration(B - 1, "last", 1)
            normalise(NG * B - 1, NG - 1)
            residual(B, "epi", B - 1)
            ln2_apply(B - 1)
            gate(B, "epi", B - 1)
            gate_weights(B - 1)
            slots_of(choices(B, "epi", B - 1), B - 1)
            s = Chain(dve, pos_step, N_POS * B)
            s.link(dve.tensor_copy(cnt32[:, :].rearrange("p (e r) -> p e r", e=E),
                                   seen[0:1, :].unsqueeze(2).broadcast_to([1, E, ROUNDS])))
            s.link(dve.tensor_tensor(act32[:, :], cnt32[:, :], thr32[:, :], ALU.is_gt))
            s.link(dve.tensor_tensor_scan(base32[:, :], act32[:, :], zero32[:, :], 0.0, ALU.add, ALU.add))
            n = E * ROUNDS
            s.link(dve.tensor_copy(A["table"][:, 3 * n:3 * n + 1], base32[:, n - 1:n]))
            s.link(dve.tensor_tensor(base32[:, :], base32[:, :], act32[:, :], ALU.subtract))
            s.link(dve.tensor_copy(A["table"][:, 0:n], act32[:, :]))
            s.link(dve.tensor_copy(A["table"][:, n:2 * n], base32[:, :]))
            s.link(dve.tensor_tensor(act32[:, :], act32[:, :], unit32[:, :], ALU.mult))
            s.link(dve.tensor_tensor_scan(base32[:, :], act32[:, :], zero32[:, :], 0.0, ALU.max, ALU.add))
            s.link(dve.tensor_copy(A["table"][:, 2 * n:2 * n + 1], zero32[:, 0:1]))
            s.link(dve.tensor_copy(A["table"][:, 2 * n + 1:3 * n], base32[:, 0:n - 1]))
            s.link(dve.tensor_copy(A["table"][:, 3 * n + 2:3 * n + 3], base32[:, n - 1:n]))
            s.link(dve.tensor_reduce(cnt32[:, 0:1], seen[0:1, :], AX.X, ALU.add))
            s.link(dve.tensor_scalar(cnt32[:, 1:2], cnt32[:, 0:1], float(2 * B * LQ), None, ALU.is_gt))
            s.link(dve.tensor_copy(A["table"][:, 3 * n + 1:3 * n + 2], cnt32[:, 1:2]))

        @block.gpsimd
        def _(pool):
            def lay_queries(G, c, nxt=None):
                if nxt is not None:
                    wait(pool, qt_step, N_QT * (nxt + 1))
                wait(pool, s_ready, NT * G)
                for dst, src, done in ((qbh, qth, qb_hi), (qbl, qtl, qb_ready)):
                    pool.tensor_tensor(dst[:, :, :], f32(src[:, c, :]).unsqueeze(1).broadcast_to([P, GH, LQ]),
                                       blockm[:, :, :], ALU.mult).then_inc(done, 1)

            def sum_tiles(G):
                pool.wait_ge(p_ready, NT * (G + 1))
                wait(pool, pv_done, G)
                s = Chain(pool, sum_step, N_SUM * G)
                s.link(pool.tensor_tensor(acc[:, :, :], prob[0:KT, 0:2, :], prob[0:KT, 2:4, :], ALU.add))
                s.link(pool.tensor_tensor(acc[:, :, :], acc[:, :, :], prob[0:KT, 4:6, :], ALU.add))
                s.then(pool.tensor_tensor(acc[:, 0, :], acc[:, 0, :], acc[:, 1, :], ALU.add))

            def ctx_lo(b, half):
                pool.wait_ge(c_hi, 2 * b + half + 1)
                pool.tensor_tensor(cl[half][:, :, :], craw[:, :, :], f32(ch[half][:, :, :]), ALU.subtract).then_inc(c_lo, 1)

            def power(n, ready, want, dst, src, done):
                pool.wait_ge(ready, want)
                alone(pool, A["passed"])
                pool.tensor_scalar(dst[:, :], src[:, 1:2], EPS, None, ALU.add).then_inc(done, 1)
                pool.wait_ge(done, 2 * n + 1)
                pool.tensor_tensor(dst[:, :], dst[:, :], mhalf[:, :], ALU.pow).then_inc(done, 1)

            def residual_bias(b):
                pool.wait_ge(xres_in, 16 * (b + 1))
                pool.tensor_tensor(x1[:, :], x1[:, :], gbo[:, :], ALU.add).then_inc(xres_ready, 1)

            def store_rows(b):
                pool.wait_ge(x1_ready, b + 1)
                alone(pool, A["passed"])
                pool.dma_start(A["x1_d"][bass.ds(b, 1)].rearrange("b l d -> (b l) d"), x1[:, :]).then_inc(x1_out, 16)
                pool.wait_ge(ln2_step, N_LN2 * (b + 1))
                alone(pool, A["passed"])
                pool.dma_start(A["xn2_d"][bass.ds(b, 1)].rearrange("b l d -> (b l) d"), xn2[:, :]).then_inc(xn2_out, 16)

            def scatter(b):
                pool.wait_ge(idx_ready, 4 * (b + 1))
                pool.wait_ge(zero_out, 16 * (b + 1))
                alone(pool, A["passed"])
                for k in range(2):
                    pool.indirect_dma_start(A["slots"], bass.IndirectOffsetOnAxis(ap=idx[:, k:k + 1], axis=0), xn2[:, :], None,
                                            bounds_check=E * ROWS - 1, oob_is_err=False).then_inc(row_out, 16)

            def iteration(b, kind, par):
                more, prev = kind != "last", kind != "first"
                for g in range(NG):
                    G = NG * b + g
                    if g < NG - 1:
                        lay_queries(G + 1, g + 1)
                    elif more:
                        lay_queries(G + 1, 0, nxt=b + 1)
                    sum_tiles(G)
                    if g == 0 and prev:
                        power(b - 1, ln2_step, N_LN2 * (b - 1) + 2, rs2, mv2, ln2_pow)
                    if g == 2 and more and not (isinstance(b, int) and b == B - 2):
                        power(b + 2, ln1_step, N_LN1 * (b + 2) + 2, rstd, mv, ln1_pow)
                    if g == 1 and prev:
                        store_rows(b - 1)
                    if g == 3:
                        residual_bias(b)
                    if more and g == 0:
                        ctx_lo(b + 1, 1)
                    if more and g == 2 and not (isinstance(b, int) and b == B - 2):
                        ctx_lo(b + 2, 0)
                    if g == 3 and prev:
                        scatter(b - 1)

            pool.memset(mhalf[:, :], -0.5).then_inc(setup_pool, 1)
            pool.memset(A["zero"][:, :], 0.0).then_inc(setup_pool, 1)
            pool.wait_ge(setup_pool, 2)
            ctx_lo(0, 0)
            power(0, ln1_step, 2, rstd, mv, ln1_pow)
            ctx_lo(0, 1)
            pool.wait_ge(const_in, 16 * NCONST)
            ctx_lo(1, 0)
            power(1, ln1_step, N_LN1 + 2, rstd, mv, ln1_pow)
            pool.wait_ge(setup_dve, 4)
            lay_queries(0, 0, nxt=0)
            iteration(0, "first", 0)
            iteration(1, "mid", 1)
            with pool.Fori(1, B // 2 - 1) as i:
                iteration(2 * i, "mid", 0)
                iteration(2 * i + 1, "mid", 1)
            iteration(B - 2, "mid", 0)
            iteration(B - 1, "last", 1)
            power(B - 1, ln2_step, N_LN2 * (B - 1) + 2, rs2, mv2, ln2_pow)
            store_rows(B - 1)
            scatter(B - 1)
            pool.wait_ge(x1_out, 16 * B)
            pool.wait_ge(xn2_out, 16 * B)
            pool.wait_ge(row_out, 32 * B)


def expert_phase(nc, A):
    with ExitStack() as ctx:
        def sb(name, shape, dt=F32):
            return ctx.enter_context(nc.sbuf_tensor(name, shape, dt))

        def sem(name):
            return ctx.enter_context(nc.semaphore(name))

        wraw = [sb(f"wraw{i}", [P, 2, 2, D]) for i in range(RAW)]
        wh = [sb(f"wh{i}", [P, 2, D], F32R) for i in range(RING)]
        wl = [sb(f"wl{i}", [P, 2, D], F32R) for i in range(RING)]
        xr = sb("xr", [P, NS, D])
        xh, xl = sb("xh", [P, DC, SLOTS], F32R), sb("xl", [P, DC, SLOTS], F32R)
        hid = [sb(f"hid{i}", [P, SLOTS]) for i in range(2)]
        hh = [sb(f"hh{i}", [P, SLOTS], F32R) for i in range(RING)]
        hl = [sb(f"hl{i}", [P, SLOTS], F32R) for i in range(RING)]
        y = sb("y", [P, NS, D])
        ident = sb("identx", [P, P])
        b1 = sb("b1", [P, E * NJ])
        b2 = sb("b2", [P, E * D])
        y0 = [sb(f"y0_{i}", [LQ, D]) for i in range(2)]
        y1 = [sb(f"y1_{i}", [LQ, D]) for i in range(2)]
        xo = [sb(f"xo{i}", [LQ, D]) for i in range(2)]
        pix = [sb(f"pix{i}", [LQ, 2], I32) for i in range(2)]
        tix, tiw = sb("tix", [LQ, E], I32), sb("tiw", [LQ, E])

        pt = [ctx.enter_context(nc.psum_tensor(f"ptx{i}", [P, 512], F32)) for i in range(2)]
        ph = [ctx.enter_context(nc.psum_tensor(f"ph{i}", [P, 512], F32)) for i in range(2)]
        py = ctx.enter_context(nc.psum_tensor("py", [P, NS, 512], F32))

        raw_in = [sem(f"raw_in{i}") for i in range(RAW)]
        xr_in, y_out = sem("xr_in"), sem("y_out")
        pair_in = [sem(f"pair_in{i}") for i in range(2)]
        res_in = [sem(f"res_in{i}") for i in range(2)]
        o_out = [sem(f"o_out{i}") for i in range(2)]
        dispatched, index_ready, tie_in, tie_step = sem("dispatched"), sem("index_ready"), sem("tie_in"), sem("tie_step")
        e_hi, e_lo = sem("e_hi"), sem("e_lo")
        xt_ready, xt_copied, xt_split = sem("xt_ready"), sem("xt_copied"), sem("xt_split")
        h_ready, h_gelu, h_hi, h_lo, w2_done = sem("h_ready"), sem("h_gelu"), sem("h_hi"), sem("h_lo"), sem("w2_done")
        y_copied, pair_step, pair_done = sem("y_copied"), sem("pair_step"), sem("pair_done")
        C_LO, C_W2, C_XT, C_XS, C_GELU, C_HLO, C_YC, C_YO, C_OUT = 2 * RAW, RING, DC, 2, 2, 2, 1, 16, 16
        table, w_all, i_all = A["table"], A["w_all"], A["i_all"]
        NU = E * ROUNDS
        block = ctx.enter_context(nc.Block())

        def over_units(eng, unit):
            with eng.Fori(0, E) as e:
                with eng.Fori(0, ROUNDS) as r:
                    active = eng.value_load(table[0:1, bass.ds(e * ROUNDS + r, 1)], min_val=0, max_val=1)
                    before = eng.value_load(table[0:1, bass.ds(e * ROUNDS + r + NU, 1)], min_val=0, max_val=NU)
                    with eng.If(active > 0):
                        unit(e, r, before)

        @block.sync
        def _(sp):
            sp.wait_ge(dispatched, 1)

            def unit(e, r, n):
                sp.wait_ge(xt_ready, C_XT + DC * n)
                alone(sp, A["passed"])
                sp.dma_start(xr[:, :, :], A["slots"][bass.ds(e * ROWS + r * SLOTS, SLOTS), :]
                             .rearrange("(s p) d -> p s d", p=P)).then_inc(xr_in, 16)
                for q in range(NJ // 2):
                    sp.wait_ge(e_lo, C_LO + NJ * n + 2 * (q - RAW) + 2)
                    alone(sp, A["passed"])
                    for m, w in enumerate(("W1", "W2")):
                        sp.dma_start(wraw[q % RAW][:, m, :, :], A[w][bass.ds(e, 1), :, 2 * q:2 * q + 2, :]
                                     .rearrange("e p j n -> (e p) j n")).then_inc(raw_in[q % RAW], 16)

            over_units(sp, unit)
            with sp.Fori(0, B // 2) as i:
                for par in range(2):
                    sp.wait_ge(o_out[par], C_OUT + 16 * i)
                    alone(sp, A["passed"])
                    sp.dma_start(xo[par][:, :], A["x1_d"][bass.ds(2 * i + par, 1)].rearrange("b l d -> (b l) d")).then_inc(res_in[par], 16)

        @block.tensor
        def _(pe):
            pe.sem_inc(xt_ready, C_XT)
            pe.sem_inc(w2_done, C_W2)
            pe.wait_ge(o_out[0], 16)

            def unit(e, r, n):
                pe.wait_ge(xr_in, 16 * n + 16)
                for c in range(DC):
                    pe.wait_ge(xt_split, C_XS + DC * n + c - 1)
                    for s in range(NS):
                        last = pe.transpose(pt[c % 2][:, s * P:(s + 1) * P], xr[:, s, c * P:(c + 1) * P], ident[:, :])
                    last.then_inc(xt_ready, 1)
                pe.wait_ge(xt_split, C_XS + DC * n + DC)

                def first(j):
                    pe.wait_ge(e_lo, C_LO + NJ * n + j + 1)
                    pe.wait_ge(h_gelu, C_GELU + NJ * n + j - 1)
                    k = 0
                    for c in range(DC):
                        w_h, w_l = wh[j % RING][:, 0, c * P:(c + 1) * P], wl[j % RING][:, 0, c * P:(c + 1) * P]
                        for w, x in ((w_h, xh), (w_h, xl), (w_l, xh)):
                            last = pe.matmul(ph[j % 2][:, :], w, x[:, c, :], start=(k == 0), stop=(k == 3 * DC - 1))
                            k += 1
                    last.then_inc(h_ready, 1)

                def second(j):
                    pe.wait_ge(h_lo, C_HLO + NJ * n + j + 1)
                    if j == 0:
                        pe.wait_ge(y_copied, C_YC + n)
                    a, b = j == 0, j == NJ - 1
                    for s in range(NS):
                        h_h, h_l = hh[j % RING][:, s * P:(s + 1) * P], hl[j % RING][:, s * P:(s + 1) * P]
                        pe.matmul(py[:, s, :], h_h, wh[j % RING][:, 1, :], start=a, stop=False)
                        pe.matmul(py[:, s, :], h_h, wl[j % RING][:, 1, :], start=False, stop=False)
                        last = pe.matmul(py[:, s, :], h_l, wh[j % RING][:, 1, :], start=False, stop=b)
                    last.then_inc(w2_done, 1)

                for j in range(NJ + 2):
                    if j < NJ:
                        first(j)
                    if j >= 2:
                        second(j - 2)

            over_units(pe, unit)

        @block.scalar
        def _(act):
            act.sem_inc(h_gelu, C_GELU)
            act.dma_start(ident[:, :], A["ident"]).then_inc(o_out[0], 16)
            act.dma_start(b1[:, :].rearrange("p (e j) -> p e j", e=E), A["b1"].rearrange("e p j -> p e j")).then_inc(o_out[1], 16)
            act.wait_ge(o_out[1], 16)

            def unit(e, r, n):
                def high(j):
                    q = j // 2
                    act.wait_ge(raw_in[q % RAW], 64 * n + 32 * (q // RAW) + 32)
                    act.wait_ge(w2_done, C_W2 + NJ * n + j - RING + 1)
                    act.activation(wh[j % RING][:, :, :], wraw[q % RAW][:, :, j % 2, :], ACT.Copy).then_inc(e_hi, 1)

                high(0)
                high(1)
                for c in range(DC):
                    act.wait_ge(xt_ready, C_XT + DC * n + c + 1)
                    act.activation(xh[:, c, :], pt[c % 2][:, :], ACT.Copy).then_inc(xt_copied, 1)
                for j in range(NJ):
                    if j + 2 < NJ:
                        high(j + 2)
                    act.wait_ge(h_ready, NJ * n + j + 1)
                    act.wait_ge(h_lo, C_HLO + NJ * n + j - 1)
                    alone(act, A["passed"])
                    act.activation(hid[j % 2][:, :], ph[j % 2][:, :], ACT.Gelu,
                                   bias=b1[:, bass.ds(e * NJ + j, 1)]).then_inc(h_gelu, 1)

            over_units(act, unit)
            with act.Fori(0, B // 2) as i:
                for par in range(2):
                    act.wait_ge(pair_done, 2 * i + par + 1)
                    act.dma_start(A["out"][bass.ds(2 * i + par, 1)].rearrange("b l d -> (b l) d"), y1[par][:, :]).then_inc(o_out[par], 16)
            for par in range(2):
                act.wait_ge(o_out[par], C_OUT + 16 * (B // 2))

        @block.vector
        def _(dve):
            dve.sem_inc(xt_split, C_XS)
            dve.sem_inc(h_lo, C_HLO)
            dve.sem_inc(y_copied, C_YC)
            dve.wait_ge(y_out, 16)

            def unit(e, r, n):
                for c in range(DC):
                    dve.wait_ge(xt_copied, DC * n + c + 1)
                    dve.tensor_tensor(xl[:, c, :], pt[c % 2][:, :], f32(xh[:, c, :]), ALU.subtract).then_inc(xt_split, 1)
                for j in range(NJ):
                    dve.wait_ge(h_gelu, C_GELU + NJ * n + j + 1)
                    dve.wait_ge(w2_done, C_W2 + NJ * n + j - RING + 1)
                    dve.tensor_copy(hh[j % RING][:, :], hid[j % 2][:, :]).then_inc(h_hi, 1)
                    dve.wait_ge(h_hi, NJ * n + j + 1)
                    dve.tensor_tensor(hl[j % RING][:, :], hid[j % 2][:, :], f32(hh[j % RING][:, :]),
                                      ALU.subtract).then_inc(h_lo, 1)
                dve.wait_ge(w2_done, C_W2 + NJ * n + NJ)
                dve.wait_ge(y_out, C_YO + 16 * n)
                dve.tensor_tensor(y[:, :, :], py[:, :, :], b2[:, bass.ds(e * D, D)].unsqueeze(1).broadcast_to([P, NS, D]),
                                  ALU.add).then_inc(y_copied, 1)

            over_units(dve, unit)
            with dve.Fori(0, B // 2) as i:
                for par in range(2):
                    dve.wait_ge(res_in[par], 16 * i + 16)
                    dve.wait_ge(pair_in[par], 32 * i + 32)
                    dve.scalar_tensor_tensor(out=y0[par][:, :], in0=y0[par][:, :], scalar=w_all[:, bass.ds(2 * E * i + E * par, 1)],
                                             in1=xo[par][:, :], op0=ALU.mult, op1=ALU.add).then_inc(pair_step, 1)
                    dve.wait_ge(pair_step, 2 * i + par + 1)
                    dve.scalar_tensor_tensor(out=y1[par][:, :], in0=y1[par][:, :], scalar=w_all[:, bass.ds(2 * E * i + E * par + 1, 1)],
                                             in1=y0[par][:, :], op0=ALU.mult, op1=ALU.add).then_inc(pair_done, 1)

        @block.gpsimd
        def _(pool):
            pool.sem_inc(e_lo, C_LO)
            pool.dma_start(b2[:, :], A["b2"].partition_broadcast(P)).then_inc(y_out, 16)
            tie = pool.value_load(table[0:1, 3 * NU + 1:3 * NU + 2], min_val=0, max_val=1)
            total = pool.value_load(table[0:1, 3 * NU:3 * NU + 1], min_val=1, max_val=NU)
            last_unit = pool.value_load(table[0:1, 3 * NU + 2:3 * NU + 3], min_val=0, max_val=NU - 1)
            with pool.If(tie > 0):
                with pool.Fori(0, B) as b:
                    pool.dma_start(y0[0][:, :], A["xn2_d"][bass.ds(b, 1)].rearrange("b l d -> (b l) d")).then_inc(tie_in, 16)
                    pool.wait_ge(tie_in, 16 * (E - 1) * b + 16)
                    alone(pool, A["passed"])
                    pool.tensor_copy(tix[:, :], i_all[:, bass.ds(E * b, E)]).then_inc(tie_step, 1)
                    pool.wait_ge(tie_step, b + 1)
                    alone(pool, A["passed"])
                    for k in range(2, E):
                        pool.indirect_dma_start(A["slots"], bass.IndirectOffsetOnAxis(ap=tix[:, k:k + 1], axis=0), y0[0][:, :], None,
                                                bounds_check=E * ROWS - 1, oob_is_err=False).then_inc(tie_in, 16)
                        pool.wait_ge(tie_in, 16 * (E - 1) * b + 16 * k)
                        alone(pool, A["passed"])
            pool.sem_inc(dispatched, 1)

            def unit(e, r, n):
                for j in range(NJ):
                    pool.wait_ge(e_hi, NJ * n + j + 1)
                    pool.tensor_tensor(wl[j % RING][:, :, :], wraw[(j // 2) % RAW][:, :, j % 2, :], f32(wh[j % RING][:, :, :]),
                                       ALU.subtract).then_inc(e_lo, 1)
                    if j == 3:
                        before = pool.value_load(table[0:1, bass.ds(e * ROUNDS + r + 2 * NU, 1)], min_val=0, max_val=NU - 1)
                        with pool.If(n > 0):
                            pool.wait_ge(y_copied, C_YC + n)
                            alone(pool, A["passed"])
                            pool.dma_start(A["slots"][bass.ds(before * SLOTS, SLOTS), :].rearrange("(s p) d -> p s d", p=P),
                                           y[:, :, :]).then_inc(y_out, 16)

            over_units(pool, unit)
            pool.wait_ge(y_copied, C_YC + total)
            alone(pool, A["passed"])
            pool.dma_start(A["slots"][bass.ds(last_unit * SLOTS, SLOTS), :].rearrange("(s p) d -> p s d", p=P),
                           y[:, :, :]).then_inc(y_out, 16)
            pool.wait_ge(y_out, C_YO + 16 * total)
            alone(pool, A["passed"])
            with pool.Fori(0, B // 2) as i:
                for par in range(2):
                    pool.wait_ge(o_out[par], C_OUT + 16 * i)
                    alone(pool, A["passed"])
                    pool.tensor_copy(pix[par][:, :], i_all[:, bass.ds(2 * E * i + E * par, 2)]).then_inc(index_ready, 1)
                    pool.wait_ge(index_ready, 2 * i + par + 1)
                    alone(pool, A["passed"])
                    for k, dst in enumerate((y0[par], y1[par])):
                        pool.indirect_dma_start(dst[:, :], None, A["slots"], bass.IndirectOffsetOnAxis(ap=pix[par][:, k:k + 1], axis=0),
                                                bounds_check=E * ROWS - 1, oob_is_err=False).then_inc(pair_in[par], 16)
            with pool.If(tie > 0):
                for par in range(2):
                    pool.wait_ge(o_out[par], C_OUT + 16 * (B // 2))
                    alone(pool, A["passed"])
                with pool.Fori(0, B) as b:
                    t_in, t_st = 16 * E * b + 16 * B * (E - 1), (3 * (E - 2) + 1) * b + B
                    pool.dma_start(y0[0][:, :], A["out"][bass.ds(b, 1)].rearrange("b l d -> (b l) d")).then_inc(tie_in, 16)
                    pool.wait_ge(tie_in, t_in + 16)
                    alone(pool, A["passed"])
                    pool.tensor_copy(tiw[:, :], w_all[:, bass.ds(E * b, E)])
                    pool.tensor_copy(tix[:, :], i_all[:, bass.ds(E * b, E)]).then_inc(tie_step, 1)
                    pool.wait_ge(tie_step, t_st + 1)
                    alone(pool, A["passed"])
                    for k in range(2, E):
                        pool.memset(y0[1][:, :], 0.0).then_inc(tie_step, 1)
                        pool.wait_ge(tie_step, t_st + 3 * (k - 2) + 2)
                        alone(pool, A["passed"])
                        pool.indirect_dma_start(y0[1][:, :], None, A["slots"], bass.IndirectOffsetOnAxis(ap=tix[:, k:k + 1], axis=0),
                                                bounds_check=E * ROWS - 1, oob_is_err=False).then_inc(tie_in, 16)
                        pool.wait_ge(tie_in, t_in + 16 * k)
                        alone(pool, A["passed"])
                        pool.tensor_scalar(y0[1][:, :], y0[1][:, :], tiw[:, k:k + 1], None, ALU.mult).then_inc(tie_step, 1)
                        pool.wait_ge(tie_step, t_st + 3 * (k - 2) + 3)
                        alone(pool, A["passed"])
                        pool.tensor_tensor(y0[0][:, :], y0[0][:, :], y0[1][:, :], ALU.add).then_inc(tie_step, 1)
                        pool.wait_ge(tie_step, t_st + 3 * (k - 2) + 4)
                        alone(pool, A["passed"])
                    pool.dma_start(A["out"][bass.ds(b, 1)].rearrange("b l d -> (b l) d"), y0[0][:, :]).then_inc(tie_in, 16)
                    pool.wait_ge(tie_in, t_in + 16 * E)
                    alone(pool, A["passed"])
            pool.nop()


def gated_block(nc, A):
    A["slots"] = nc.dram_tensor("expert_slots", [E * ROWS, D], F32, kind="Internal").ap()
    A["x1_d"] = nc.dram_tensor("after_attention", [B, LQ, D], F32, kind="Internal").ap()
    A["xn2_d"] = nc.dram_tensor("normalised", [B, LQ, D], F32, kind="Internal").ap()
    with ExitStack() as ctx:
        A["w_all"] = ctx.enter_context(nc.sbuf_tensor("w_all", [LQ, B * E], F32))
        A["i_all"] = ctx.enter_context(nc.sbuf_tensor("i_all", [LQ, B * E], I32))
        A["table"] = ctx.enter_context(nc.sbuf_tensor("table", [1, 3 * E * ROUNDS + 3], I32))
        A["zero"] = ctx.enter_context(nc.sbuf_tensor("zero", [P, D], F32))
        A["passed"] = ctx.enter_context(nc.semaphore("passed"))
        attention_phase(nc, A)
        expert_phase(nc, A)


def kernel(x, ctx_1024, mask_Bx1x1xS2_bf0, g_xattn, g_ffn, L0_xattn_W_q, L0_xattn_b_q, L0_xattn_W_k, L0_xattn_b_k,
           L0_xattn_W_v, L0_xattn_b_v, L0_xattn_W_o, L0_xattn_b_o, L0_ffn_W1, L0_ffn_b1, L0_ffn_W2, L0_ffn_b2,
           L0_ffn_Wr, L0_ffn_br):
    import numpy as np
    import concourse.bacc as bacc
    from concourse.bass_utils import run_bass_kernel_spmd

    def rows(a):
        return np.asarray(a).T.reshape(DC, P, -1).transpose(1, 0, 2)

    def columns(a):
        return np.asarray(a).reshape(DC, P).T

    mask = np.pad(np.asarray(mask_Bx1x1xS2_bf0).reshape(B, S), ((0, 0), (0, SP_ - S)), constant_values=True)
    u = np.arange(E * ROUNDS, dtype=np.float32)
    arrays = {
        "x": np.asarray(x),
        "ctx": np.asarray(ctx_1024).transpose(0, 2, 1).reshape(B, DC, P, S).transpose(0, 2, 1, 3),
        "mrow": mask,
        "mkey": mask.reshape(B, NT, KT).transpose(2, 0, 1).reshape(KT, B * NT),
        "gx": np.asarray(g_xattn), "gf": np.asarray(g_ffn),
        "wq": rows(L0_xattn_W_q), "wk": rows(L0_xattn_W_k), "wv": rows(L0_xattn_W_v), "wo": rows(L0_xattn_W_o),
        "bq": columns(L0_xattn_b_q), "bk": columns(L0_xattn_b_k), "bv": columns(L0_xattn_b_v),
        "bo": np.asarray(L0_xattn_b_o),
        "wr": np.asarray(L0_ffn_Wr).reshape(DC, P, E).transpose(1, 0, 2), "br": np.asarray(L0_ffn_br),
        "W1": np.asarray(L0_ffn_W1).reshape(E, DC, P, NJ, P).transpose(0, 2, 3, 1, 4).reshape(E, P, NJ, D),
        "W2": np.asarray(L0_ffn_W2).reshape(E, NJ, P, D).transpose(0, 2, 1, 3),
        "b1": np.asarray(L0_ffn_b1).reshape(E, NJ, P).transpose(0, 2, 1),
        "b2": np.asarray(L0_ffn_b2).reshape(E * D),
        "ident": np.eye(P, dtype=np.float32),
        "tri": np.triu(np.ones((LQ, LQ), np.float32), 1),
        "blockm": np.repeat(np.repeat(np.eye(GH, dtype=np.float32), DK, 0)[:, :, None], LQ, 2),
        "rankc": np.broadcast_to(np.arange(1, E + 1, dtype=np.float32)[None, :, None], (LQ, E, E)),
        "rankv": np.broadcast_to(np.arange(1, E + 1, dtype=np.float32)[None, :], (LQ, E)),
        "rowbase": np.broadcast_to(np.arange(E, dtype=np.float32)[None, :] * ROWS, (LQ, E)),
        "thr32": (u % ROUNDS * SLOTS)[None, :], "unit32": u[None, :],
    }
    nc = bacc.Bacc("TRN2", target_bir_lowering=False, num_devices=1)
    feeds, aps = {}, {}
    for name, a in arrays.items():
        a = np.ascontiguousarray(a)
        feeds[f"in_{name}"] = a
        aps[name] = nc.dram_tensor(f"in_{name}", a.shape, mybir.dt.from_np(a.dtype), kind="ExternalInput").ap()
    aps["out"] = nc.dram_tensor("out", (B, LQ, D), F32, kind="ExternalOutput").ap()
    gated_block(nc, aps)
    result = run_bass_kernel_spmd(nc, [feeds], core_ids=[0])
    return result.results[0]["out"]
```

```python
from contextlib import ExitStack

import concourse.bass as bass
from concourse import mybir

B, LQ, D = 16, 100, 512
S = 722
H, DK = 16, 32
E, HID = 8, 2048
EPS = 1e-5
SCALE = float(DK) ** -0.5

P = 128
DC = D // P
KT = 122
NT = 6
SP_ = KT * NT
HALF = SP_ // 2
HT = NT // 2
REAL = (HALF, S - HALF)
GH = P // DK
NG = H // GH
NQ = GH * LQ
UK = DC
UH = UK + HT
SLOTS = 512
ROUNDS = 4
ROWS = SLOTS * ROUNDS
NS = SLOTS // P
NJ = HID // P
RAW = 8
CHUNKS = -(-B * LQ // P)
NU = E * ROUNDS
PLACES = 4
RING = 4
MASKED = -3.0e38
OOB = float(1 << 20)

ALU = mybir.AluOpType
ACT = mybir.ActivationFunctionType
AX = mybir.AxisListType
F32 = mybir.dt.float32
F32R = mybir.dt.float32r
BF16 = mybir.dt.bfloat16
I32 = mybir.dt.int32
U8 = mybir.dt.uint8

T_PRO = ["xT", "Q", "QT", "bc3"]
T_0 = ["xT", "bc0", "Q", "bc1", "QT", "bc2", "bc3"]
T_MID = ["op", "xT", "bc0", "Q", "rT", "bc1", "rm", "QT", "bc2", "pos", "bc3"]
T_LAST = ["op", "bc0", "rT", "bc1", "rm", "bc2", "pos"]
T_EPI = ["op", "rT", "rm", "pos"]


def t_index(b, kind, name):
    if kind == "pro":
        return T_PRO.index(name)
    if kind == "first":
        return len(T_PRO) + T_0.index(name)
    if kind == "epi":
        return len(T_PRO) + len(T_0) + (B - 2) * len(T_MID) + len(T_LAST) + T_EPI.index(name)
    order = T_MID if kind == "mid" else T_LAST
    return len(T_PRO) + len(T_0) - len(T_MID) + len(T_MID) * b + order.index(name)


def unit_sizes(chunks):
    if chunks == 0:
        return [0] * ROUNDS
    units = -(-chunks // NS)
    return [max(2, chunks // units + (r < chunks % units)) if r < units else 0 for r in range(ROUNDS)]


T_SIZE, T_ROW, T_EXPERT, T_ACTIVE, T_IS2, T_IS3, T_IS4 = (k * (NU + 1) for k in range(7))
T_TIE = 7 * (NU + 1)
T_TOTAL = T_TIE + 1
C_THR, C_DSIZE, C_DROW, C_BASE, C_EXP = (0, NU * CHUNKS, 2 * NU * CHUNKS, 3 * NU * CHUNKS, 3 * NU * CHUNKS + NU)
C_RANK = C_EXP + NU


def f32(ap):
    return ap.bitcast(F32)


def wait(eng, sem, value):
    if isinstance(value, int) and value <= 0:
        return
    eng.wait_ge(sem, value)


def alone(eng, passed):
    eng.sem_inc(passed, 1)


class Chain:

    def __init__(self, eng, sem, base, passed=None):
        self.eng, self.sem, self.base, self.n, self.passed = eng, sem, base, 0, passed

    def then(self, ins):
        ins.then_inc(self.sem, 1)
        self.n += 1

    def link(self, ins):
        self.then(ins)
        self.eng.wait_ge(self.sem, self.base + self.n)
        if self.passed is not None:
            alone(self.eng, self.passed)


def attention_phase(nc, A):
    with ExitStack() as ctx:
        def sb(name, shape, dt=F32):
            return ctx.enter_context(nc.sbuf_tensor(name, shape, dt))

        def sem(name):
            return ctx.enter_context(nc.semaphore(name))

        wkh, wkl = sb("wkh", [P, DC, D], F32R), sb("wkl", [P, DC, D], F32R)
        wvh, wvl = sb("wvh", [P, DC, D], F32R), sb("wvl", [P, DC, D], F32R)
        wqh, wql = sb("wqh", [P, DC, D], F32R), sb("wql", [P, DC, D], F32R)
        wo = sb("wo", [P, DC, D])
        kh = [sb(f"kh{i}", [P, NG, SP_], F32R) for i in range(2)]
        kl = [sb(f"kl{i}", [P, NG, SP_], F32R) for i in range(2)]
        vv = [sb(f"vv{i}", [KT, NT, D]) for i in range(2)]
        craw = sb("craw", [P, DC, HALF])
        ch = [sb(f"ch{i}", [P, DC, HALF], F32R) for i in range(2)]
        cl = [sb(f"cl{i}", [P, DC, HALF], F32R) for i in range(2)]
        prob = sb("prob", [P, NT, NQ])
        acc = sb("acc", [KT, 2, NQ])
        shift = sb("shift", [KT, NQ])
        diag = sb("diag", [LQ, GH, LQ], F32R)
        mx = sb("mx", [LQ, GH])
        junk = sb("junk", [LQ, 2, HALF], BF16)
        qbh, qbl = sb("qbh", [P, GH, LQ], F32R), sb("qbl", [P, GH, LQ], F32R)
        qt = sb("qt", [P, NG, LQ])
        qth, qtl = sb("qth", [P, NG, LQ], F32R), sb("qtl", [P, NG, LQ], F32R)
        qs = sb("qs", [LQ, D])
        xn = sb("xn", [LQ, D])
        xth, xtl = sb("xth", [P, DC, LQ], F32R), sb("xtl", [P, DC, LQ], F32R)
        rden = sb("rden", [P, LQ])
        ot = sb("ot", [P, NG, LQ])
        x1 = sb("x1", [LQ, D])
        xn2 = sb("xn2", [LQ, D])
        x2t = qt
        mrow8 = sb("mrow8", [LQ, SP_], U8)
        mrow = [sb(f"mrow{i}", [LQ, 2, HALF], BF16) for i in range(2)]
        mkey8 = sb("mkey8", [KT, B * NT], U8)
        mkey = sb("mkey", [KT, B * NT])
        ident, tri = sb("ident", [P, P]), sb("tri", [LQ, LQ])
        blockm = sb("blockm", [P, GH, LQ])
        rankc = sb("rankc", [LQ, E, E])
        rankv = sb("rankv", [LQ, E])
        rowbase = sb("rowbase", [LQ, E])
        ones = sb("ones", [P, P])
        onesr = sb("onesr", [LQ, P], F32R)
        gbo = sb("gbo", [LQ, D])
        bq, bk, bv = sb("bq", [P, NG]), sb("bk", [P, NG]), sb("bv", [P, NG])
        wr = sb("wr", [P, DC, E])
        br = sb("br", [LQ, E])
        gx = sb("gx", [P, 2])
        tg = sb("tg", [P, 2])
        st = sb("st", [LQ, 6])
        mv = sb("mv", [LQ, 2])
        rstd, rs2 = sb("rstd", [LQ, 1]), sb("rs2", [LQ, 1])
        mhalf = sb("mhalf", [LQ, 1])
        st2 = sb("st2", [LQ, 6])
        mv2 = sb("mv2", [LQ, 2])
        lg, m8, nm1 = sb("lg", [LQ, E]), sb("m8", [LQ, 8]), sb("nm1", [LQ, 1])
        ex, sel, cum = sb("ex", [LQ, E]), sb("sel", [LQ, E]), sb("cum", [LQ, E])
        zero8 = sb("zero8", [LQ, E])
        we, wsum, wgt = sb("we", [LQ, E]), sb("wsum", [LQ, 1]), sb("wgt", [LQ, E])
        seen, slot = sb("seen", [LQ, E]), sb("slot", [LQ, E])
        sk, skv = sb("sk", [LQ, E, E]), sb("skv", [LQ, E, E])
        idf, gone = sb("idf", [LQ, E]), sb("gone", [LQ, E])
        idx = sb("idx", [LQ, 2], I32)
        choices_all, unit_v = sb("choices_all", [1, 1]), sb("unit_v", [NU, 3])

        pa = [ctx.enter_context(nc.psum_tensor(f"pa{i}", [P, 512], F32)) for i in range(2)]
        psc = [ctx.enter_context(nc.psum_tensor(f"psc{i}", [P, 512], F32)) for i in range(2)]
        pm = ctx.enter_context(nc.psum_tensor("pm", [P, 2, 512], F32))
        po = ctx.enter_context(nc.psum_tensor("po", [P, 512], F32))
        pt = ctx.enter_context(nc.psum_tensor("pt", [P, 512], F32))

        def s_bank(t):
            return pm[0:KT, t - 2, 0:NQ] if t in (2, 3) else psc[t % 2][0:KT, 0:NQ]

        w_in = [sem(f"w_in_{n}") for n in "kvqo"]
        const_in, units_in, c_in, x_in = sem("const_in"), sem("units_in"), sem("c_in"), sem("x_in")
        units_step = sem("units_step")
        m_in, xres_in = sem("m_in"), sem("xres_in")
        row_out, x1_out, xn2_out, zero_out = sem("row_out"), sem("x1_out"), sem("xn2_out"), sem("zero_out")
        w_hi, w_lo = sem("w_hi"), sem("w_lo")
        setup_act, setup_dve, setup_pool = sem("setup_act"), sem("setup_dve"), sem("setup_pool")
        c_hi, c_lo = sem("c_hi"), sem("c_lo")
        proj_ready, k_hi, k_lo, v_copy = sem("proj_ready"), sem("k_hi"), sem("k_lo"), sem("v_copy")
        s_ready, s_used, p_ready = sem("s_ready"), sem("s_used"), sem("p_ready")
        max_ready, max_used, diag_ready, shift_ready = sem("max_ready"), sem("max_used"), sem("diag_ready"), sem("shift_ready")
        qb_hi, qb_ready, sum_step, pv_done, norm_step = sem("qb_hi"), sem("qb_ready"), sem("sum_step"), sem("pv_done"), sem("norm_step")
        t_ready = sem("t_ready")
        ln1_step, ln1_pow, xt_hi, xt_lo, qs_ready, qt_step = sem("ln1_step"), sem("ln1_pow"), sem("xt_hi"), sem("xt_lo"), sem("qs_ready"), sem("qt_step")
        m_used, xres_ready, x1_ready, ln2_step, ln2_pow = sem("m_used"), sem("xres_ready"), sem("x1_ready"), sem("ln2_step"), sem("ln2_pow")
        x2t_ready, gate_step, gate_exp, pos_step, idx_ready = sem("x2t_ready"), sem("gate_step"), sem("gate_exp"), sem("pos_step"), sem("idx_ready")

        NCONST = 15
        N_LN1, N_LN2, N_GATE, N_POS, N_NORM, N_QT, N_SUM = 3, 3, 7, 9, 3, 3, 3
        block = ctx.enter_context(nc.Block())

        @block.sync
        def _(sp):
            flat = prob[:, :, :].rearrange("p t n -> p (t n)")

            def load_w(n, name):
                wait(sp, w_lo, n)
                sp.dma_start(flat[:, 0:DC * D], A[name].rearrange("p c n -> p (c n)")).then_inc(w_in[n], 16)

            def load_ctx(b, half):
                wait(sp, c_lo, 2 * b + half)
                alone(sp, A["passed"])
                sp.dma_start(craw[:, :, 0:REAL[half]],
                             A["ctx"][bass.ds(b, 1), :, :, half * HALF:half * HALF + REAL[half]]
                             .rearrange("b p c n -> (b p) c n")).then_inc(c_in, 16)

            def load_x(b):
                wait(sp, xt_hi, b)
                alone(sp, A["passed"])
                sp.dma_start(xn[:, :], A["x"][bass.ds(b, 1)].rearrange("b l d -> (b l) d")).then_inc(x_in, 16)

            def load_mask(b):
                wait(sp, m_used, b)
                alone(sp, A["passed"])
                sp.dma_start(mrow8[:, :], A["mrow"][bass.ds(b, 1), :].rearrange("b s -> (b s)")
                             .partition_broadcast(LQ)).then_inc(m_in, 16)

            def load_res(b):
                wait(sp, x1_out, 16 * b)
                alone(sp, A["passed"])
                wait(sp, ln2_step, N_LN2 * b)
                alone(sp, A["passed"])
                sp.dma_start(x1[:, :], A["x"][bass.ds(b, 1)].rearrange("b l d -> (b l) d")).then_inc(xres_in, 16)

            def clear_slots(b):
                wait(sp, zero_out, 16 * b)
                alone(sp, A["passed"])
                sp.dma_start(A["slots"].rearrange("(e n p) d -> n p e d", e=E, p=P)[bass.ds(b, 1)]
                             .rearrange("n p e d -> (n p) e d"),
                             A["zero"][:, :].unsqueeze(1).broadcast_to([P, E, D])).then_inc(zero_out, 16)

            def batch(b):
                load_ctx(b, 0)
                load_x(b)
                load_mask(b)
                load_ctx(b, 1)
                clear_slots(b)

            load_w(0, "wk")
            sp.dma_start(craw[:, :, 0:REAL[0]], A["ctx"][0, :, :, 0:REAL[0]]).then_inc(c_in, 16)
            for dst, src in ((ident, A["ident"]), (tri, A["tri"]), (blockm, A["blockm"]), (rankc, A["rankc"]),
                             (rankv, A["rankv"]), (rowbase, A["rowbase"]), (bq, A["bq"]), (bk, A["bk"]), (bv, A["bv"]),
                             (wr, A["wr"]), (mkey8, A["mkey"])):
                sp.dma_start(dst[:], src).then_inc(const_in, 16)
            sp.dma_start(br[:, :], A["br"].partition_broadcast(LQ)).then_inc(const_in, 16)
            sp.dma_start(gbo[:, :], A["bo"].partition_broadcast(LQ)).then_inc(const_in, 16)
            sp.dma_start(gx[:, 0:1], A["gx"].partition_broadcast(P)).then_inc(const_in, 16)
            sp.dma_start(gx[:, 1:2], A["gf"].partition_broadcast(P)).then_inc(const_in, 16)
            load_x(0)
            load_mask(0)
            load_w(1, "wv")
            load_w(2, "wq")
            load_ctx(0, 1)
            sp.dma_start(wo[:, :, :], A["wo"]).then_inc(w_in[3], 16)
            load_res(0)
            sp.wait_ge(setup_pool, 2)
            clear_slots(0)
            batch(1)
            with sp.Fori(2, B) as b:
                batch(b)
                load_res(b - 1)
            load_res(B - 1)
            sp.wait_ge(c_lo, 2 * B)
            sp.dma_start(craw[0:NU, :, :].rearrange("p c n -> p (c n)")[:, 0:C_RANK + 1], A["units"]).then_inc(units_in, 16)

        def pe_units(pe, nxt, half):
            hh = 2 * nxt + half

            def bank(k):
                return pa[(UH * half + k) % 2]

            def unit(k):
                if k == 0:
                    wait(pe, v_copy, HT * hh - 1)
                elif k == 1:
                    wait(pe, v_copy, HT * hh)
                elif k < UK + 2:
                    wait(pe, k_lo, UK * hh + k - 1)
                else:
                    wait(pe, v_copy, HT * hh + k - UK - 1)
                if k == 0:
                    wait(pe, c_lo, hh + 1)
                if k < UK:
                    o = bank(k)[:, 0:HALF]
                    n = 0
                    for c in range(DC):
                        wh, wl = wkh[:, c, k * P:(k + 1) * P], wkl[:, c, k * P:(k + 1) * P]
                        for w, x in ((wh, ch[half]), (wh, cl[half]), (wl, ch[half])):
                            last = pe.matmul(o, w, x[:, c, :], start=(n == 0), stop=(n == 3 * DC - 1))
                            n += 1
                else:
                    t = k - UK
                    o = bank(k)[0:KT, 0:D]
                    n = 0
                    for c in range(DC):
                        xh, xl = ch[half][:, c, t * KT:(t + 1) * KT], cl[half][:, c, t * KT:(t + 1) * KT]
                        for x, w in ((xh, wvh), (xl, wvh), (xh, wvl)):
                            last = pe.matmul(o, x, w[:, c, :], start=(n == 0), stop=(n == 3 * DC - 1))
                            n += 1
                last.then_inc(proj_ready, 1)
            return unit

        @block.tensor
        def _(pe):
            def t_use(b, kind, name):
                order = {"pro": T_PRO, "first": T_0, "mid": T_MID, "last": T_LAST, "epi": T_EPI}[kind]
                at = order.index(name)
                if kind == "pro":
                    b = -1
                    if at == 0:
                        return
                if at:
                    before = order[at - 1]
                elif kind == "epi":
                    before, b = "pos", b - 1
                else:
                    before, b = "bc3", b - 1
                read_by = {"xT": (xt_lo, b + 2), "Q": (qs_ready, b + 2), "QT": (qt_step, N_QT * (b + 1) + 1),
                           "op": (x1_ready, b), "rT": (x2t_ready, b), "rm": (gate_step, N_GATE * (b - 1) + 1),
                           "pos": (pos_step, N_POS * (b - 1) + 2)}
                if before in read_by:
                    pe.wait_ge(*read_by[before])
                else:
                    pe.wait_ge(shift_ready, NG * b + int(before[2]) + 2)

            def x_transposes(b, kind, nxt):
                wait(pe, ln1_step, N_LN1 * (nxt + 1))
                t_use(b, kind, "xT")
                for c in range(DC):
                    last = pe.transpose(pt[:, c * LQ:(c + 1) * LQ], xn[:, c * P:(c + 1) * P], ident[0:LQ, 0:LQ])
                last.then_inc(t_ready, 1)

            def q_product(b, kind, nxt):
                wait(pe, xt_lo, nxt + 1)
                if kind == "pro":
                    wait(pe, w_lo, 3)
                t_use(b, kind, "Q")
                n = 0
                for c in range(DC):
                    for x, w in ((xth, wqh), (xth, wql), (xtl, wqh)):
                        last = pe.matmul(pt[0:LQ, 0:D], x[:, c, :], w[:, c, :], start=(n == 0), stop=(n == 3 * DC - 1))
                        n += 1
                last.then_inc(t_ready, 1)

            def q_transposes(b, kind, nxt):
                wait(pe, qs_ready, nxt + 1)
                t_use(b, kind, "QT")
                for c in range(DC):
                    last = pe.transpose(pt[:, c * LQ:(c + 1) * LQ], qs[:, c * P:(c + 1) * P], ident[0:LQ, 0:LQ])
                last.then_inc(t_ready, 1)

            def max_head(G, kpar, c, h, nxt=None):
                if h == 0:
                    wait(pe, qb_hi, G + 1)
                    if nxt is not None:
                        wait(pe, k_lo, 2 * UK * (nxt + 1))
                    wait(pe, s_used, NT * (G - 1) + 4)
                wait(pe, max_used, GH * G + h)
                for i in range(2):
                    last = pe.matmul(pm[0:LQ, i, 0:HALF], qbh[:, h, :], kh[kpar][:, c, i * HALF:(i + 1) * HALF],
                                     start=True, stop=True)
                last.then_inc(max_ready, 1)

            def broadcast_shift(b, kind, name, G):
                wait(pe, diag_ready, G + 1)
                t_use(b, kind, name)
                pe.matmul(pt[:, 0:NQ], onesr[:, :], diag[:, :, :].rearrange("p h q -> p (h q)"),
                          start=True, stop=True).then_inc(t_ready, 1)

            def scores(b, kind, g, par):
                G = NG * b + g
                wait(pe, qb_ready, G + 1)
                q_h = qbh[:, :, :].rearrange("p h q -> p (h q)")
                q_l = qbl[:, :, :].rearrange("p h q -> p (h q)")
                for t in range(NT):
                    if t in (0, 1):
                        wait(pe, s_used, NT * G + t - 1)
                    elif t in (2, 3):
                        wait(pe, max_used, GH * (G + 1))
                    else:
                        wait(pe, s_used, NT * G + t - 3)
                    if t == 2:
                        if g:
                            broadcast_shift(b, kind, f"bc{g - 1}", G)
                        else:
                            before = {"first": "pro", "mid": "first" if isinstance(b, int) and b == 1 else "mid"}
                            broadcast_shift(b - 1, before.get(kind, "mid"), "bc3", G)
                    k_h, k_l = kh[par][:, g, t * KT:(t + 1) * KT], kl[par][:, g, t * KT:(t + 1) * KT]
                    o = s_bank(t)
                    pe.matmul(o, k_h, q_h, start=True, stop=False)
                    pe.matmul(o, k_h, q_l, start=False, stop=False)
                    pe.matmul(o, k_l, q_h, start=False, stop=True).then_inc(s_ready, 1)

            def weigh_values(b, G, par, c, part):
                if part == 0:
                    if c == 0:
                        wait(pe, v_copy, 2 * HT * (b + 1))
                    wait(pe, norm_step, N_NORM * G)
                wait(pe, p_ready, NT * G + HT * (part + 1))
                for t in range(part * HT, (part + 1) * HT):
                    for h in range(GH):
                        pe.matmul(po[h * DK:(h + 1) * DK, 0:LQ],
                                  vv[par][:, t, c * P + h * DK:c * P + (h + 1) * DK],
                                  prob[0:KT, t, h * LQ:(h + 1) * LQ], start=(t == 0), stop=(t == NT - 1),
                                  tile_position=(0, h * DK))

            def sum_probs(G):
                wait(pe, sum_step, N_SUM * (G + 1))
                for h in range(GH):
                    last = pe.matmul(po[h * DK:(h + 1) * DK, P:P + LQ], ones[0:KT, 0:DK],
                                     acc[:, 0, h * LQ:(h + 1) * LQ], start=True, stop=True,
                                     tile_position=(0, h * DK))
                last.then_inc(pv_done, 1)

            def out_product(b, kind, prev):
                wait(pe, norm_step, N_NORM * NG * (prev + 1))
                t_use(b, kind, "op")
                for c in range(DC):
                    last = pe.matmul(pt[0:LQ, 0:D], ot[:, c, :], wo[:, c, :], start=(c == 0), stop=(c == DC - 1))
                last.then_inc(t_ready, 1)

            def gate_transposes(b, kind, prev):
                wait(pe, ln2_step, N_LN2 * (prev + 1))
                t_use(b, kind, "rT")
                for c in range(DC):
                    last = pe.transpose(pt[:, c * LQ:(c + 1) * LQ], xn2[:, c * P:(c + 1) * P], ident[0:LQ, 0:LQ])
                last.then_inc(t_ready, 1)

            def gate_product(b, kind, prev):
                wait(pe, x2t_ready, prev + 1)
                t_use(b, kind, "rm")
                for c in range(DC):
                    last = pe.matmul(pt[0:LQ, 0:E], x2t[:, c, :], wr[:, c, :], start=(c == 0), stop=(c == DC - 1))
                last.then_inc(t_ready, 1)

            def positions(b, kind, prev):
                wait(pe, gate_step, N_GATE * prev + 3)
                t_use(b, kind, "pos")
                pe.matmul(pt[0:LQ, 0:E], tri[:, :], sel[:, :], start=True, stop=True)
                pe.matmul(pt[0:LQ, E:2 * E], ones[0:LQ, 0:LQ], sel[:, :], start=True, stop=True).then_inc(t_ready, 1)

            def iteration(b, kind, par):
                more, prev = kind != "last", kind != "first"
                for g in range(NG):
                    G = NG * b + g
                    scores(b, kind, g, par)
                    unit = pe_units(pe, b + 1, g // 2) if more else None
                    ks = list(range(UK)) if g % 2 == 0 else list(range(UK, UH))
                    for i in range(GH):
                        if more and i < len(ks):
                            unit(ks[i])
                        if i == GH - 1:
                            weigh_values(b, G, par, g, 0)
                        if g < NG - 1:
                            max_head(G + 1, par, g + 1, i)
                        elif more:
                            max_head(G + 1, 1 - par, 0, i, nxt=b + 1)
                        if g == 0 and i == 0 and prev:
                            out_product(b, kind, b - 1)
                        if g == 0 and i == 1 and more:
                            x_transposes(b, kind, b + 1)
                        if g == 1 and i == 0 and more:
                            q_product(b, kind, b + 1)
                        if g == 1 and i == 1 and prev:
                            gate_transposes(b, kind, b - 1)
                        if g == 2 and i == 0 and prev:
                            gate_product(b, kind, b - 1)
                        if g == 2 and i == 1 and more:
                            q_transposes(b, kind, b + 1)
                        if g == 3 and i == 0 and prev:
                            positions(b, kind, b - 1)
                    weigh_values(b, G, par, g, 1)
                    sum_probs(G)

            pe.wait_ge(w_lo, 1)
            pe.wait_ge(const_in, 16 * NCONST)
            pe.wait_ge(setup_dve, 1)
            first = pe_units(pe, 0, 0)
            for k in range(UK):
                first(k)
            x_transposes(0, "pro", 0)
            pe.wait_ge(w_lo, 2)
            for k in range(UK, UH):
                first(k)
            q_product(0, "pro", 0)
            second = pe_units(pe, 0, 1)
            for k in range(UK):
                second(k)
            q_transposes(0, "pro", 0)
            for k in range(UK, UH):
                second(k)
            for h in range(GH):
                max_head(0, 0, 0, h, nxt=0)
            iteration(0, "first", 0)
            pe.wait_ge(w_in[3], 16)
            iteration(1, "mid", 1)
            with pe.Fori(1, B // 2 - 1) as i:
                iteration(2 * i, "mid", 0)
                iteration(2 * i + 1, "mid", 1)
            iteration(B - 2, "mid", 0)
            iteration(B - 1, "last", 1)
            out_product(B, "epi", B - 1)
            gate_transposes(B, "epi", B - 1)
            gate_product(B, "epi", B - 1)
            positions(B, "epi", B - 1)
            pe.wait_ge(units_step, 13)
            for k in range(3):
                last = pe.matmul(pt[0:1, 2 * E + k * NU:2 * E + (k + 1) * NU], unit_v[:, k:k + 1], ident[0:NU, 0:NU],
                                 start=True, stop=True)
            last.then_inc(t_ready, 1)

        @block.scalar
        def _(act):
            raww = prob[:, :, :].rearrange("p t n -> p (t n)")[:, 0:DC * D]

            def split_weight(n, hi):
                act.wait_ge(w_in[n], 16)
                act.activation(hi[:, :, :].rearrange("p c n -> p (c n)"), raww, ACT.Copy).then_inc(w_hi, 1)

            def split_ctx(b, half):
                hh = 2 * b + half
                act.wait_ge(c_in, 16 * (hh + 1))
                wait(act, proj_ready, UH * (hh - 1))
                act.activation(ch[half][:, :, :], craw[:, :, :], ACT.Copy).then_inc(c_hi, 1)

            def unit(b, half, k, par):
                hh = 2 * b + half
                act.wait_ge(proj_ready, UH * hh + k + 1)
                src = pa[(UH * half + k) % 2]
                if k < UK:
                    wait(act, s_ready, NT * NG * (b - 1))
                    act.activation(kh[par][:, k, half * HALF:(half + 1) * HALF], src[:, 0:HALF], ACT.Identity,
                                   bias=bk[:, k:k + 1]).then_inc(k_hi, 1)
                else:
                    wait(act, pv_done, NG * (b - 1))
                    act.activation(vv[par][:, half * HT + k - UK, :], src[0:KT, 0:D], ACT.Copy).then_inc(v_copy, 1)

            def x_hi(b, kind, nxt):
                act.wait_ge(t_ready, t_index(b, kind, "xT") + 1)
                act.activation(xth[:, :, :].rearrange("p c q -> p (c q)"), pt[:, 0:DC * LQ], ACT.Copy).then_inc(xt_hi, 1)

            def q_copy(b, kind):
                act.wait_ge(t_ready, t_index(b, kind, "Q") + 1)
                act.activation(qs[:, :], pt[0:LQ, 0:D], ACT.Copy).then_inc(qs_ready, 1)

            def gate_copy(b, kind, prev):
                act.wait_ge(t_ready, t_index(b, kind, "rT") + 1)
                act.activation(x2t[:, :, :].rearrange("p c q -> p (c q)"), pt[:, 0:DC * LQ], ACT.Copy).then_inc(x2t_ready, 1)

            def shift_copy(b, kind, name, G):
                act.wait_ge(t_ready, t_index(b, kind, name) + 1)
                wait(act, s_used, NT * G)
                act.activation(shift[:, :], pt[0:KT, 0:NQ], ACT.Copy).then_inc(shift_ready, 1)

            def exps(b, G):
                for t in range(NT):
                    act.wait_ge(s_used, NT * G + t + 1)
                    alone(act, A["passed"])
                    act.activation(prob[0:KT, t, :], prob[0:KT, t, :], ACT.Exp,
                                   bias=mkey[:, bass.ds(NT * b + t, 1)], scale=SCALE).then_inc(p_ready, 1)

            def gate_exps(prev):
                act.wait_ge(gate_step, N_GATE * prev + 3)
                act.activation(ex[:, :], lg[:, :], ACT.Exp, bias=nm1[:, :]).then_inc(gate_exp, 1)

            def iteration(b, kind, par):
                more, prev = kind != "last", kind != "first"
                for g in range(NG):
                    G = NG * b + g
                    exps(b, G)
                    ks = list(range(UK)) if g % 2 == 0 else list(range(UK, UH))
                    for i in range(GH):
                        if more and i < len(ks):
                            unit(b + 1, g // 2, ks[i], 1 - par)
                        if i == 1 and more and g == 0:
                            x_hi(b, kind, b + 1)
                        if i == 0 and more and g == 1:
                            q_copy(b, kind)
                        if i == 0 and prev and g == 3:
                            gate_exps(b - 1)
                        if i == 1 and prev and g == 1:
                            gate_copy(b, kind, b - 1)
                    if more and g == 0:
                        split_ctx(b + 1, 1)
                    if more and g == 2 and not (isinstance(b, int) and b == B - 2):
                        split_ctx(b + 2, 0)
                    if g < NG - 1 or more:
                        shift_copy(b, kind, f"bc{g}", G + 1)

            split_weight(0, wkh)
            split_ctx(0, 0)
            act.wait_ge(const_in, 16 * NCONST)
            act.activation(tg[:, :], gx[:, :], ACT.Tanh).then_inc(setup_act, 1)
            split_weight(1, wvh)
            for k in range(UK):
                unit(0, 0, k, 0)
            x_hi(0, "pro", 0)
            split_weight(2, wqh)
            split_ctx(0, 1)
            for k in range(UK, UH):
                unit(0, 0, k, 0)
            q_copy(0, "pro")
            split_ctx(1, 0)
            for k in range(UH):
                unit(0, 1, k, 0)
            shift_copy(0, "pro", "bc3", 0)
            iteration(0, "first", 0)
            iteration(1, "mid", 1)
            with act.Fori(1, B // 2 - 1) as i:
                iteration(2 * i, "mid", 0)
                iteration(2 * i + 1, "mid", 1)
            iteration(B - 2, "mid", 0)
            iteration(B - 1, "last", 1)
            gate_copy(B, "epi", B - 1)
            gate_exps(B - 1)

        @block.vector
        def _(dve):
            raww = prob[:, :, :].rearrange("p t n -> p (t n)")[:, 0:DC * D]

            def split_weight(n, hi, lo):
                dve.wait_ge(w_hi, n + 1)
                dve.tensor_tensor(lo[:, :, :].rearrange("p c n -> p (c n)"), raww,
                                  f32(hi[:, :, :]).rearrange("p c n -> p (c n)"), ALU.subtract).then_inc(w_lo, 1)

            def shifted(G):
                dve.wait_ge(shift_ready, G + 1)
                wait(dve, pv_done, G)
                for t in range(NT):
                    dve.wait_ge(s_ready, NT * G + t + 1)
                    dve.tensor_tensor(prob[0:KT, t, :], s_bank(t), shift[:, :],
                                      ALU.subtract).then_inc(s_used, 1)

            def key_lo(b, half, k, par):
                hh = 2 * b + half
                dve.wait_ge(k_hi, UK * hh + k + 1)
                at = slice(half * HALF, (half + 1) * HALF)
                dve.scalar_tensor_tensor(out=kl[par][:, k, at], in0=pa[(UH * half + k) % 2][:, 0:HALF],
                                         scalar=bk[:, k:k + 1], in1=f32(kh[par][:, k, at]),
                                         op0=ALU.add, op1=ALU.subtract).then_inc(k_lo, 1)

            def head_max(G, h, mpar):
                dve.wait_ge(max_ready, GH * G + h + 1)
                alone(dve, A["passed"])
                dve.tensor_tensor_reduce(junk[:, :, :], pm[0:LQ, :, 0:HALF], mrow[mpar][:, :, :], 1.0, MASKED,
                                         ALU.add, ALU.max, mx[:, h:h + 1]).then_inc(max_used, 1)

            def diagonals(G):
                dve.wait_ge(max_used, GH * (G + 1))
                dve.tensor_tensor(diag[:, :, :], ident[0:LQ, 0:LQ].unsqueeze(1).broadcast_to([LQ, GH, LQ]),
                                  mx[:, :].unsqueeze(2).broadcast_to([LQ, GH, LQ]), ALU.mult).then_inc(diag_ready, 1)

            def normalise(G, c):
                dve.wait_ge(pv_done, G + 1)
                s = Chain(dve, norm_step, N_NORM * G)
                s.link(dve.reciprocal(rden[:, :], po[:, P:P + LQ]))
                s.link(dve.tensor_tensor(rden[:, :], po[:, 0:LQ], rden[:, :], ALU.mult))
                s.link(dve.tensor_scalar(ot[:, c, :], rden[:, :], bv[:, c:c + 1], None, ALU.add))

            def ln1_stats(b):
                dve.wait_ge(x_in, 16 * (b + 1))
                s = Chain(dve, ln1_step, N_LN1 * b, A["passed"])
                s.link(dve.bn_stats(st[:, :], xn[:, :]))
                s.link(dve.bn_aggr(mv[:, :], st[:, :]))

            def ln1_apply(b):
                dve.wait_ge(ln1_pow, 2 * (b + 1))
                dve.tensor_scalar(xn[:, :], xn[:, :], mv[:, 0:1], rstd[:, :], ALU.subtract, ALU.mult).then_inc(ln1_step, 1)

            def x_lo(b, kind, nxt):
                dve.wait_ge(xt_hi, nxt + 1)
                dve.tensor_tensor(xtl[:, :, :].rearrange("p c q -> p (c q)"), pt[:, 0:DC * LQ],
                                  f32(xth[:, :, :]).rearrange("p c q -> p (c q)"), ALU.subtract).then_inc(xt_lo, 1)

            def q_split(b, kind, nxt):
                dve.wait_ge(t_ready, t_index(b, kind, "QT") + 1)
                wait(dve, qb_ready, NG * nxt)
                s = Chain(dve, qt_step, N_QT * nxt)
                s.link(dve.tensor_tensor(qt[:, :, :], pt[:, 0:NQ].rearrange("p (c q) -> p c q", c=NG),
                                         bq[:, :].unsqueeze(2).broadcast_to([P, NG, LQ]), ALU.add)
                       )
                s.link(dve.tensor_copy(qth[:, :, :], qt[:, :, :]))
                s.link(dve.tensor_tensor(qtl[:, :, :], qt[:, :, :], f32(qth[:, :, :]), ALU.subtract))

            def mask_row(b, par):
                dve.wait_ge(m_in, 16 * (b + 1))
                dve.tensor_scalar(mrow[par][:, :, :].rearrange("p a n -> p (a n)"), mrow8[:, :], MASKED, None,
                                  ALU.mult).then_inc(m_used, 1)
                dve.wait_ge(m_used, b + 1)

            def residual(b, kind, prev):
                dve.wait_ge(t_ready, t_index(b, kind, "op") + 1)
                dve.wait_ge(xres_ready, prev + 1)
                dve.scalar_tensor_tensor(out=x1[:, :], in0=pt[0:LQ, 0:D], scalar=tg[0:LQ, 0:1], in1=x1[:, :],
                                         op0=ALU.mult, op1=ALU.add).then_inc(x1_ready, 1)
                dve.wait_ge(x1_ready, prev + 1)
                s = Chain(dve, ln2_step, N_LN2 * prev, A["passed"])
                s.link(dve.bn_stats(st2[:, :], x1[:, :]))
                s.link(dve.bn_aggr(mv2[:, :], st2[:, :]))

            def ln2_apply(prev):
                dve.wait_ge(ln2_pow, 2 * (prev + 1))
                wait(dve, xn2_out, 16 * prev)
                wait(dve, row_out, 32 * prev)
                dve.tensor_scalar(xn2[:, :], x1[:, :], mv2[:, 0:1], rs2[:, :], ALU.subtract, ALU.mult).then_inc(ln2_step, 1)

            def gate(b, kind, prev):
                dve.wait_ge(t_ready, t_index(b, kind, "rm") + 1)
                s = Chain(dve, gate_step, N_GATE * prev, A["passed"])
                s.link(dve.tensor_tensor(lg[:, :], pt[0:LQ, 0:E], br[:, :], ALU.add))
                s.link(dve.max(m8[:, :], lg[:, :]))
                dve.tensor_scalar(nm1[:, :], m8[:, 0:1], -1.0, None, ALU.mult)
                s.link(dve.tensor_scalar(sel[:, :], lg[:, :], m8[:, 1:2], None, ALU.is_ge))

            def gate_weights(prev):
                dve.wait_ge(gate_exp, prev + 1)
                s = Chain(dve, gate_step, N_GATE * prev + 3)
                s.link(dve.tensor_tensor_reduce(we[:, :], ex[:, :], sel[:, :], 1.0, 0.0, ALU.mult, ALU.add, wsum[:, :]))
                s.link(dve.reciprocal(wsum[:, :], wsum[:, :]))
                s.link(dve.tensor_scalar(wgt[:, :], we[:, :], wsum[:, :], tg[0:LQ, 1:2], ALU.mult, ALU.mult))
                s.link(dve.tensor_tensor_scan(cum[:, :], sel[:, :], zero8[:, :], 0.0, ALU.add, ALU.add))

            def choices(b, kind, prev):
                dve.wait_ge(t_ready, t_index(b, kind, "pos") + 1)
                s = Chain(dve, pos_step, N_POS * prev)
                s.link(dve.tensor_tensor(slot[:, :], pt[0:LQ, 0:E], seen[:, :], ALU.add))
                s.link(dve.tensor_tensor(seen[:, :], pt[0:LQ, E:2 * E], seen[:, :], ALU.add))
                s.link(dve.tensor_tensor(slot[:, :], slot[:, :], rowbase[:, :], ALU.add))
                s.link(dve.tensor_tensor(sk[:, :, :], rankc[:, :, :], cum[:, :].unsqueeze(1).broadcast_to([LQ, E, E]),
                                         ALU.is_equal))
                s.link(dve.tensor_tensor(sk[:, :, :], sk[:, :, :], sel[:, :].unsqueeze(1).broadcast_to([LQ, E, E]),
                                         ALU.mult))
                return s

            def slots_of(s, prev):
                s.link(dve.tensor_tensor(skv[:, :, :], sk[:, :, :], slot[:, :].unsqueeze(1).broadcast_to([LQ, E, E]),
                                         ALU.mult))
                s.link(dve.tensor_reduce(idf[:, :], skv[:, :, :], AX.X, ALU.add))
                s.link(dve.tensor_scalar(gone[:, :], rankv[:, :], cum[:, E - 1:E], OOB, ALU.is_gt, ALU.mult))
                s.link(dve.tensor_tensor(idf[:, :], idf[:, :], gone[:, :], ALU.add))
                dve.tensor_tensor(skv[:, :, :], sk[:, :, :], wgt[:, :].unsqueeze(1).broadcast_to([LQ, E, E]),
                                  ALU.mult).then_inc(idx_ready, 1)
                dve.wait_ge(idx_ready, 4 * prev + 1)
                dve.tensor_reduce(A["w_all"][:, bass.ds(E * prev, E)], skv[:, :, :], AX.X, ALU.add).then_inc(idx_ready, 1)
                dve.tensor_copy(A["i_all"][:, bass.ds(E * prev, E)], idf[:, :]).then_inc(idx_ready, 1)
                wait(dve, row_out, 32 * prev)
                dve.tensor_copy(idx[:, :], idf[:, 0:2]).then_inc(idx_ready, 1)
                dve.wait_ge(idx_ready, 4 * prev + 4)

            def iteration(b, kind, par):
                more, prev = kind != "last", kind != "first"
                skip = not more or isinstance(b, int) and b == B - 2
                for g in range(NG):
                    G = NG * b + g
                    shifted(G)
                    if g or prev:
                        normalise(G - 1, (g - 1) % NG)
                    if g == 1 and prev:
                        ln2_apply(b - 1)
                    if g == 3 and not skip:
                        ln1_apply(b + 2)
                    for i in range(GH):
                        if more and g % 2 == 0:
                            key_lo(b + 1, g // 2, i, 1 - par)
                        if g < NG - 1:
                            head_max(G + 1, i, par)
                        elif more:
                            head_max(G + 1, i, 1 - par)
                        if g == 0 and i == 0 and prev:
                            residual(b, kind, b - 1)
                        if g == 0 and i == 1 and more:
                            x_lo(b, kind, b + 1)
                        if g == 1 and i == 2 and more:
                            mask_row(b + 1, 1 - par)
                        if g == 2 and i == 0 and prev:
                            gate(b, kind, b - 1)
                        if g == 2 and i == 1 and more:
                            q_split(b, kind, b + 1)
                        if g == 2 and i == 2 and not skip:
                            ln1_stats(b + 2)
                        if g == 3 and i == 0 and prev:
                            gate_weights(b - 1)
                        if g == 3 and i == 1 and prev:
                            chosen = choices(b, kind, b - 1)
                        if g == 3 and i == 2 and prev:
                            slots_of(chosen, b - 1)
                    if g < NG - 1 or more:
                        diagonals(G + 1)

            split_weight(0, wkh, wkl)
            dve.memset(ones[:, :], 1.0).then_inc(setup_dve, 1)
            dve.memset(zero8[:, :], 0.0)
            dve.memset(seen[:, :], 0.0)
            dve.memset(A["table"][:, :], 0)
            dve.wait_ge(setup_dve, 1)
            dve.tensor_copy(onesr[:, :], ones[0:LQ, :]).then_inc(setup_dve, 1)
            split_weight(1, wvh, wvl)
            dve.wait_ge(const_in, 16 * NCONST)
            dve.tensor_scalar(mkey[:, :], mkey8[:, :], MASKED, None, ALU.mult).then_inc(setup_dve, 1)
            dve.wait_ge(setup_act, 1)
            dve.tensor_scalar(gbo[:, :], gbo[:, :], tg[0:LQ, 0:1], None, ALU.mult).then_inc(setup_dve, 1)
            ln1_stats(0)
            ln1_apply(0)
            mask_row(0, 0)
            for k in range(UK):
                key_lo(0, 0, k, 0)
            x_lo(0, "pro", 0)
            split_weight(2, wqh, wql)
            for k in range(UK):
                key_lo(0, 1, k, 0)
            q_split(0, "pro", 0)
            ln1_stats(1)
            ln1_apply(1)
            for h in range(GH):
                head_max(0, h, 0)
            diagonals(0)
            dve.wait_ge(setup_dve, 4)
            iteration(0, "first", 0)
            iteration(1, "mid", 1)
            with dve.Fori(1, B // 2 - 1) as i:
                iteration(2 * i, "mid", 0)
                iteration(2 * i + 1, "mid", 1)
            iteration(B - 2, "mid", 0)
            iteration(B - 1, "last", 1)
            normalise(NG * B - 1, NG - 1)
            residual(B, "epi", B - 1)
            ln2_apply(B - 1)
            gate(B, "epi", B - 1)
            gate_weights(B - 1)
            slots_of(choices(B, "epi", B - 1), B - 1)
            dve.wait_ge(units_in, 16)
            s = Chain(dve, units_step, 0)
            flat = craw[0:NU, :, :].rearrange("p c n -> p (c n)")
            work = prob[0:NU, 0:4, :].rearrange("p t n -> p (t n)")
            above, steps = work[:, 0:NU * CHUNKS], work[:, NU * CHUNKS:2 * NU * CHUNKS]
            size, row, active, rank, zeros, picked = (prob[0:NU, 4, k * NU:(k + 1) * NU] for k in range(6))

            def const(at, n=NU):
                return flat[:, at:at + n]

            s.link(dve.memset(zeros, 0.0))
            s.link(dve.tensor_tensor(above.rearrange("p (e n) -> p e n", e=E),
                                     seen[0:NU, :].unsqueeze(2).broadcast_to([NU, E, ROUNDS * CHUNKS]),
                                     const(C_THR, NU * CHUNKS).rearrange("p (e n) -> p e n", e=E), ALU.is_gt))
            s.link(dve.tensor_tensor(steps, above, const(C_DSIZE, NU * CHUNKS), ALU.mult))
            s.link(dve.tensor_reduce(size, steps.rearrange("p (u n) -> p u n", u=NU), AX.X, ALU.add))
            s.link(dve.tensor_tensor(steps, above, const(C_DROW, NU * CHUNKS), ALU.mult))
            s.link(dve.tensor_reduce(row, steps.rearrange("p (u n) -> p u n", u=NU), AX.X, ALU.add))
            s.link(dve.tensor_tensor(row, row, const(C_BASE), ALU.add))
            s.link(dve.tensor_scalar(active, size, 0.0, None, ALU.is_gt))
            s.link(dve.tensor_tensor_scan(rank, active, zeros, 0.0, ALU.add, ALU.add))
            s.link(dve.scalar_tensor_tensor(out=picked, in0=rank, scalar=flat[:, C_RANK:C_RANK + 1],
                                            in1=active, op0=ALU.is_equal, op1=ALU.mult))
            dve.tensor_copy(A["table"][:, T_TOTAL:T_TOTAL + 1], rank[0:1, NU - 1:NU])
            for k, values in enumerate((size, row, const(C_EXP))):
                s.link(dve.tensor_tensor_reduce(zeros, picked, values, 1.0, 0.0, ALU.mult, ALU.add,
                                                unit_v[:, k:k + 1]))
            dve.wait_ge(t_ready, t_index(B, "epi", "pos") + 2)
            table = A["table"]
            dve.tensor_copy(table[:, 0:3 * (NU + 1)].rearrange("p (k n) -> p k n", k=3)[:, :, 0:NU],
                            pt[0:1, 2 * E:2 * E + 3 * NU].rearrange("p (k n) -> p k n", k=3))
            sizes = pt[0:1, 2 * E:2 * E + NU]
            dve.tensor_scalar(table[:, T_ACTIVE:T_ACTIVE + NU], sizes, 0.0, None, ALU.is_gt)
            for at, k in ((T_IS2, 2), (T_IS3, 3), (T_IS4, 4)):
                dve.tensor_scalar(table[:, at:at + NU], sizes, float(k), None, ALU.is_equal)
            s.link(dve.tensor_reduce(choices_all[:, :], seen[0:1, :], AX.X, ALU.add))
            dve.tensor_scalar(table[:, T_TIE:T_TIE + 1], choices_all[:, :], float(2 * B * LQ), None, ALU.is_gt)

        @block.gpsimd
        def _(pool):
            def lay_queries(G, c, nxt=None):
                if nxt is not None:
                    wait(pool, qt_step, N_QT * (nxt + 1))
                wait(pool, s_ready, NT * G)
                for dst, src, done in ((qbh, qth, qb_hi), (qbl, qtl, qb_ready)):
                    pool.tensor_tensor(dst[:, :, :], f32(src[:, c, :]).unsqueeze(1).broadcast_to([P, GH, LQ]),
                                       blockm[:, :, :], ALU.mult).then_inc(done, 1)

            def sum_tiles(G):
                pool.wait_ge(p_ready, NT * (G + 1))
                wait(pool, pv_done, G)
                s = Chain(pool, sum_step, N_SUM * G)
                s.link(pool.tensor_tensor(acc[:, :, :], prob[0:KT, 0:2, :], prob[0:KT, 2:4, :], ALU.add))
                s.link(pool.tensor_tensor(acc[:, :, :], acc[:, :, :], prob[0:KT, 4:6, :], ALU.add))
                s.then(pool.tensor_tensor(acc[:, 0, :], acc[:, 0, :], acc[:, 1, :], ALU.add))

            def ctx_lo(b, half):
                pool.wait_ge(c_hi, 2 * b + half + 1)
                pool.tensor_tensor(cl[half][:, :, :], craw[:, :, :], f32(ch[half][:, :, :]), ALU.subtract).then_inc(c_lo, 1)

            def power(n, ready, want, dst, src, done):
                pool.wait_ge(ready, want)
                alone(pool, A["passed"])
                pool.tensor_scalar(dst[:, :], src[:, 1:2], EPS, None, ALU.add).then_inc(done, 1)
                pool.wait_ge(done, 2 * n + 1)
                pool.tensor_tensor(dst[:, :], dst[:, :], mhalf[:, :], ALU.pow).then_inc(done, 1)

            def residual_bias(b):
                pool.wait_ge(xres_in, 16 * (b + 1))
                pool.tensor_tensor(x1[:, :], x1[:, :], gbo[:, :], ALU.add).then_inc(xres_ready, 1)

            def store_rows(b):
                pool.wait_ge(x1_ready, b + 1)
                alone(pool, A["passed"])
                pool.dma_start(A["x1_d"][bass.ds(b, 1)].rearrange("b l d -> (b l) d"), x1[:, :]).then_inc(x1_out, 16)
                pool.wait_ge(ln2_step, N_LN2 * (b + 1))
                alone(pool, A["passed"])
                pool.dma_start(A["xn2_d"][bass.ds(b, 1)].rearrange("b l d -> (b l) d"), xn2[:, :]).then_inc(xn2_out, 16)

            def scatter(b):
                pool.wait_ge(idx_ready, 4 * (b + 1))
                pool.wait_ge(zero_out, 16 * (b + 1))
                alone(pool, A["passed"])
                for k in range(2):
                    pool.indirect_dma_start(A["slots"], bass.IndirectOffsetOnAxis(ap=idx[:, k:k + 1], axis=0), xn2[:, :], None,
                                            bounds_check=E * ROWS - 1, oob_is_err=False).then_inc(row_out, 16)

            def iteration(b, kind, par):
                more, prev = kind != "last", kind != "first"
                for g in range(NG):
                    G = NG * b + g
                    if g < NG - 1:
                        lay_queries(G + 1, g + 1)
                    elif more:
                        lay_queries(G + 1, 0, nxt=b + 1)
                    sum_tiles(G)
                    if g == 0 and prev:
                        power(b - 1, ln2_step, N_LN2 * (b - 1) + 2, rs2, mv2, ln2_pow)
                    if g == 2 and more and not (isinstance(b, int) and b == B - 2):
                        power(b + 2, ln1_step, N_LN1 * (b + 2) + 2, rstd, mv, ln1_pow)
                    if g == 1 and prev:
                        store_rows(b - 1)
                    if g == 3:
                        residual_bias(b)
                    if more and g == 0:
                        ctx_lo(b + 1, 1)
                    if more and g == 2 and not (isinstance(b, int) and b == B - 2):
                        ctx_lo(b + 2, 0)
                    if g == 3 and prev:
                        scatter(b - 1)

            pool.memset(mhalf[:, :], -0.5).then_inc(setup_pool, 1)
            pool.memset(A["zero"][:, :], 0.0).then_inc(setup_pool, 1)
            pool.wait_ge(setup_pool, 2)
            ctx_lo(0, 0)
            power(0, ln1_step, 2, rstd, mv, ln1_pow)
            ctx_lo(0, 1)
            pool.wait_ge(const_in, 16 * NCONST)
            ctx_lo(1, 0)
            power(1, ln1_step, N_LN1 + 2, rstd, mv, ln1_pow)
            pool.wait_ge(setup_dve, 4)
            lay_queries(0, 0, nxt=0)
            iteration(0, "first", 0)
            iteration(1, "mid", 1)
            with pool.Fori(1, B // 2 - 1) as i:
                iteration(2 * i, "mid", 0)
                iteration(2 * i + 1, "mid", 1)
            iteration(B - 2, "mid", 0)
            iteration(B - 1, "last", 1)
            power(B - 1, ln2_step, N_LN2 * (B - 1) + 2, rs2, mv2, ln2_pow)
            store_rows(B - 1)
            scatter(B - 1)
            pool.wait_ge(x1_out, 16 * B)
            pool.wait_ge(xn2_out, 16 * B)
            pool.wait_ge(row_out, 32 * B)


def expert_phase(nc, A):
    with ExitStack() as ctx:
        def sb(name, shape, dt=F32):
            return ctx.enter_context(nc.sbuf_tensor(name, shape, dt))

        def sem(name):
            return ctx.enter_context(nc.semaphore(name))

        wraw = [sb(f"wraw{i}", [P, 2, 2, D]) for i in range(RAW)]
        wh = [sb(f"wh{i}", [P, 2, D], F32R) for i in range(RING)]
        wl = [sb(f"wl{i}", [P, 2, D], F32R) for i in range(RING)]
        xr = sb("xr", [P, NS, D])
        xh, xl = sb("xh", [P, DC, SLOTS], F32R), sb("xl", [P, DC, SLOTS], F32R)
        hid = [sb(f"hid{i}", [P, SLOTS]) for i in range(2)]
        hh = [sb(f"hh{i}", [P, SLOTS], F32R) for i in range(RING)]
        hl = [sb(f"hl{i}", [P, SLOTS], F32R) for i in range(RING)]
        y = sb("y", [P, NS, D])
        ident = sb("identx", [P, P])
        b1 = sb("b1", [P, E * NJ])
        b2 = sb("b2", [P, E * D])
        y0 = [sb(f"y0_{i}", [LQ, D]) for i in range(PLACES)]
        y1 = [sb(f"y1_{i}", [LQ, D]) for i in range(PLACES)]
        xo = [sb(f"xo{i}", [LQ, D]) for i in range(PLACES)]
        pix = [sb(f"pix{i}", [LQ, 2], I32) for i in range(PLACES)]
        tix, tiw = sb("tix", [LQ, E], I32), sb("tiw", [LQ, E])

        pt = [ctx.enter_context(nc.psum_tensor(f"ptx{i}", [P, 512], F32)) for i in range(2)]
        ph = [ctx.enter_context(nc.psum_tensor(f"ph{i}", [P, 512], F32)) for i in range(2)]
        py = ctx.enter_context(nc.psum_tensor("py", [P, NS, 512], F32))

        raw_in = [sem(f"raw_in{i}") for i in range(RAW)]
        xr_in, y_out = sem("xr_in"), sem("y_out")
        pair_in = [sem(f"pair_in{i}") for i in range(PLACES)]
        res_in = [sem(f"res_in{i}") for i in range(PLACES)]
        o_out = [sem(f"o_out{i}") for i in range(PLACES)]
        dispatched, index_ready, tie_in, tie_step = sem("dispatched"), sem("index_ready"), sem("tie_in"), sem("tie_step")
        e_hi, e_lo = sem("e_hi"), sem("e_lo")
        xt_ready, xt_copied, xt_split = sem("xt_ready"), sem("xt_copied"), sem("xt_split")
        h_ready, h_gelu, h_hi, h_lo, w2_done = sem("h_ready"), sem("h_gelu"), sem("h_hi"), sem("h_lo"), sem("w2_done")
        y_copied, pair_step, pair_done = sem("y_copied"), sem("pair_step"), sem("pair_done")
        C_LO, C_W2, C_XS, C_GELU, C_HLO, C_YC, C_YO, C_OUT = 2 * RAW, RING, 2, 2, 2, 1, 16, 16
        table, w_all, i_all = A["table"], A["w_all"], A["i_all"]
        PAIRS = NJ // 2
        PART = 8
        block = ctx.enter_context(nc.Block())

        def entry(eng, at, n, most):
            return eng.value_load(table[0:1, bass.ds(n + at, 1)], min_val=0, max_val=most)

        def over_units(eng, unit):
            with eng.Fori(0, NU // PART) as part:
                some = entry(eng, T_ACTIVE, part * PART, 1)
                with eng.If(some > 0):
                    with eng.Fori(0, PART) as i:
                        n = part * PART + i
                        active = entry(eng, T_ACTIVE, n, 1)
                        with eng.If(active > 0):
                            unit(n)

        def by_size(eng, n, body):
            for k, at in ((2, T_IS2), (3, T_IS3), (4, T_IS4)):
                fits = entry(eng, at, n, 1)
                with eng.If(fits > 0):
                    body(n, k)

        def if_more(eng, n):
            return eng.If(entry(eng, T_ACTIVE, n + 1, 1) > 0)

        @block.sync
        def _(sp):
            def load_rows(row):
                sp.dma_start(xr[:, :, :], A["slots"][bass.ds(row, SLOTS), :].rearrange("(s p) d -> p s d", p=P)).then_inc(xr_in, 16)

            def load_weights(n, e, q):
                wait(sp, e_lo, C_LO + NJ * n + 2 * (q - RAW) + 2)
                if not isinstance(n, int):
                    alone(sp, A["passed"])
                for m, w in enumerate(("W1", "W2")):
                    sp.dma_start(wraw[q % RAW][:, m, :, :], A[w][bass.ds(e, 1), :, 2 * q:2 * q + 2, :]
                                 .rearrange("e p j n -> (e p) j n")).then_inc(raw_in[q % RAW], 16)

            sp.wait_ge(e_lo, C_LO)
            alone(sp, A["passed"])
            load_weights(0, entry(sp, T_EXPERT, 0, E - 1), 0)
            sp.wait_ge(dispatched, 1)
            alone(sp, A["passed"])
            load_rows(entry(sp, T_ROW, 0, E * ROWS - SLOTS))

            def unit(n):
                e = entry(sp, T_EXPERT, n, E - 1)
                for q in range(1, PAIRS):
                    load_weights(n, e, q)
                with if_more(sp, n):
                    sp.wait_ge(xt_ready, DC * (n + 1))
                    alone(sp, A["passed"])
                    load_rows(entry(sp, T_ROW, n + 1, E * ROWS - SLOTS))
                    load_weights(n + 1, entry(sp, T_EXPERT, n + 1, E - 1), 0)

            over_units(sp, unit)
            with sp.Fori(0, B // PLACES) as i:
                for k in range(PLACES):
                    sp.wait_ge(o_out[k], C_OUT + 16 * i)
                    alone(sp, A["passed"])
                    sp.dma_start(xo[k][:, :], A["x1_d"][bass.ds(PLACES * i + k, 1)].rearrange("b l d -> (b l) d")).then_inc(res_in[k], 16)

        @block.tensor
        def _(pe):
            pe.sem_inc(w2_done, C_W2)
            pe.wait_ge(o_out[0], 16)

            def transposes(n, chunks):
                pe.wait_ge(xr_in, 16 * n + 16)
                for c in chunks:
                    pe.wait_ge(xt_split, C_XS + DC * n + c - 1)
                    for s in range(NS):
                        last = pe.transpose(pt[c % 2][:, s * P:(s + 1) * P], xr[:, s, c * P:(c + 1) * P], ident[:, :])
                    last.then_inc(xt_ready, 1)

            def body(n, size):
                cols = size * P
                pe.wait_ge(xt_split, C_XS + DC * n + DC)

                def first(j):
                    pe.wait_ge(e_lo, C_LO + NJ * n + j + 1)
                    pe.wait_ge(h_gelu, C_GELU + NJ * n + j - 1)
                    k = 0
                    for c in range(DC):
                        w_h, w_l = wh[j % RING][:, 0, c * P:(c + 1) * P], wl[j % RING][:, 0, c * P:(c + 1) * P]
                        for w, x in ((w_h, xh), (w_h, xl), (w_l, xh)):
                            last = pe.matmul(ph[j % 2][:, 0:cols], w, x[:, c, 0:cols], start=(k == 0), stop=(k == 3 * DC - 1))
                            k += 1
                    last.then_inc(h_ready, 1)

                def second(j):
                    pe.wait_ge(h_lo, C_HLO + NJ * n + j + 1)
                    if j == 0:
                        pe.wait_ge(y_copied, C_YC + n)
                    a, b = j == 0, j == NJ - 1
                    for s in range(size):
                        h_h, h_l = hh[j % RING][:, s * P:(s + 1) * P], hl[j % RING][:, s * P:(s + 1) * P]
                        pe.matmul(py[:, s, :], h_h, wh[j % RING][:, 1, :], start=a, stop=False)
                        pe.matmul(py[:, s, :], h_h, wl[j % RING][:, 1, :], start=False, stop=False)
                        last = pe.matmul(py[:, s, :], h_l, wh[j % RING][:, 1, :], start=False, stop=b)
                    last.then_inc(w2_done, 1)

                for j in range(NJ):
                    first(j)
                    if j >= 2:
                        second(j - 2)
                with if_more(pe, n):
                    transposes(n + 1, (0, 1))
                second(NJ - 2)
                with if_more(pe, n):
                    transposes(n + 1, (2, 3))
                second(NJ - 1)

            transposes(0, range(DC))
            over_units(pe, lambda n: by_size(pe, n, body))

        @block.scalar
        def _(act):
            act.sem_inc(h_gelu, C_GELU)
            quarter = E // 4 * D
            act.dma_start(ident[:, :], A["ident"]).then_inc(o_out[0], 16)
            act.dma_start(b1[:, :].rearrange("p (e j) -> p e j", e=E), A["b1"].rearrange("e p j -> p e j")).then_inc(o_out[1], 16)
            act.dma_start(b2[:, 0:quarter], A["b2"][0:quarter].partition_broadcast(P)).then_inc(o_out[2], 16)
            act.dma_start(b2[:, quarter:2 * quarter], A["b2"][quarter:2 * quarter].partition_broadcast(P)).then_inc(o_out[3], 16)
            act.dma_start(b2[:, 2 * quarter:E * D], A["b2"][2 * quarter:E * D].partition_broadcast(P)).then_inc(y_out, 16)
            act.wait_ge(o_out[1], 16)

            def high(n, j):
                q = j // 2
                act.wait_ge(raw_in[q % RAW], 32 * (PAIRS // RAW * n + q // RAW) + 32)
                act.wait_ge(w2_done, C_W2 + NJ * n + j - RING + 1)
                act.activation(wh[j % RING][:, :, :], wraw[q % RAW][:, :, j % 2, :], ACT.Copy).then_inc(e_hi, 1)

            def start(n):
                for c in range(DC):
                    if c % 2 == 0:
                        high(n, c // 2)
                    act.wait_ge(xt_ready, DC * n + c + 1)
                    act.activation(xh[:, c, :], pt[c % 2][:, :], ACT.Copy).then_inc(xt_copied, 1)

            def body(n, size):
                cols = size * P
                e = entry(act, T_EXPERT, n, E - 1)
                for j in range(NJ):
                    if j + 2 < NJ:
                        high(n, j + 2)
                    act.wait_ge(h_ready, NJ * n + j + 1)
                    act.wait_ge(h_lo, C_HLO + NJ * n + j - 1)
                    alone(act, A["passed"])
                    act.activation(hid[j % 2][:, 0:cols], ph[j % 2][:, 0:cols], ACT.Gelu,
                                   bias=b1[:, bass.ds(e * NJ + j, 1)]).then_inc(h_gelu, 1)
                with if_more(act, n):
                    start(n + 1)
                act.wait_ge(y_copied, C_YC + n + 1)
                alone(act, A["passed"])
                act.dma_start(A["slots"][bass.ds(entry(act, T_ROW, n, E * ROWS - SLOTS), cols), :]
                              .rearrange("(s p) d -> p s d", p=P), y[:, 0:size, :]).then_inc(y_out, 16)

            start(0)
            over_units(act, lambda n: by_size(act, n, body))
            with act.Fori(0, B // PLACES) as i:
                for k in range(PLACES):
                    act.wait_ge(pair_done, PLACES * i + k + 1)
                    act.dma_start(A["out"][bass.ds(PLACES * i + k, 1)].rearrange("b l d -> (b l) d"), y1[k][:, :]).then_inc(o_out[k], 16)
            for k in range(PLACES):
                act.wait_ge(o_out[k], C_OUT + 16 * (B // PLACES))

        @block.vector
        def _(dve):
            dve.sem_inc(xt_split, C_XS)
            dve.sem_inc(h_lo, C_HLO)
            dve.sem_inc(y_copied, C_YC)
            dve.wait_ge(o_out[2], 16)
            dve.wait_ge(o_out[3], 16)
            dve.wait_ge(y_out, 16)

            def start(n):
                for c in range(DC):
                    dve.wait_ge(xt_copied, DC * n + c + 1)
                    dve.tensor_tensor(xl[:, c, :], pt[c % 2][:, :], f32(xh[:, c, :]), ALU.subtract).then_inc(xt_split, 1)

            def body(n, size):
                cols = size * P
                e = entry(dve, T_EXPERT, n, E - 1)
                for j in range(NJ):
                    dve.wait_ge(h_gelu, C_GELU + NJ * n + j + 1)
                    dve.wait_ge(w2_done, C_W2 + NJ * n + j - RING + 1)
                    dve.tensor_copy(hh[j % RING][:, 0:cols], hid[j % 2][:, 0:cols]).then_inc(h_hi, 1)
                    dve.wait_ge(h_hi, NJ * n + j + 1)
                    dve.tensor_tensor(hl[j % RING][:, 0:cols], hid[j % 2][:, 0:cols], f32(hh[j % RING][:, 0:cols]),
                                      ALU.subtract).then_inc(h_lo, 1)
                with if_more(dve, n):
                    start(n + 1)
                dve.wait_ge(w2_done, C_W2 + NJ * n + NJ)
                dve.wait_ge(y_out, C_YO + 16 * n)
                dve.tensor_tensor(y[:, 0:size, :], py[:, 0:size, :],
                                  b2[:, bass.ds(e * D, D)].unsqueeze(1).broadcast_to([P, size, D]),
                                  ALU.add).then_inc(y_copied, 1)

            start(0)
            over_units(dve, lambda n: by_size(dve, n, body))
            with dve.Fori(0, B // PLACES) as i:
                for k in range(PLACES):
                    at = PLACES * E * i + E * k
                    dve.wait_ge(res_in[k], 16 * i + 16)
                    dve.wait_ge(pair_in[k], 32 * i + 32)
                    dve.scalar_tensor_tensor(out=y0[k][:, :], in0=y0[k][:, :], scalar=w_all[:, bass.ds(at, 1)],
                                             in1=xo[k][:, :], op0=ALU.mult, op1=ALU.add).then_inc(pair_step, 1)
                    dve.wait_ge(pair_step, PLACES * i + k + 1)
                    dve.scalar_tensor_tensor(out=y1[k][:, :], in0=y1[k][:, :], scalar=w_all[:, bass.ds(at + 1, 1)],
                                             in1=y0[k][:, :], op0=ALU.mult, op1=ALU.add).then_inc(pair_done, 1)

        @block.gpsimd
        def _(pool):
            pool.sem_inc(e_lo, C_LO)
            tie = pool.value_load(table[0:1, T_TIE:T_TIE + 1], min_val=0, max_val=1)
            total = pool.value_load(table[0:1, T_TOTAL:T_TOTAL + 1], min_val=1, max_val=NU)
            with pool.If(tie > 0):
                with pool.Fori(0, B) as b:
                    pool.dma_start(y0[0][:, :], A["xn2_d"][bass.ds(b, 1)].rearrange("b l d -> (b l) d")).then_inc(tie_in, 16)
                    pool.wait_ge(tie_in, 16 * (E - 1) * b + 16)
                    alone(pool, A["passed"])
                    pool.tensor_copy(tix[:, :], i_all[:, bass.ds(E * b, E)]).then_inc(tie_step, 1)
                    pool.wait_ge(tie_step, b + 1)
                    alone(pool, A["passed"])
                    for k in range(2, E):
                        pool.indirect_dma_start(A["slots"], bass.IndirectOffsetOnAxis(ap=tix[:, k:k + 1], axis=0), y0[0][:, :], None,
                                                bounds_check=E * ROWS - 1, oob_is_err=False).then_inc(tie_in, 16)
                        pool.wait_ge(tie_in, 16 * (E - 1) * b + 16 * k)
                        alone(pool, A["passed"])
            pool.sem_inc(dispatched, 1)


            def low(n, j):
                pool.wait_ge(e_hi, NJ * n + j + 1)
                pool.tensor_tensor(wl[j % RING][:, :, :], wraw[(j // 2) % RAW][:, :, j % 2, :], f32(wh[j % RING][:, :, :]),
                                   ALU.subtract).then_inc(e_lo, 1)

            def unit(n):
                for j in range(2, NJ):
                    low(n, j)
                with if_more(pool, n):
                    low(n + 1, 0)
                    low(n + 1, 1)

            low(0, 0)
            low(0, 1)
            over_units(pool, unit)
            pool.wait_ge(y_out, C_YO + 16 * total)
            alone(pool, A["passed"])
            with pool.Fori(0, B // PLACES) as i:
                for k in range(PLACES):
                    pool.wait_ge(o_out[k], C_OUT + 16 * i)
                    alone(pool, A["passed"])
                    pool.tensor_copy(pix[k][:, :], i_all[:, bass.ds(PLACES * E * i + E * k, 2)]).then_inc(index_ready, 1)
                    pool.wait_ge(index_ready, PLACES * i + k + 1)
                    alone(pool, A["passed"])
                    for m, dst in enumerate((y0[k], y1[k])):
                        pool.indirect_dma_start(dst[:, :], None, A["slots"], bass.IndirectOffsetOnAxis(ap=pix[k][:, m:m + 1], axis=0),
                                                bounds_check=E * ROWS - 1, oob_is_err=False).then_inc(pair_in[k], 16)
            with pool.If(tie > 0):
                for k in range(PLACES):
                    pool.wait_ge(o_out[k], C_OUT + 16 * (B // PLACES))
                    alone(pool, A["passed"])
                with pool.Fori(0, B) as b:
                    t_in, t_st = 16 * E * b + 16 * B * (E - 1), (3 * (E - 2) + 1) * b + B
                    pool.dma_start(y0[0][:, :], A["out"][bass.ds(b, 1)].rearrange("b l d -> (b l) d")).then_inc(tie_in, 16)
                    pool.wait_ge(tie_in, t_in + 16)
                    alone(pool, A["passed"])
                    pool.tensor_copy(tiw[:, :], w_all[:, bass.ds(E * b, E)])
                    pool.tensor_copy(tix[:, :], i_all[:, bass.ds(E * b, E)]).then_inc(tie_step, 1)
                    pool.wait_ge(tie_step, t_st + 1)
                    alone(pool, A["passed"])
                    for k in range(2, E):
                        pool.memset(y0[1][:, :], 0.0).then_inc(tie_step, 1)
                        pool.wait_ge(tie_step, t_st + 3 * (k - 2) + 2)
                        alone(pool, A["passed"])
                        pool.indirect_dma_start(y0[1][:, :], None, A["slots"], bass.IndirectOffsetOnAxis(ap=tix[:, k:k + 1], axis=0),
                                                bounds_check=E * ROWS - 1, oob_is_err=False).then_inc(tie_in, 16)
                        pool.wait_ge(tie_in, t_in + 16 * k)
                        alone(pool, A["passed"])
                        pool.tensor_scalar(y0[1][:, :], y0[1][:, :], tiw[:, k:k + 1], None, ALU.mult).then_inc(tie_step, 1)
                        pool.wait_ge(tie_step, t_st + 3 * (k - 2) + 3)
                        alone(pool, A["passed"])
                        pool.tensor_tensor(y0[0][:, :], y0[0][:, :], y0[1][:, :], ALU.add).then_inc(tie_step, 1)
                        pool.wait_ge(tie_step, t_st + 3 * (k - 2) + 4)
                        alone(pool, A["passed"])
                    pool.dma_start(A["out"][bass.ds(b, 1)].rearrange("b l d -> (b l) d"), y0[0][:, :]).then_inc(tie_in, 16)
                    pool.wait_ge(tie_in, t_in + 16 * E)
                    alone(pool, A["passed"])
            pool.nop()


def gated_block(nc, A):
    A["slots"] = nc.dram_tensor("expert_slots", [E * ROWS, D], F32, kind="Internal").ap()
    A["x1_d"] = nc.dram_tensor("after_attention", [B, LQ, D], F32, kind="Internal").ap()
    A["xn2_d"] = nc.dram_tensor("normalised", [B, LQ, D], F32, kind="Internal").ap()
    with ExitStack() as ctx:
        A["w_all"] = ctx.enter_context(nc.sbuf_tensor("w_all", [LQ, B * E], F32))
        A["i_all"] = ctx.enter_context(nc.sbuf_tensor("i_all", [LQ, B * E], I32))
        A["table"] = ctx.enter_context(nc.sbuf_tensor("table", [1, T_TOTAL + 1], I32))
        A["zero"] = ctx.enter_context(nc.sbuf_tensor("zero", [P, D], F32))
        A["passed"] = ctx.enter_context(nc.semaphore("passed"))
        attention_phase(nc, A)
        expert_phase(nc, A)


def unit_constants(np):
    sizes = np.array([unit_sizes(c) for c in range(CHUNKS + 1)])
    starts = np.cumsum(sizes, 1) - sizes
    starts[sizes == 0] = 0
    row = np.concatenate([
        np.tile(np.arange(CHUNKS) * P, NU),
        np.tile(np.diff(sizes, axis=0).T.reshape(-1), E),
        np.tile(np.diff(starts, axis=0).T.reshape(-1) * P, E),
        np.add.outer(np.arange(E) * ROWS, np.zeros(ROUNDS)).reshape(-1),
        np.repeat(np.arange(E), ROUNDS)])
    return np.concatenate([np.tile(row, (NU, 1)), np.arange(1, NU + 1)[:, None]], 1).astype(np.float32)


def kernel(x, ctx_1024, mask_Bx1x1xS2_bf0, g_xattn, g_ffn, L0_xattn_W_q, L0_xattn_b_q, L0_xattn_W_k, L0_xattn_b_k,
           L0_xattn_W_v, L0_xattn_b_v, L0_xattn_W_o, L0_xattn_b_o, L0_ffn_W1, L0_ffn_b1, L0_ffn_W2, L0_ffn_b2,
           L0_ffn_Wr, L0_ffn_br):
    import numpy as np
    import concourse.bacc as bacc
    from concourse.bass_utils import run_bass_kernel_spmd

    def rows(a):
        return np.asarray(a).T.reshape(DC, P, -1).transpose(1, 0, 2)

    def columns(a):
        return np.asarray(a).reshape(DC, P).T

    mask = np.pad(np.asarray(mask_Bx1x1xS2_bf0).reshape(B, S), ((0, 0), (0, SP_ - S)), constant_values=True)
    arrays = {
        "x": np.asarray(x),
        "ctx": np.asarray(ctx_1024).transpose(0, 2, 1).reshape(B, DC, P, S).transpose(0, 2, 1, 3),
        "mrow": mask,
        "mkey": mask.reshape(B, NT, KT).transpose(2, 0, 1).reshape(KT, B * NT),
        "gx": np.asarray(g_xattn), "gf": np.asarray(g_ffn),
        "wq": rows(L0_xattn_W_q), "wk": rows(L0_xattn_W_k), "wv": rows(L0_xattn_W_v), "wo": rows(L0_xattn_W_o),
        "bq": columns(L0_xattn_b_q), "bk": columns(L0_xattn_b_k), "bv": columns(L0_xattn_b_v),
        "bo": np.asarray(L0_xattn_b_o),
        "wr": np.asarray(L0_ffn_Wr).reshape(DC, P, E).transpose(1, 0, 2), "br": np.asarray(L0_ffn_br),
        "W1": np.asarray(L0_ffn_W1).reshape(E, DC, P, NJ, P).transpose(0, 2, 3, 1, 4).reshape(E, P, NJ, D),
        "W2": np.asarray(L0_ffn_W2).reshape(E, NJ, P, D).transpose(0, 2, 1, 3),
        "b1": np.asarray(L0_ffn_b1).reshape(E, NJ, P).transpose(0, 2, 1),
        "b2": np.asarray(L0_ffn_b2).reshape(E * D),
        "ident": np.eye(P, dtype=np.float32),
        "tri": np.triu(np.ones((LQ, LQ), np.float32), 1),
        "blockm": np.repeat(np.repeat(np.eye(GH, dtype=np.float32), DK, 0)[:, :, None], LQ, 2),
        "rankc": np.broadcast_to(np.arange(1, E + 1, dtype=np.float32)[None, :, None], (LQ, E, E)),
        "rankv": np.broadcast_to(np.arange(1, E + 1, dtype=np.float32)[None, :], (LQ, E)),
        "rowbase": np.broadcast_to(np.arange(E, dtype=np.float32)[None, :] * ROWS, (LQ, E)),
"units": unit_constants(np),
    }
    nc = bacc.Bacc("TRN2", target_bir_lowering=False, num_devices=1)
    feeds, aps = {}, {}
    for name, a in arrays.items():
        a = np.ascontiguousarray(a)
        feeds[f"in_{name}"] = a
        aps[name] = nc.dram_tensor(f"in_{name}", a.shape, mybir.dt.from_np(a.dtype), kind="ExternalInput").ap()
    aps["out"] = nc.dram_tensor("out", (B, LQ, D), F32, kind="ExternalOutput").ap()
    gated_block(nc, aps)
    result = run_bass_kernel_spmd(nc, [feeds], core_ids=[0])
    return result.results[0]["out"]
```

```python
from contextlib import ExitStack

import concourse.bass as bass
from concourse import mybir

B, LQ, D = 16, 100, 512
S = 722
H, DK = 16, 32
E, HID = 8, 2048
EPS = 1e-5
SCALE = float(DK) ** -0.5

P = 128
DC = D // P
KT = 122
NT = 6
SP_ = KT * NT
HALF = SP_ // 2
HT = NT // 2
REAL = (HALF, S - HALF)
GH = P // DK
NG = H // GH
NQ = GH * LQ
UK = DC
UH = UK + HT
DIAGONALS = (slice(0, GH - 1), slice(GH - 1, GH))
SLOTS = 512
ROUNDS = 4
ROWS = SLOTS * ROUNDS
NS = SLOTS // P
NJ = HID // P
RAW = 4
CHUNKS = -(-B * LQ // P)
NU = E * ROUNDS
PLACES = 8
RING = 8
AHEAD = 4
HRING = 4
MASKED = -3.0e38
OOB = float(1 << 20)

ALU = mybir.AluOpType
ACT = mybir.ActivationFunctionType
AX = mybir.AxisListType
F32 = mybir.dt.float32
F32R = mybir.dt.float32r
BF16 = mybir.dt.bfloat16
I32 = mybir.dt.int32
U8 = mybir.dt.uint8

T_PRO = ["xT", "Q", "QT", "bc3"]
T_0 = ["xT", "bc0", "Q", "bc1", "QT", "bc2", "bc3"]
T_MID = ["op", "xT", "bc0", "Q", "rT", "bc1", "rm", "QT", "bc2", "pos", "bc3"]
T_LAST = ["op", "bc0", "rT", "bc1", "rm", "bc2", "pos"]
T_EPI = ["op", "rT", "rm", "pos"]


def t_index(b, kind, name):
    if kind == "pro":
        return T_PRO.index(name)
    if kind == "first":
        return len(T_PRO) + T_0.index(name)
    if kind == "epi":
        return len(T_PRO) + len(T_0) + (B - 2) * len(T_MID) + len(T_LAST) + T_EPI.index(name)
    order = T_MID if kind == "mid" else T_LAST
    return len(T_PRO) + len(T_0) - len(T_MID) + len(T_MID) * b + order.index(name)


def unit_sizes(chunks):
    if chunks == 0:
        return [0] * ROUNDS
    units = -(-chunks // NS)
    return [max(2, chunks // units + (r < chunks % units)) if r < units else 0 for r in range(ROUNDS)]


T_SIZE, T_ROW, T_EXPERT = (k * (NU + 1) for k in range(3))
T_TIE = 3 * (NU + 1)
T_TOTAL = T_TIE + 1
C_THR, C_DSIZE, C_DROW, C_BASE, C_EXP = (0, NU * CHUNKS, 2 * NU * CHUNKS, 3 * NU * CHUNKS, 3 * NU * CHUNKS + NU)
C_RANK = C_EXP + NU


def f32(ap):
    return ap.bitcast(F32)


def wait(eng, sem, value):
    if isinstance(value, int) and value <= 0:
        return
    eng.wait_ge(sem, value)


def alone(eng, passed):
    eng.sem_inc(passed, 1)


class Chain:

    def __init__(self, eng, sem, base, passed=None):
        self.eng, self.sem, self.base, self.n, self.passed = eng, sem, base, 0, passed

    def then(self, ins):
        ins.then_inc(self.sem, 1)
        self.n += 1

    def link(self, ins):
        self.then(ins)
        self.eng.wait_ge(self.sem, self.base + self.n)
        if self.passed is not None:
            alone(self.eng, self.passed)


def attention_phase(nc, A):
    with ExitStack() as ctx:
        def sb(name, shape, dt=F32):
            return ctx.enter_context(nc.sbuf_tensor(name, shape, dt))

        def sem(name):
            return ctx.enter_context(nc.semaphore(name))

        wkh, wkl = sb("wkh", [P, DC, D], F32R), sb("wkl", [P, DC, D], F32R)
        wvh, wvl = sb("wvh", [P, DC, D], F32R), sb("wvl", [P, DC, D], F32R)
        wqh, wql = sb("wqh", [P, DC, D], F32R), sb("wql", [P, DC, D], F32R)
        wo = sb("wo", [P, DC, D])
        kh = [sb(f"kh{i}", [P, NG, SP_], F32R) for i in range(2)]
        kl = [sb(f"kl{i}", [P, NG, SP_], F32R) for i in range(2)]
        vv = [sb(f"vv{i}", [KT, NT, D]) for i in range(2)]
        craw = sb("craw", [P, DC, HALF])
        ch = [sb(f"ch{i}", [P, DC, HALF], F32R) for i in range(2)]
        cl = [sb(f"cl{i}", [P, DC, HALF], F32R) for i in range(2)]
        prob = sb("prob", [P, NT, NQ])
        acc = sb("acc", [KT, 2, NQ])
        shift = sb("shift", [KT, NQ])
        diag = sb("diag", [LQ, GH, LQ], F32R)
        mx = sb("mx", [LQ, GH])
        junk = sb("junk", [LQ, 2, HALF], BF16)
        qbh, qbl = sb("qbh", [P, GH, LQ], F32R), sb("qbl", [P, GH, LQ], F32R)
        qt = sb("qt", [P, NG, LQ])
        qth, qtl = sb("qth", [P, NG, LQ], F32R), sb("qtl", [P, NG, LQ], F32R)
        qs = sb("qs", [LQ, D])
        xn = sb("xn", [LQ, D])
        xth, xtl = sb("xth", [P, DC, LQ], F32R), sb("xtl", [P, DC, LQ], F32R)
        rden = sb("rden", [P, LQ])
        ot = sb("ot", [P, NG, LQ])
        x1 = sb("x1", [LQ, D])
        xn2 = sb("xn2", [LQ, D])
        x2t = qt
        mrow8 = sb("mrow8", [LQ, SP_], U8)
        mrow = [sb(f"mrow{i}", [LQ, 2, HALF], BF16) for i in range(2)]
        mkey8 = sb("mkey8", [KT, B * NT], U8)
        mkey = sb("mkey", [KT, B * NT])
        ident, tri = sb("ident", [P, P]), sb("tri", [LQ, LQ])
        blockm = sb("blockm", [P, GH, LQ])
        rankc = sb("rankc", [LQ, E, E])
        rankv = sb("rankv", [LQ, E])
        rowbase = sb("rowbase", [LQ, E])
        ones = sb("ones", [P, P])
        onesr = sb("onesr", [LQ, P], F32R)
        gbo = sb("gbo", [LQ, D])
        bq, bk, bv = sb("bq", [P, NG]), sb("bk", [P, NG]), sb("bv", [P, NG])
        wr = sb("wr", [P, DC, E])
        br = sb("br", [LQ, E])
        gx = sb("gx", [P, 2])
        tg = sb("tg", [P, 2])
        st = sb("st", [LQ, 6])
        mv = sb("mv", [LQ, 2])
        rstd, rs2 = sb("rstd", [LQ, 1]), sb("rs2", [LQ, 1])
        mhalf = sb("mhalf", [LQ, 1])
        st2 = sb("st2", [LQ, 6])
        mv2 = sb("mv2", [LQ, 2])
        lg, m8, nm1 = sb("lg", [LQ, E]), sb("m8", [LQ, 8]), sb("nm1", [LQ, 1])
        ex, sel, cum = sb("ex", [LQ, E]), sb("sel", [LQ, E]), sb("cum", [LQ, E])
        zero8 = sb("zero8", [LQ, E])
        we, wsum, wgt = sb("we", [LQ, E]), sb("wsum", [LQ, 1]), sb("wgt", [LQ, E])
        seen, slot = sb("seen", [LQ, E]), sb("slot", [LQ, E])
        sk, skv = sb("sk", [LQ, E, E]), sb("skv", [LQ, E, E])
        idf, gone = sb("idf", [LQ, E]), sb("gone", [LQ, E])
        idx = sb("idx", [LQ, 2], I32)
        choices_all, unit_v = sb("choices_all", [1, 1]), sb("unit_v", [NU, 3])

        pa = [ctx.enter_context(nc.psum_tensor(f"pa{i}", [P, 512], F32)) for i in range(2)]
        psc = [ctx.enter_context(nc.psum_tensor(f"psc{i}", [P, 512], F32)) for i in range(2)]
        pm = ctx.enter_context(nc.psum_tensor("pm", [P, 2, 512], F32))
        po = ctx.enter_context(nc.psum_tensor("po", [P, 512], F32))
        pt = ctx.enter_context(nc.psum_tensor("pt", [P, 512], F32))

        def s_bank(t):
            return pm[0:KT, t - 2, 0:NQ] if t in (2, 3) else psc[t % 2][0:KT, 0:NQ]

        w_in = [sem(f"w_in_{n}") for n in "kvqo"]
        const_in, units_in, c_in, x_in = sem("const_in"), sem("units_in"), sem("c_in"), sem("x_in")
        units_step = sem("units_step")
        m_in, xres_in = sem("m_in"), sem("xres_in")
        row_out, x1_out, xn2_out, zero_out = sem("row_out"), sem("x1_out"), sem("xn2_out"), sem("zero_out")
        w_hi, w_lo = sem("w_hi"), sem("w_lo")
        setup_act, setup_dve, setup_pool = sem("setup_act"), sem("setup_dve"), sem("setup_pool")
        c_hi, c_lo = sem("c_hi"), sem("c_lo")
        proj_ready, k_hi, k_lo, v_copy = sem("proj_ready"), sem("k_hi"), sem("k_lo"), sem("v_copy")
        s_ready, s_used, p_ready = sem("s_ready"), sem("s_used"), sem("p_ready")
        max_ready, max_used, diag_ready = sem("max_ready"), sem("max_used"), sem("diag_ready")
        shift_ready, qb_hi, qb_ready = sem("shift_ready"), sem("qb_hi"), sem("qb_ready")
        sum_step, pv_done, norm_step = sem("sum_step"), sem("pv_done"), sem("norm_step")
        t_ready = sem("t_ready")
        ln1_step, ln1_pow, xt_hi, xt_lo = sem("ln1_step"), sem("ln1_pow"), sem("xt_hi"), sem("xt_lo")
        qs_ready, qt_step, m_used = sem("qs_ready"), sem("qt_step"), sem("m_used")
        xres_ready, x1_ready, ln2_step, ln2_pow = sem("xres_ready"), sem("x1_ready"), sem("ln2_step"), sem("ln2_pow")
        x2t_ready, gate_step, gate_exp = sem("x2t_ready"), sem("gate_step"), sem("gate_exp")
        pos_step, idx_ready = sem("pos_step"), sem("idx_ready")

        NCONST = 15
        N_LN1, N_LN2, N_GATE, N_POS, N_NORM, N_QT, N_SUM = 3, 3, 7, 9, 3, 3, 3
        block = ctx.enter_context(nc.Block())

        @block.sync
        def _(sp):
            flat = prob[:, :, :].rearrange("p t n -> p (t n)")

            def load_w(n, name):
                wait(sp, w_lo, n)
                sp.dma_start(flat[:, 0:DC * D], A[name].rearrange("p c n -> p (c n)")).then_inc(w_in[n], 16)

            def load_ctx(b, half):
                wait(sp, c_lo, 2 * b + half)
                alone(sp, A["passed"])
                sp.dma_start(craw[:, :, 0:REAL[half]],
                             A["ctx"][bass.ds(b, 1), :, :, half * HALF:half * HALF + REAL[half]]
                             .rearrange("b p c n -> (b p) c n")).then_inc(c_in, 16)

            def load_x(b):
                wait(sp, xt_hi, b)
                alone(sp, A["passed"])
                sp.dma_start(xn[:, :], A["x"][bass.ds(b, 1)].rearrange("b l d -> (b l) d")).then_inc(x_in, 16)

            def load_mask(b):
                wait(sp, m_used, b)
                alone(sp, A["passed"])
                sp.dma_start(mrow8[:, :], A["mrow"][bass.ds(b, 1), :].rearrange("b s -> (b s)")
                             .partition_broadcast(LQ)).then_inc(m_in, 16)

            def load_res(b):
                wait(sp, x1_out, 16 * b)
                alone(sp, A["passed"])
                wait(sp, ln2_step, N_LN2 * b)
                alone(sp, A["passed"])
                sp.dma_start(x1[:, :], A["x"][bass.ds(b, 1)].rearrange("b l d -> (b l) d")).then_inc(xres_in, 16)

            def clear_slots(b):
                wait(sp, zero_out, 16 * b)
                alone(sp, A["passed"])
                sp.dma_start(A["slots"].rearrange("(e n p) d -> n p e d", e=E, p=P)[bass.ds(b, 1)]
                             .rearrange("n p e d -> (n p) e d"),
                             A["zero"][:, :].unsqueeze(1).broadcast_to([P, E, D])).then_inc(zero_out, 16)

            def batch(b):
                load_ctx(b, 0)
                load_x(b)
                load_mask(b)
                load_ctx(b, 1)
                clear_slots(b)

            load_w(0, "wk")
            sp.dma_start(craw[:, :, 0:REAL[0]], A["ctx"][0, :, :, 0:REAL[0]]).then_inc(c_in, 16)
            for dst, src in ((ident, A["ident"]), (tri, A["tri"]), (blockm, A["blockm"]), (rankc, A["rankc"]),
                             (rankv, A["rankv"]), (rowbase, A["rowbase"]), (bq, A["bq"]), (bk, A["bk"]), (bv, A["bv"]),
                             (wr, A["wr"]), (mkey8, A["mkey"])):
                sp.dma_start(dst[:], src).then_inc(const_in, 16)
            sp.dma_start(br[:, :], A["br"].partition_broadcast(LQ)).then_inc(const_in, 16)
            sp.dma_start(gbo[:, :], A["bo"].partition_broadcast(LQ)).then_inc(const_in, 16)
            sp.dma_start(gx[:, 0:1], A["gx"].partition_broadcast(P)).then_inc(const_in, 16)
            sp.dma_start(gx[:, 1:2], A["gf"].partition_broadcast(P)).then_inc(const_in, 16)
            load_x(0)
            load_mask(0)
            load_w(1, "wv")
            load_w(2, "wq")
            load_ctx(0, 1)
            sp.dma_start(wo[:, :, :], A["wo"]).then_inc(w_in[3], 16)
            load_res(0)
            sp.wait_ge(setup_pool, 2)
            clear_slots(0)
            batch(1)
            with sp.Fori(2, B) as b:
                batch(b)
                load_res(b - 1)
            load_res(B - 1)
            sp.wait_ge(c_lo, 2 * B)
            sp.dma_start(craw[0:NU, :, :].rearrange("p c n -> p (c n)")[:, 0:C_RANK + 1], A["units"]).then_inc(units_in, 16)

        def pe_units(pe, nxt, half):
            hh = 2 * nxt + half

            def bank(k):
                return pa[(UH * half + k) % 2]

            def unit(k):
                if k == 0:
                    wait(pe, v_copy, HT * hh - 1)
                elif k == 1:
                    wait(pe, v_copy, HT * hh)
                elif k < UK + 2:
                    wait(pe, k_lo, UK * hh + k - 1)
                else:
                    wait(pe, v_copy, HT * hh + k - UK - 1)
                if k == 0:
                    wait(pe, c_lo, hh + 1)
                if k < UK:
                    o = bank(k)[:, 0:HALF]
                    n = 0
                    for c in range(DC):
                        wh, wl = wkh[:, c, k * P:(k + 1) * P], wkl[:, c, k * P:(k + 1) * P]
                        for w, x in ((wh, ch[half]), (wh, cl[half]), (wl, ch[half])):
                            last = pe.matmul(o, w, x[:, c, :], start=(n == 0), stop=(n == 3 * DC - 1))
                            n += 1
                else:
                    t = k - UK
                    o = bank(k)[0:KT, 0:D]
                    n = 0
                    for c in range(DC):
                        xh, xl = ch[half][:, c, t * KT:(t + 1) * KT], cl[half][:, c, t * KT:(t + 1) * KT]
                        for x, w in ((xh, wvh), (xl, wvh), (xh, wvl)):
                            last = pe.matmul(o, x, w[:, c, :], start=(n == 0), stop=(n == 3 * DC - 1))
                            n += 1
                last.then_inc(proj_ready, 1)
            return unit

        @block.tensor
        def _(pe):
            def t_use(b, kind, name):
                order = {"pro": T_PRO, "first": T_0, "mid": T_MID, "last": T_LAST, "epi": T_EPI}[kind]
                at = order.index(name)
                if kind == "pro":
                    b = -1
                    if at == 0:
                        return
                if at:
                    before = order[at - 1]
                elif kind == "epi":
                    before, b = "pos", b - 1
                else:
                    before, b = "bc3", b - 1
                read_by = {"xT": (xt_lo, b + 2), "Q": (qs_ready, b + 2), "QT": (qt_step, N_QT * (b + 1) + 1),
                           "op": (x1_ready, b), "rT": (x2t_ready, b), "rm": (gate_step, N_GATE * (b - 1) + 1),
                           "pos": (pos_step, N_POS * (b - 1) + 2)}
                if before in read_by:
                    pe.wait_ge(*read_by[before])
                else:
                    pe.wait_ge(shift_ready, NG * b + int(before[2]) + 2)

            def x_transposes(b, kind, nxt):
                wait(pe, ln1_step, N_LN1 * (nxt + 1))
                t_use(b, kind, "xT")
                for c in range(DC):
                    last = pe.transpose(pt[:, c * LQ:(c + 1) * LQ], xn[:, c * P:(c + 1) * P], ident[0:LQ, 0:LQ])
                last.then_inc(t_ready, 1)

            def q_product(b, kind, nxt):
                wait(pe, xt_lo, nxt + 1)
                if kind == "pro":
                    wait(pe, w_lo, 3)
                t_use(b, kind, "Q")
                n = 0
                for c in range(DC):
                    for x, w in ((xth, wqh), (xth, wql), (xtl, wqh)):
                        last = pe.matmul(pt[0:LQ, 0:D], x[:, c, :], w[:, c, :], start=(n == 0), stop=(n == 3 * DC - 1))
                        n += 1
                last.then_inc(t_ready, 1)

            def q_transposes(b, kind, nxt):
                wait(pe, qs_ready, nxt + 1)
                t_use(b, kind, "QT")
                for c in range(DC):
                    last = pe.transpose(pt[:, c * LQ:(c + 1) * LQ], qs[:, c * P:(c + 1) * P], ident[0:LQ, 0:LQ])
                last.then_inc(t_ready, 1)

            def max_head(G, kpar, c, h, nxt=None):
                if h == 0:
                    wait(pe, qb_hi, G + 1)
                    if nxt is not None:
                        wait(pe, k_lo, 2 * UK * (nxt + 1))
                    wait(pe, s_used, NT * (G - 1) + 4)
                wait(pe, max_used, GH * G + h)
                for i in range(2):
                    last = pe.matmul(pm[0:LQ, i, 0:HALF], qbh[:, h, :], kh[kpar][:, c, i * HALF:(i + 1) * HALF],
                                     start=True, stop=True)
                last.then_inc(max_ready, 1)

            def broadcast_shift(b, kind, name, G):
                wait(pe, diag_ready, len(DIAGONALS) * (G + 1))
                t_use(b, kind, name)
                pe.matmul(pt[:, 0:NQ], onesr[:, :], diag[:, :, :].rearrange("p h q -> p (h q)"),
                          start=True, stop=True).then_inc(t_ready, 1)

            def scores(b, kind, g, par):
                G = NG * b + g
                wait(pe, qb_ready, G + 1)
                q_h = qbh[:, :, :].rearrange("p h q -> p (h q)")
                q_l = qbl[:, :, :].rearrange("p h q -> p (h q)")
                for t in range(NT):
                    if t in (0, 1):
                        wait(pe, s_used, NT * G + t - 1)
                    elif t in (2, 3):
                        wait(pe, max_used, GH * (G + 1))
                    else:
                        wait(pe, s_used, NT * G + t - 3)
                    if t == 1:
                        if g:
                            broadcast_shift(b, kind, f"bc{g - 1}", G)
                        else:
                            before = {"first": "pro", "mid": "first" if isinstance(b, int) and b == 1 else "mid"}
                            broadcast_shift(b - 1, before.get(kind, "mid"), "bc3", G)
                    k_h, k_l = kh[par][:, g, t * KT:(t + 1) * KT], kl[par][:, g, t * KT:(t + 1) * KT]
                    o = s_bank(t)
                    pe.matmul(o, k_h, q_h, start=True, stop=False)
                    pe.matmul(o, k_h, q_l, start=False, stop=False)
                    pe.matmul(o, k_l, q_h, start=False, stop=True).then_inc(s_ready, 1)

            def weigh_values(b, G, par, c, part):
                if part == 0:
                    if c == 0:
                        wait(pe, v_copy, 2 * HT * (b + 1))
                    wait(pe, norm_step, N_NORM * G)
                wait(pe, p_ready, NT * G + HT * (part + 1))
                for t in range(part * HT, (part + 1) * HT):
                    for h in range(GH):
                        pe.matmul(po[h * DK:(h + 1) * DK, 0:LQ],
                                  vv[par][:, t, c * P + h * DK:c * P + (h + 1) * DK],
                                  prob[0:KT, t, h * LQ:(h + 1) * LQ], start=(t == 0), stop=(t == NT - 1),
                                  tile_position=(0, h * DK))

            def sum_probs(G):
                wait(pe, sum_step, N_SUM * (G + 1))
                for h in range(GH):
                    last = pe.matmul(po[h * DK:(h + 1) * DK, P:P + LQ], ones[0:KT, 0:DK],
                                     acc[:, 0, h * LQ:(h + 1) * LQ], start=True, stop=True,
                                     tile_position=(0, h * DK))
                last.then_inc(pv_done, 1)

            def out_product(b, kind, prev):
                wait(pe, norm_step, N_NORM * NG * (prev + 1))
                t_use(b, kind, "op")
                for c in range(DC):
                    last = pe.matmul(pt[0:LQ, 0:D], ot[:, c, :], wo[:, c, :], start=(c == 0), stop=(c == DC - 1))
                last.then_inc(t_ready, 1)

            def gate_transposes(b, kind, prev):
                wait(pe, ln2_step, N_LN2 * (prev + 1))
                t_use(b, kind, "rT")
                for c in range(DC):
                    last = pe.transpose(pt[:, c * LQ:(c + 1) * LQ], xn2[:, c * P:(c + 1) * P], ident[0:LQ, 0:LQ])
                last.then_inc(t_ready, 1)

            def gate_product(b, kind, prev):
                wait(pe, x2t_ready, prev + 1)
                t_use(b, kind, "rm")
                for c in range(DC):
                    last = pe.matmul(pt[0:LQ, 0:E], x2t[:, c, :], wr[:, c, :], start=(c == 0), stop=(c == DC - 1))
                last.then_inc(t_ready, 1)

            def positions(b, kind, prev):
                wait(pe, gate_step, N_GATE * prev + 3)
                t_use(b, kind, "pos")
                pe.matmul(pt[0:LQ, 0:E], tri[:, :], sel[:, :], start=True, stop=True)
                pe.matmul(pt[0:LQ, E:2 * E], ones[0:LQ, 0:LQ], sel[:, :], start=True, stop=True).then_inc(t_ready, 1)

            def iteration(b, kind, par):
                more, prev = kind != "last", kind != "first"
                for g in range(NG):
                    G = NG * b + g
                    scores(b, kind, g, par)
                    unit = pe_units(pe, b + 1, g // 2) if more else None
                    ks = list(range(UK)) if g % 2 == 0 else list(range(UK, UH))
                    for i in range(GH):
                        if more and i < len(ks):
                            unit(ks[i])
                        if i == GH - 1:
                            weigh_values(b, G, par, g, 0)
                        if g < NG - 1:
                            max_head(G + 1, par, g + 1, i)
                        elif more:
                            max_head(G + 1, 1 - par, 0, i, nxt=b + 1)
                        if g == 0 and i == 0 and prev:
                            out_product(b, kind, b - 1)
                        if g == 0 and i == 1 and more:
                            x_transposes(b, kind, b + 1)
                        if g == 1 and i == 0 and more:
                            q_product(b, kind, b + 1)
                        if g == 1 and i == 1 and prev:
                            gate_transposes(b, kind, b - 1)
                        if g == 2 and i == 0 and prev:
                            gate_product(b, kind, b - 1)
                        if g == 2 and i == 1 and more:
                            q_transposes(b, kind, b + 1)
                        if g == 3 and i == 0 and prev:
                            positions(b, kind, b - 1)
                    weigh_values(b, G, par, g, 1)
                    sum_probs(G)

            pe.wait_ge(w_lo, 1)
            pe.wait_ge(const_in, 16 * NCONST)
            pe.wait_ge(setup_dve, 1)
            first = pe_units(pe, 0, 0)
            for k in range(UK):
                first(k)
            x_transposes(0, "pro", 0)
            pe.wait_ge(w_lo, 2)
            for k in range(UK, UH):
                first(k)
            q_product(0, "pro", 0)
            second = pe_units(pe, 0, 1)
            for k in range(UK):
                second(k)
            q_transposes(0, "pro", 0)
            for h in range(GH):
                if h < HT:
                    second(UK + h)
                max_head(0, 0, 0, h, nxt=0)
            iteration(0, "first", 0)
            pe.wait_ge(w_in[3], 16)
            iteration(1, "mid", 1)
            with pe.Fori(1, B // 2 - 1) as i:
                iteration(2 * i, "mid", 0)
                iteration(2 * i + 1, "mid", 1)
            iteration(B - 2, "mid", 0)
            iteration(B - 1, "last", 1)
            out_product(B, "epi", B - 1)
            gate_transposes(B, "epi", B - 1)
            gate_product(B, "epi", B - 1)
            positions(B, "epi", B - 1)
            pe.wait_ge(units_step, 13)
            for k in range(3):
                last = pe.matmul(pt[0:1, 2 * E + k * NU:2 * E + (k + 1) * NU], unit_v[:, k:k + 1], ident[0:NU, 0:NU],
                                 start=True, stop=True)
            last.then_inc(t_ready, 1)

        @block.scalar
        def _(act):
            raww = prob[:, :, :].rearrange("p t n -> p (t n)")[:, 0:DC * D]

            def split_weight(n, hi):
                act.wait_ge(w_in[n], 16)
                act.activation(hi[:, :, :].rearrange("p c n -> p (c n)"), raww, ACT.Copy).then_inc(w_hi, 1)

            def split_ctx(b, half):
                hh = 2 * b + half
                act.wait_ge(c_in, 16 * (hh + 1))
                wait(act, proj_ready, UH * (hh - 1))
                act.activation(ch[half][:, :, :], craw[:, :, :], ACT.Copy).then_inc(c_hi, 1)

            def unit(b, half, k, par):
                hh = 2 * b + half
                act.wait_ge(proj_ready, UH * hh + k + 1)
                src = pa[(UH * half + k) % 2]
                if k < UK:
                    wait(act, s_ready, NT * NG * (b - 1))
                    act.activation(kh[par][:, k, half * HALF:(half + 1) * HALF], src[:, 0:HALF], ACT.Identity,
                                   bias=bk[:, k:k + 1]).then_inc(k_hi, 1)
                else:
                    wait(act, pv_done, NG * (b - 1))
                    act.activation(vv[par][:, half * HT + k - UK, :], src[0:KT, 0:D], ACT.Copy).then_inc(v_copy, 1)

            def x_hi(b, kind, nxt):
                act.wait_ge(t_ready, t_index(b, kind, "xT") + 1)
                act.activation(xth[:, :, :].rearrange("p c q -> p (c q)"), pt[:, 0:DC * LQ], ACT.Copy).then_inc(xt_hi, 1)

            def q_copy(b, kind):
                act.wait_ge(t_ready, t_index(b, kind, "Q") + 1)
                act.activation(qs[:, :], pt[0:LQ, 0:D], ACT.Copy).then_inc(qs_ready, 1)

            def gate_copy(b, kind, prev):
                act.wait_ge(t_ready, t_index(b, kind, "rT") + 1)
                act.activation(x2t[:, :, :].rearrange("p c q -> p (c q)"), pt[:, 0:DC * LQ], ACT.Copy).then_inc(x2t_ready, 1)

            def shift_copy(b, kind, name, G):
                act.wait_ge(t_ready, t_index(b, kind, name) + 1)
                wait(act, s_used, NT * G)
                act.activation(shift[:, :], pt[0:KT, 0:NQ], ACT.Copy).then_inc(shift_ready, 1)

            def exps(b, G):
                for t in range(NT):
                    act.wait_ge(s_used, NT * G + t + 1)
                    alone(act, A["passed"])
                    act.activation(prob[0:KT, t, :], prob[0:KT, t, :], ACT.Exp,
                                   bias=mkey[:, bass.ds(NT * b + t, 1)], scale=SCALE).then_inc(p_ready, 1)

            def gate_exps(prev):
                act.wait_ge(gate_step, N_GATE * prev + 3)
                act.activation(ex[:, :], lg[:, :], ACT.Exp, bias=nm1[:, :]).then_inc(gate_exp, 1)

            def iteration(b, kind, par):
                more, prev = kind != "last", kind != "first"
                for g in range(NG):
                    G = NG * b + g
                    exps(b, G)
                    ks = list(range(UK)) if g % 2 == 0 else list(range(UK, UH))
                    for i in range(GH):
                        if more and i < len(ks):
                            unit(b + 1, g // 2, ks[i], 1 - par)
                        if i == 1 and more and g == 0:
                            x_hi(b, kind, b + 1)
                        if i == 0 and more and g == 1:
                            q_copy(b, kind)
                        if i == 3 and prev and g == 2:
                            gate_exps(b - 1)
                        if i == 1 and prev and g == 1:
                            gate_copy(b, kind, b - 1)
                    if more and g == 0:
                        split_ctx(b + 1, 1)
                    if more and g == 2 and not (isinstance(b, int) and b == B - 2):
                        split_ctx(b + 2, 0)
                    if g < NG - 1 or more:
                        shift_copy(b, kind, f"bc{g}", G + 1)

            split_weight(0, wkh)
            split_ctx(0, 0)
            act.wait_ge(const_in, 16 * NCONST)
            act.activation(tg[:, :], gx[:, :], ACT.Tanh).then_inc(setup_act, 1)
            split_weight(1, wvh)
            for k in range(UK):
                unit(0, 0, k, 0)
            x_hi(0, "pro", 0)
            split_weight(2, wqh)
            split_ctx(0, 1)
            for k in range(UK, UH):
                unit(0, 0, k, 0)
            q_copy(0, "pro")
            split_ctx(1, 0)
            for k in range(UH):
                unit(0, 1, k, 0)
            shift_copy(0, "pro", "bc3", 0)
            iteration(0, "first", 0)
            iteration(1, "mid", 1)
            with act.Fori(1, B // 2 - 1) as i:
                iteration(2 * i, "mid", 0)
                iteration(2 * i + 1, "mid", 1)
            iteration(B - 2, "mid", 0)
            iteration(B - 1, "last", 1)
            gate_copy(B, "epi", B - 1)
            gate_exps(B - 1)

        @block.vector
        def _(dve):
            raww = prob[:, :, :].rearrange("p t n -> p (t n)")[:, 0:DC * D]

            def split_weight(n, hi, lo):
                dve.wait_ge(w_hi, n + 1)
                dve.tensor_tensor(lo[:, :, :].rearrange("p c n -> p (c n)"), raww,
                                  f32(hi[:, :, :]).rearrange("p c n -> p (c n)"), ALU.subtract).then_inc(w_lo, 1)

            def shifted(G):
                dve.wait_ge(shift_ready, G + 1)
                wait(dve, pv_done, G)
                for t in range(NT):
                    dve.wait_ge(s_ready, NT * G + t + 1)
                    dve.tensor_tensor(prob[0:KT, t, :], s_bank(t), shift[:, :],
                                      ALU.subtract).then_inc(s_used, 1)

            def key_lo(b, half, k, par):
                hh = 2 * b + half
                dve.wait_ge(k_hi, UK * hh + k + 1)
                at = slice(half * HALF, (half + 1) * HALF)
                dve.scalar_tensor_tensor(out=kl[par][:, k, at], in0=pa[(UH * half + k) % 2][:, 0:HALF],
                                         scalar=bk[:, k:k + 1], in1=f32(kh[par][:, k, at]),
                                         op0=ALU.add, op1=ALU.subtract).then_inc(k_lo, 1)

            def head_max(G, h, mpar):
                dve.wait_ge(max_ready, GH * G + h + 1)
                alone(dve, A["passed"])
                dve.tensor_tensor_reduce(junk[:, :, :], pm[0:LQ, :, 0:HALF], mrow[mpar][:, :, :], 1.0, MASKED,
                                         ALU.add, ALU.max, mx[:, h:h + 1]).then_inc(max_used, 1)

            def diagonals(G, heads):
                n = heads.stop - heads.start
                dve.wait_ge(max_used, GH * G + heads.stop)
                dve.tensor_tensor(diag[:, heads, :], ident[0:LQ, 0:LQ].unsqueeze(1).broadcast_to([LQ, n, LQ]),
                                  mx[:, heads].unsqueeze(2).broadcast_to([LQ, n, LQ]), ALU.mult).then_inc(diag_ready, 1)

            def normalise(G, c):
                dve.wait_ge(pv_done, G + 1)
                s = Chain(dve, norm_step, N_NORM * G)
                s.link(dve.reciprocal(rden[:, :], po[:, P:P + LQ]))
                s.link(dve.tensor_tensor(rden[:, :], po[:, 0:LQ], rden[:, :], ALU.mult))
                s.link(dve.tensor_scalar(ot[:, c, :], rden[:, :], bv[:, c:c + 1], None, ALU.add))

            def ln1_stats(b):
                dve.wait_ge(x_in, 16 * (b + 1))
                s = Chain(dve, ln1_step, N_LN1 * b, A["passed"])
                s.link(dve.bn_stats(st[:, :], xn[:, :]))
                s.link(dve.bn_aggr(mv[:, :], st[:, :]))

            def ln1_apply(b):
                dve.wait_ge(ln1_pow, 2 * (b + 1))
                dve.tensor_scalar(xn[:, :], xn[:, :], mv[:, 0:1], rstd[:, :], ALU.subtract, ALU.mult).then_inc(ln1_step, 1)

            def x_lo(b, kind, nxt):
                dve.wait_ge(xt_hi, nxt + 1)
                dve.tensor_tensor(xtl[:, :, :].rearrange("p c q -> p (c q)"), pt[:, 0:DC * LQ],
                                  f32(xth[:, :, :]).rearrange("p c q -> p (c q)"), ALU.subtract).then_inc(xt_lo, 1)

            def q_split(b, kind, nxt):
                dve.wait_ge(t_ready, t_index(b, kind, "QT") + 1)
                wait(dve, qb_ready, NG * nxt)
                s = Chain(dve, qt_step, N_QT * nxt)
                s.link(dve.tensor_tensor(qt[:, :, :], pt[:, 0:NQ].rearrange("p (c q) -> p c q", c=NG),
                                         bq[:, :].unsqueeze(2).broadcast_to([P, NG, LQ]), ALU.add)
                       )
                s.link(dve.tensor_copy(qth[:, :, :], qt[:, :, :]))
                s.link(dve.tensor_tensor(qtl[:, :, :], qt[:, :, :], f32(qth[:, :, :]), ALU.subtract))

            def mask_row(b, par):
                dve.wait_ge(m_in, 16 * (b + 1))
                dve.tensor_scalar(mrow[par][:, :, :].rearrange("p a n -> p (a n)"), mrow8[:, :], MASKED, None,
                                  ALU.mult).then_inc(m_used, 1)
                dve.wait_ge(m_used, b + 1)

            def residual(b, kind, prev):
                dve.wait_ge(t_ready, t_index(b, kind, "op") + 1)
                dve.wait_ge(xres_ready, prev + 1)
                dve.scalar_tensor_tensor(out=x1[:, :], in0=pt[0:LQ, 0:D], scalar=tg[0:LQ, 0:1], in1=x1[:, :],
                                         op0=ALU.mult, op1=ALU.add).then_inc(x1_ready, 1)
                dve.wait_ge(x1_ready, prev + 1)
                s = Chain(dve, ln2_step, N_LN2 * prev, A["passed"])
                s.link(dve.bn_stats(st2[:, :], x1[:, :]))
                s.link(dve.bn_aggr(mv2[:, :], st2[:, :]))

            def ln2_apply(prev):
                dve.wait_ge(ln2_pow, 2 * (prev + 1))
                wait(dve, xn2_out, 16 * prev)
                wait(dve, row_out, 32 * prev)
                dve.tensor_scalar(xn2[:, :], x1[:, :], mv2[:, 0:1], rs2[:, :], ALU.subtract, ALU.mult).then_inc(ln2_step, 1)

            def gate(b, kind, prev):
                dve.wait_ge(t_ready, t_index(b, kind, "rm") + 1)
                s = Chain(dve, gate_step, N_GATE * prev, A["passed"])
                s.link(dve.tensor_tensor(lg[:, :], pt[0:LQ, 0:E], br[:, :], ALU.add))
                s.link(dve.max(m8[:, :], lg[:, :]))
                dve.tensor_scalar(nm1[:, :], m8[:, 0:1], -1.0, None, ALU.mult)
                s.link(dve.tensor_scalar(sel[:, :], lg[:, :], m8[:, 1:2], None, ALU.is_ge))

            def gate_weights(prev):
                dve.wait_ge(gate_exp, prev + 1)
                s = Chain(dve, gate_step, N_GATE * prev + 3)
                s.link(dve.tensor_tensor_reduce(we[:, :], ex[:, :], sel[:, :], 1.0, 0.0, ALU.mult, ALU.add, wsum[:, :]))
                s.link(dve.reciprocal(wsum[:, :], wsum[:, :]))
                s.link(dve.tensor_scalar(wgt[:, :], we[:, :], wsum[:, :], tg[0:LQ, 1:2], ALU.mult, ALU.mult))
                s.link(dve.tensor_tensor_scan(cum[:, :], sel[:, :], zero8[:, :], 0.0, ALU.add, ALU.add))

            def choices(b, kind, prev):
                dve.wait_ge(t_ready, t_index(b, kind, "pos") + 1)
                s = Chain(dve, pos_step, N_POS * prev)
                s.link(dve.tensor_tensor(slot[:, :], pt[0:LQ, 0:E], seen[:, :], ALU.add))
                s.link(dve.tensor_tensor(seen[:, :], pt[0:LQ, E:2 * E], seen[:, :], ALU.add))
                s.link(dve.tensor_tensor(slot[:, :], slot[:, :], rowbase[:, :], ALU.add))
                s.link(dve.tensor_tensor(sk[:, :, :], rankc[:, :, :], cum[:, :].unsqueeze(1).broadcast_to([LQ, E, E]),
                                         ALU.is_equal))
                s.link(dve.tensor_tensor(sk[:, :, :], sk[:, :, :], sel[:, :].unsqueeze(1).broadcast_to([LQ, E, E]),
                                         ALU.mult))
                return s

            def slots_of(s, prev):
                s.link(dve.tensor_tensor(skv[:, :, :], sk[:, :, :], slot[:, :].unsqueeze(1).broadcast_to([LQ, E, E]),
                                         ALU.mult))
                s.link(dve.tensor_reduce(idf[:, :], skv[:, :, :], AX.X, ALU.add))
                s.link(dve.tensor_scalar(gone[:, :], rankv[:, :], cum[:, E - 1:E], OOB, ALU.is_gt, ALU.mult))
                s.link(dve.tensor_tensor(idf[:, :], idf[:, :], gone[:, :], ALU.add))

            def keep_choices(prev):
                dve.wait_ge(pos_step, N_POS * (prev + 1))
                dve.tensor_tensor(skv[:, :, :], sk[:, :, :], wgt[:, :].unsqueeze(1).broadcast_to([LQ, E, E]),
                                  ALU.mult).then_inc(idx_ready, 1)
                dve.wait_ge(idx_ready, 4 * prev + 1)
                dve.tensor_reduce(A["w_all"][:, bass.ds(E * prev, E)], skv[:, :, :], AX.X, ALU.add).then_inc(idx_ready, 1)
                dve.tensor_copy(A["i_all"][:, bass.ds(E * prev, E)], idf[:, :]).then_inc(idx_ready, 1)
                wait(dve, row_out, 32 * prev)
                dve.tensor_copy(idx[:, :], idf[:, 0:2]).then_inc(idx_ready, 1)
                dve.wait_ge(idx_ready, 4 * prev + 4)

            def iteration(b, kind, par):
                more, prev = kind != "last", kind != "first"
                skip = not more or isinstance(b, int) and b == B - 2
                for g in range(NG):
                    G = NG * b + g
                    shifted(G)
                    if g or prev:
                        normalise(G - 1, (g - 1) % NG)
                    if g == 1 and prev:
                        ln2_apply(b - 1)
                    if g == 0 and more and prev:
                        ln1_apply(b + 1)
                    if g == 3 and not skip:
                        ln1_stats(b + 2)
                    if g == 3 and prev:
                        gate_weights(b - 1)
                    for i in range(GH):
                        if more and g % 2 == 0:
                            key_lo(b + 1, g // 2, i, 1 - par)
                        if g < NG - 1:
                            head_max(G + 1, i, par)
                        elif more:
                            head_max(G + 1, i, 1 - par)
                        if g == 0 and i == 0 and prev:
                            residual(b, kind, b - 1)
                        if g == 0 and i == 1 and more:
                            x_lo(b, kind, b + 1)
                        if g == 1 and i == 1 and more:
                            mask_row(b + 1, 1 - par)
                        if g == 2 and i == 0 and prev:
                            gate(b, kind, b - 1)
                        if g == 2 and i == 1 and more:
                            q_split(b, kind, b + 1)
                        if g == 3 and i == 0 and prev:
                            chosen = choices(b, kind, b - 1)
                        if g == 3 and i == 1 and prev:
                            slots_of(chosen, b - 1)
                        if i >= GH - 2 and (g < NG - 1 or more):
                            diagonals(G + 1, DIAGONALS[i - GH + 2])
                    if g == 3 and prev:
                        keep_choices(b - 1)

            split_weight(0, wkh, wkl)
            dve.memset(ones[:, :], 1.0).then_inc(setup_dve, 1)
            dve.memset(zero8[:, :], 0.0)
            dve.memset(seen[:, :], 0.0)
            dve.memset(A["table"][:, :], 0)
            dve.wait_ge(setup_dve, 1)
            dve.tensor_copy(onesr[:, :], ones[0:LQ, :]).then_inc(setup_dve, 1)
            split_weight(1, wvh, wvl)
            dve.wait_ge(const_in, 16 * NCONST)
            dve.tensor_scalar(mkey[:, :], mkey8[:, :], MASKED, None, ALU.mult).then_inc(setup_dve, 1)
            dve.wait_ge(setup_act, 1)
            dve.tensor_scalar(gbo[:, :], gbo[:, :], tg[0:LQ, 0:1], None, ALU.mult).then_inc(setup_dve, 1)
            ln1_stats(0)
            ln1_apply(0)
            mask_row(0, 0)
            for k in range(UK):
                key_lo(0, 0, k, 0)
            x_lo(0, "pro", 0)
            split_weight(2, wqh, wql)
            for k in range(UK):
                key_lo(0, 1, k, 0)
            q_split(0, "pro", 0)
            ln1_stats(1)
            ln1_apply(1)
            for h in range(GH):
                head_max(0, h, 0)
            for heads in DIAGONALS:
                diagonals(0, heads)
            dve.wait_ge(setup_dve, 4)
            iteration(0, "first", 0)
            iteration(1, "mid", 1)
            with dve.Fori(1, B // 2 - 1) as i:
                iteration(2 * i, "mid", 0)
                iteration(2 * i + 1, "mid", 1)
            iteration(B - 2, "mid", 0)
            iteration(B - 1, "last", 1)
            normalise(NG * B - 1, NG - 1)
            residual(B, "epi", B - 1)
            ln2_apply(B - 1)
            gate(B, "epi", B - 1)
            gate_weights(B - 1)
            slots_of(choices(B, "epi", B - 1), B - 1)
            keep_choices(B - 1)
            dve.wait_ge(units_in, 16)
            s = Chain(dve, units_step, 0)
            flat = craw[0:NU, :, :].rearrange("p c n -> p (c n)")
            work = prob[0:NU, 0:4, :].rearrange("p t n -> p (t n)")
            above, steps = work[:, 0:NU * CHUNKS], work[:, NU * CHUNKS:2 * NU * CHUNKS]
            size, row, active, rank, zeros, picked = (prob[0:NU, 4, k * NU:(k + 1) * NU] for k in range(6))

            def const(at, n=NU):
                return flat[:, at:at + n]

            s.link(dve.memset(zeros, 0.0))
            s.link(dve.tensor_tensor(above.rearrange("p (e n) -> p e n", e=E),
                                     seen[0:NU, :].unsqueeze(2).broadcast_to([NU, E, ROUNDS * CHUNKS]),
                                     const(C_THR, NU * CHUNKS).rearrange("p (e n) -> p e n", e=E), ALU.is_gt))
            s.link(dve.tensor_tensor(steps, above, const(C_DSIZE, NU * CHUNKS), ALU.mult))
            s.link(dve.tensor_reduce(size, steps.rearrange("p (u n) -> p u n", u=NU), AX.X, ALU.add))
            s.link(dve.tensor_tensor(steps, above, const(C_DROW, NU * CHUNKS), ALU.mult))
            s.link(dve.tensor_reduce(row, steps.rearrange("p (u n) -> p u n", u=NU), AX.X, ALU.add))
            s.link(dve.tensor_tensor(row, row, const(C_BASE), ALU.add))
            s.link(dve.tensor_scalar(active, size, 0.0, None, ALU.is_gt))
            s.link(dve.tensor_tensor_scan(rank, active, zeros, 0.0, ALU.add, ALU.add))
            s.link(dve.scalar_tensor_tensor(out=picked, in0=rank, scalar=flat[:, C_RANK:C_RANK + 1],
                                            in1=active, op0=ALU.is_equal, op1=ALU.mult))
            dve.tensor_copy(A["table"][:, T_TOTAL:T_TOTAL + 1], rank[0:1, NU - 1:NU])
            for k, values in enumerate((size, row, const(C_EXP))):
                s.link(dve.tensor_tensor_reduce(zeros, picked, values, 1.0, 0.0, ALU.mult, ALU.add,
                                                unit_v[:, k:k + 1]))
            dve.wait_ge(t_ready, t_index(B, "epi", "pos") + 2)
            table = A["table"]
            dve.tensor_copy(table[:, 0:3 * (NU + 1)].rearrange("p (k n) -> p k n", k=3)[:, :, 0:NU],
                            pt[0:1, 2 * E:2 * E + 3 * NU].rearrange("p (k n) -> p k n", k=3))
            s.link(dve.tensor_reduce(choices_all[:, :], seen[0:1, :], AX.X, ALU.add))
            dve.tensor_scalar(table[:, T_TIE:T_TIE + 1], choices_all[:, :], float(2 * B * LQ), None, ALU.is_gt)

        @block.gpsimd
        def _(pool):
            def lay_queries(G, c, nxt=None):
                if nxt is not None:
                    wait(pool, qt_step, N_QT * (nxt + 1))
                wait(pool, s_ready, NT * G)
                for dst, src, done in ((qbh, qth, qb_hi), (qbl, qtl, qb_ready)):
                    pool.tensor_tensor(dst[:, :, :], f32(src[:, c, :]).unsqueeze(1).broadcast_to([P, GH, LQ]),
                                       blockm[:, :, :], ALU.mult).then_inc(done, 1)

            def sum_tiles(G):
                pool.wait_ge(p_ready, NT * (G + 1))
                wait(pool, pv_done, G)
                s = Chain(pool, sum_step, N_SUM * G)
                s.link(pool.tensor_tensor(acc[:, :, :], prob[0:KT, 0:2, :], prob[0:KT, 2:4, :], ALU.add))
                s.link(pool.tensor_tensor(acc[:, :, :], acc[:, :, :], prob[0:KT, 4:6, :], ALU.add))
                s.then(pool.tensor_tensor(acc[:, 0, :], acc[:, 0, :], acc[:, 1, :], ALU.add))

            def ctx_lo(b, half):
                pool.wait_ge(c_hi, 2 * b + half + 1)
                pool.tensor_tensor(cl[half][:, :, :], craw[:, :, :], f32(ch[half][:, :, :]), ALU.subtract).then_inc(c_lo, 1)

            def power(n, ready, want, dst, src, done):
                pool.wait_ge(ready, want)
                alone(pool, A["passed"])
                pool.tensor_scalar(dst[:, :], src[:, 1:2], EPS, None, ALU.add).then_inc(done, 1)
                pool.wait_ge(done, 2 * n + 1)
                pool.tensor_tensor(dst[:, :], dst[:, :], mhalf[:, :], ALU.pow).then_inc(done, 1)

            def residual_bias(b):
                pool.wait_ge(xres_in, 16 * (b + 1))
                pool.tensor_tensor(x1[:, :], x1[:, :], gbo[:, :], ALU.add).then_inc(xres_ready, 1)

            def store_rows(b):
                pool.wait_ge(x1_ready, b + 1)
                alone(pool, A["passed"])
                pool.dma_start(A["x1_d"][bass.ds(b, 1)].rearrange("b l d -> (b l) d"), x1[:, :]).then_inc(x1_out, 16)
                pool.wait_ge(ln2_step, N_LN2 * (b + 1))
                alone(pool, A["passed"])
                pool.dma_start(A["xn2_d"][bass.ds(b, 1)].rearrange("b l d -> (b l) d"), xn2[:, :]).then_inc(xn2_out, 16)

            def scatter(b):
                pool.wait_ge(idx_ready, 4 * (b + 1))
                pool.wait_ge(zero_out, 16 * (b + 1))
                alone(pool, A["passed"])
                for k in range(2):
                    pool.indirect_dma_start(A["slots"], bass.IndirectOffsetOnAxis(ap=idx[:, k:k + 1], axis=0), xn2[:, :], None,
                                            bounds_check=E * ROWS - 1, oob_is_err=False).then_inc(row_out, 16)

            def iteration(b, kind, par):
                more, prev = kind != "last", kind != "first"
                for g in range(NG):
                    G = NG * b + g
                    if g < NG - 1:
                        lay_queries(G + 1, g + 1)
                    elif more:
                        lay_queries(G + 1, 0, nxt=b + 1)
                    sum_tiles(G)
                    if g == 0 and prev:
                        power(b - 1, ln2_step, N_LN2 * (b - 1) + 2, rs2, mv2, ln2_pow)
                    if g == 3 and more and not (isinstance(b, int) and b == B - 2):
                        power(b + 2, ln1_step, N_LN1 * (b + 2) + 2, rstd, mv, ln1_pow)
                    if g == 1 and prev:
                        store_rows(b - 1)
                    if g == 3:
                        residual_bias(b)
                    if more and g == 0:
                        ctx_lo(b + 1, 1)
                    if more and g == 2 and not (isinstance(b, int) and b == B - 2):
                        ctx_lo(b + 2, 0)
                    if g == 3 and prev:
                        scatter(b - 1)

            pool.memset(mhalf[:, :], -0.5).then_inc(setup_pool, 1)
            pool.memset(A["zero"][:, :], 0.0).then_inc(setup_pool, 1)
            pool.wait_ge(setup_pool, 2)
            ctx_lo(0, 0)
            power(0, ln1_step, 2, rstd, mv, ln1_pow)
            ctx_lo(0, 1)
            pool.wait_ge(const_in, 16 * NCONST)
            ctx_lo(1, 0)
            power(1, ln1_step, N_LN1 + 2, rstd, mv, ln1_pow)
            pool.wait_ge(setup_dve, 4)
            lay_queries(0, 0, nxt=0)
            iteration(0, "first", 0)
            iteration(1, "mid", 1)
            with pool.Fori(1, B // 2 - 1) as i:
                iteration(2 * i, "mid", 0)
                iteration(2 * i + 1, "mid", 1)
            iteration(B - 2, "mid", 0)
            iteration(B - 1, "last", 1)
            power(B - 1, ln2_step, N_LN2 * (B - 1) + 2, rs2, mv2, ln2_pow)
            store_rows(B - 1)
            scatter(B - 1)
            pool.wait_ge(x1_out, 16 * B)
            pool.wait_ge(xn2_out, 16 * B)
            pool.wait_ge(row_out, 32 * B)


def expert_phase(nc, A):
    with ExitStack() as ctx:
        def sb(name, shape, dt=F32):
            return ctx.enter_context(nc.sbuf_tensor(name, shape, dt))

        def sem(name):
            return ctx.enter_context(nc.semaphore(name))

        wraw_all = sb("wraw", [P, RAW, 2, 2, D])
        wraw = [wraw_all[:, i] for i in range(RAW)]
        wh = [sb(f"wh{i}", [P, 2, D], F32R) for i in range(RING)]
        wl = [sb(f"wl{i}", [P, 2, D], F32R) for i in range(RING)]
        xr = sb("xr", [P, NS, D])
        xh, xl = sb("xh", [P, DC, SLOTS], F32R), sb("xl", [P, DC, SLOTS], F32R)
        hid = [sb(f"hid{i}", [P, SLOTS]) for i in range(2)]
        hh = [sb(f"hh{i}", [P, SLOTS], F32R) for i in range(HRING)]
        hl = [sb(f"hl{i}", [P, SLOTS], F32R) for i in range(HRING)]
        y = sb("y", [P, NS, D])
        y0 = sb("y0", [LQ, B, D])
        y1 = [(xr, y)[k // NS][0:LQ, k % NS, :] for k in range(PLACES)]
        ident = sb("identx", [P, P])
        b1 = sb("b1", [P, E * NJ])
        b2 = sb("b2", [P, E * D])
        tix, tiw = sb("tix", [LQ, E], I32), sb("tiw", [LQ, E])

        pt = [ctx.enter_context(nc.psum_tensor(f"ptx{i}", [P, 512], F32)) for i in range(2)]
        ph = [ctx.enter_context(nc.psum_tensor(f"ph{i}", [P, 512], F32)) for i in range(2)]
        py = ctx.enter_context(nc.psum_tensor("py", [P, NS, 512], F32))

        raw_in = [sem(f"raw_in{i}") for i in range(RAW)]
        xr_in, y_out = sem("xr_in"), sem("y_out")
        ident_in, b1_in, b2_in = sem("ident_in"), sem("b1_in"), sem("b2_in")
        pair_in = [sem(f"pair_in{i}") for i in range(PLACES)]
        res_in, first_in = sem("res_in"), sem("first_in")
        o_out = [sem(f"o_out{i}") for i in range(PLACES)]
        dispatched, tie_in, tie_step = sem("dispatched"), sem("tie_in"), sem("tie_step")
        e_hi, e_lo = sem("e_hi"), sem("e_lo")
        xt_ready, xt_copied, xt_split = sem("xt_ready"), sem("xt_copied"), sem("xt_split")
        h_ready, h_gelu, h_hi, h_lo, w2_done = sem("h_ready"), sem("h_gelu"), sem("h_hi"), sem("h_lo"), sem("w2_done")
        y_copied, pair_step, pair_done = sem("y_copied"), sem("pair_step"), sem("pair_done")
        C_LO, C_W2, C_XS, C_GELU, C_HLO, C_YC, C_YO = 2 * RAW, RING, 2, 2, 2, 1, 16
        table, w_all, i_all = A["table"], A["w_all"], A["i_all"]
        PAIRS = NJ // 2
        own = wraw_all[0:LQ].rearrange("p r m j d -> p (r m j) d")
        quarter = E * D // 4
        PART = 4
        block = ctx.enter_context(nc.Block())

        def entry(eng, at, n, most):
            return eng.value_load(table[0:1, bass.ds(n + at, 1)], min_val=0, max_val=most)

        def over_units(eng, unit):
            with eng.Fori(0, NU // PART ** 2) as i:
                with eng.If(entry(eng, T_SIZE, i * PART ** 2, NS) > 0):
                    with eng.Fori(0, PART) as j:
                        with eng.If(entry(eng, T_SIZE, i * PART ** 2 + j * PART, NS) > 0):
                            with eng.Fori(0, PART) as k:
                                n = i * PART ** 2 + j * PART + k
                                size = entry(eng, T_SIZE, n, NS)
                                with eng.If(size > 0):
                                    unit(n, size)

        def by_size(eng, n, size, body):
            with eng.If(size < 3):
                body(n, 2)
            with eng.If(size > 2):
                with eng.If(size < 4):
                    body(n, 3)
            with eng.If(size > 3):
                body(n, 4)

        def following(eng, n):
            return entry(eng, T_SIZE, n + 1, NS)

        @block.sync
        def _(sp):
            def load_rows(row):
                sp.dma_start(xr[:, :, :], A["slots"][bass.ds(row, SLOTS), :].rearrange("(s p) d -> p s d", p=P)).then_inc(xr_in, 16)

            def load_weights(n, e, q):
                wait(sp, e_lo, C_LO + NJ * n + 2 * (q - RAW) + 2)
                if not isinstance(n, int):
                    alone(sp, A["passed"])
                for m, w in enumerate(("W1", "W2")):
                    sp.dma_start(wraw[q % RAW][:, m, :, :], A[w][bass.ds(e, 1), :, 2 * q:2 * q + 2, :]
                                 .rearrange("e p j n -> (e p) j n")).then_inc(raw_in[q % RAW], 16)

            sp.wait_ge(e_lo, C_LO)
            alone(sp, A["passed"])
            sp.wait_ge(dispatched, 1)
            alone(sp, A["passed"])
            load_rows(entry(sp, T_ROW, 0, E * ROWS - SLOTS))
            load_weights(0, entry(sp, T_EXPERT, 0, E - 1), 0)

            def unit(n, size):
                e = entry(sp, T_EXPERT, n, E - 1)
                more = following(sp, n)
                for q in range(1, PAIRS):
                    load_weights(n, e, q)
                with sp.If(more > 0):
                    sp.wait_ge(xt_ready, DC * (n + 1))
                    alone(sp, A["passed"])
                    load_rows(entry(sp, T_ROW, n + 1, E * ROWS - SLOTS))
                    load_weights(n + 1, entry(sp, T_EXPERT, n + 1, E - 1), 0)

            over_units(sp, unit)
            sp.wait_ge(e_lo, C_LO + NJ * sp.value_load(table[0:1, T_TOTAL:T_TOTAL + 1], min_val=1, max_val=NU))
            alone(sp, A["passed"])
            for i in range(RAW):
                m = B // RAW
                sp.dma_start(own[:, i * m:(i + 1) * m, :], A["x1_d"][i * m:(i + 1) * m].rearrange("b l d -> l b d")).then_inc(res_in, 16)

        @block.tensor
        def _(pe):
            pe.sem_inc(w2_done, C_W2)
            pe.wait_ge(ident_in, 16)

            def transposes(n, chunks):
                pe.wait_ge(xr_in, 16 * n + 16)
                for c in chunks:
                    pe.wait_ge(xt_split, C_XS + DC * n + c - 1)
                    for s in range(NS):
                        last = pe.transpose(pt[c % 2][:, s * P:(s + 1) * P], xr[:, s, c * P:(c + 1) * P], ident[:, :])
                    last.then_inc(xt_ready, 1)

            def body(n, size):
                cols = size * P
                pe.wait_ge(xt_split, C_XS + DC * n + DC)

                def first(j):
                    pe.wait_ge(e_lo, C_LO + NJ * n + j + 1)
                    pe.wait_ge(h_gelu, C_GELU + NJ * n + j - 1)
                    k = 0
                    for c in range(DC):
                        w_h, w_l = wh[j % RING][:, 0, c * P:(c + 1) * P], wl[j % RING][:, 0, c * P:(c + 1) * P]
                        for w, x in ((w_h, xh), (w_h, xl), (w_l, xh)):
                            last = pe.matmul(ph[j % 2][:, 0:cols], w, x[:, c, 0:cols], start=(k == 0), stop=(k == 3 * DC - 1))
                            k += 1
                    last.then_inc(h_ready, 1)

                def second(j):
                    pe.wait_ge(h_lo, C_HLO + NJ * n + j + 1)
                    if j == 0:
                        pe.wait_ge(y_copied, C_YC + n)
                    a, b = j == 0, j == NJ - 1
                    for s in range(size):
                        h_h, h_l = hh[j % HRING][:, s * P:(s + 1) * P], hl[j % HRING][:, s * P:(s + 1) * P]
                        pe.matmul(py[:, s, :], h_h, wh[j % RING][:, 1, :], start=a, stop=False)
                        pe.matmul(py[:, s, :], h_h, wl[j % RING][:, 1, :], start=False, stop=False)
                        last = pe.matmul(py[:, s, :], h_l, wh[j % RING][:, 1, :], start=False, stop=b)
                    last.then_inc(w2_done, 1)

                for j in range(NJ):
                    first(j)
                    if j == 2:
                        more = following(pe, n)
                    if j >= 2:
                        second(j - 2)
                with pe.If(more > 0):
                    transposes(n + 1, (0, 1))
                second(NJ - 2)
                with pe.If(more > 0):
                    transposes(n + 1, (2, 3))
                second(NJ - 1)

            transposes(0, range(DC))
            over_units(pe, lambda n, size: by_size(pe, n, size, body))

        @block.scalar
        def _(act):
            act.sem_inc(h_gelu, C_GELU)
            act.dma_start(ident[:, :], A["ident"]).then_inc(ident_in, 16)
            act.dma_start(b1[:, :].rearrange("p (e j) -> p e j", e=E), A["b1"].rearrange("e p j -> p e j")).then_inc(b1_in, 16)
            act.wait_ge(b1_in, 16)

            def high(n, j):
                q = j // 2
                act.wait_ge(raw_in[q % RAW], 32 * (PAIRS // RAW * n + q // RAW) + 32)
                act.wait_ge(w2_done, C_W2 + NJ * n + j - RING + 1)
                act.activation(wh[j % RING][:, :, :], wraw[q % RAW][:, :, j % 2, :], ACT.Copy).then_inc(e_hi, 1)

            def start(n):
                for c in range(DC):
                    act.wait_ge(xt_ready, DC * n + c + 1)
                    act.activation(xh[:, c, :], pt[c % 2][:, :], ACT.Copy).then_inc(xt_copied, 1)

            def body(n, size):
                cols = size * P
                e = entry(act, T_EXPERT, n, E - 1)
                more = following(act, n)
                for j in range(NJ):
                    act.wait_ge(h_ready, NJ * n + j + 1)
                    act.wait_ge(h_lo, C_HLO + NJ * n + j - 1)
                    alone(act, A["passed"])
                    act.activation(hid[j % 2][:, 0:cols], ph[j % 2][:, 0:cols], ACT.Gelu,
                                   bias=b1[:, bass.ds(e * NJ + j, 1)]).then_inc(h_gelu, 1)
                    if j + AHEAD < NJ:
                        high(n, j + AHEAD)
                    elif j % 2 == 0:
                        with act.If(more > 0):
                            high(n + 1, j + AHEAD - NJ)
                            high(n + 1, j + AHEAD - NJ + 1)
                with act.If(more > 0):
                    start(n + 1)

            high(0, 0)
            start(0)
            for j in range(1, AHEAD):
                high(0, j)
            act.dma_start(b2[:, 0:quarter], A["b2"][0:quarter].partition_broadcast(P)).then_inc(b2_in, 16)
            act.dma_start(b2[:, quarter:2 * quarter], A["b2"][quarter:2 * quarter].partition_broadcast(P)).then_inc(b2_in, 16)
            over_units(act, lambda n, size: by_size(act, n, size, body))
            with act.Fori(0, B // PLACES) as i:
                for k in range(PLACES):
                    act.wait_ge(pair_done, PLACES * i + k + 1)
                    act.dma_start(A["out"][bass.ds(PLACES * i + k, 1)].rearrange("b l d -> (b l) d"), y1[k]).then_inc(o_out[k], 16)
            for k in range(PLACES):
                act.wait_ge(o_out[k], 16 * (B // PLACES))

        @block.vector
        def _(dve):
            dve.sem_inc(xt_split, C_XS)
            dve.sem_inc(h_lo, C_HLO)
            dve.sem_inc(y_copied, C_YC)

            def start(n):
                for c in range(DC):
                    dve.wait_ge(xt_copied, DC * n + c + 1)
                    dve.tensor_tensor(xl[:, c, :], pt[c % 2][:, :], f32(xh[:, c, :]), ALU.subtract).then_inc(xt_split, 1)

            def body(n, size):
                cols = size * P
                e = entry(dve, T_EXPERT, n, E - 1)
                more = following(dve, n)
                for j in range(NJ):
                    dve.wait_ge(h_gelu, C_GELU + NJ * n + j + 1)
                    dve.wait_ge(w2_done, C_W2 + NJ * n + j - HRING + 1)
                    dve.tensor_copy(hh[j % HRING][:, 0:cols], hid[j % 2][:, 0:cols]).then_inc(h_hi, 1)
                    dve.wait_ge(h_hi, NJ * n + j + 1)
                    dve.tensor_tensor(hl[j % HRING][:, 0:cols], hid[j % 2][:, 0:cols], f32(hh[j % HRING][:, 0:cols]),
                                      ALU.subtract).then_inc(h_lo, 1)
                with dve.If(more > 0):
                    start(n + 1)
                dve.wait_ge(w2_done, C_W2 + NJ * n + NJ)
                dve.wait_ge(y_out, C_YO + 16 * n)
                dve.wait_ge(b2_in, 32)
                dve.tensor_tensor(y[:, 0:size, :], py[:, 0:size, :],
                                  b2[:, bass.ds(e * D, D)].unsqueeze(1).broadcast_to([P, size, D]),
                                  ALU.add).then_inc(y_copied, 1)

            start(0)
            over_units(dve, lambda n, size: by_size(dve, n, size, body))
            dve.wait_ge(res_in, 16 * RAW)
            dve.wait_ge(first_in, 16 * B)
            with dve.Fori(0, B // PLACES) as i:
                with dve.Fori(0, PLACES) as k:
                    b = PLACES * i + k
                    row = y0[:, bass.ds(b, 1), :].rearrange("p b d -> p (b d)")
                    dve.scalar_tensor_tensor(out=row, in0=row, scalar=w_all[:, bass.ds(E * b, 1)],
                                             in1=own[:, bass.ds(b, 1), :].rearrange("p b d -> p (b d)"),
                                             op0=ALU.mult, op1=ALU.add).then_inc(pair_step, 1)
                for k in range(PLACES):
                    b = PLACES * i + k
                    dve.wait_ge(pair_in[k], 16 * i + 16)
                    dve.wait_ge(pair_step, b + 1)
                    dve.scalar_tensor_tensor(out=y1[k], in0=y1[k], scalar=w_all[:, bass.ds(E * b + 1, 1)],
                                             in1=y0[:, bass.ds(b, 1), :].rearrange("p b d -> p (b d)"),
                                             op0=ALU.mult, op1=ALU.add).then_inc(pair_done, 1)

        @block.gpsimd
        def _(pool):
            pool.sem_inc(e_lo, C_LO)
            tie = pool.value_load(table[0:1, T_TIE:T_TIE + 1], min_val=0, max_val=1)
            total = pool.value_load(table[0:1, T_TOTAL:T_TOTAL + 1], min_val=1, max_val=NU)
            with pool.If(tie > 0):
                with pool.Fori(0, B) as b:
                    pool.dma_start(y1[0], A["xn2_d"][bass.ds(b, 1)].rearrange("b l d -> (b l) d")).then_inc(tie_in, 16)
                    pool.wait_ge(tie_in, 16 * (E - 1) * b + 16)
                    alone(pool, A["passed"])
                    pool.tensor_copy(tix[:, :], i_all[:, bass.ds(E * b, E)]).then_inc(tie_step, 1)
                    pool.wait_ge(tie_step, b + 1)
                    alone(pool, A["passed"])
                    for k in range(2, E):
                        pool.indirect_dma_start(A["slots"], bass.IndirectOffsetOnAxis(ap=tix[:, k:k + 1], axis=0), y1[0], None,
                                                bounds_check=E * ROWS - 1, oob_is_err=False).then_inc(tie_in, 16)
                        pool.wait_ge(tie_in, 16 * (E - 1) * b + 16 * k)
                        alone(pool, A["passed"])
            pool.sem_inc(dispatched, 1)


            def gather(dst, b, rank, arrived):
                pool.indirect_dma_start(dst, None, A["slots"],
                                        bass.IndirectOffsetOnAxis(ap=i_all[:, E * b + rank:E * b + rank + 1], axis=0),
                                        bounds_check=E * ROWS - 1, oob_is_err=False).then_inc(arrived, 16)

            def low(n, j):
                pool.wait_ge(e_hi, NJ * n + j + 1)
                pool.tensor_tensor(wl[j % RING][:, :, :], wraw[(j // 2) % RAW][:, :, j % 2, :], f32(wh[j % RING][:, :, :]),
                                   ALU.subtract).then_inc(e_lo, 1)

            def unit(n, size):
                more, row = following(pool, n), entry(pool, T_ROW, n, E * ROWS - SLOTS)
                for j in range(AHEAD, NJ):
                    low(n, j)
                    if j % 3 == 0:
                        with pool.If(more < 1):
                            if j == 6:
                                pool.wait_ge(y_out, C_YO + 16 * n)
                                alone(pool, A["passed"])
                            for b in range(B // 4 * (j // 3 - 2), B // 4 * (j // 3 - 1)):
                                gather(y0[:, b, :], b, 0, first_in)
                with pool.If(more > 0):
                    for j in range(AHEAD):
                        low(n + 1, j)
                pool.wait_ge(y_copied, C_YC + n + 1)
                alone(pool, A["passed"])
                by_size(pool, n, size, lambda n, k: pool.dma_start(
                    A["slots"][bass.ds(row, k * P), :].rearrange("(s p) d -> p s d", p=P), y[:, 0:k, :]).then_inc(y_out, 16))

            for j in range(AHEAD):
                low(0, j)
            pool.dma_start(b2[:, 2 * quarter:E * D], A["b2"][2 * quarter:E * D].partition_broadcast(P)).then_inc(y_out, 16)
            over_units(pool, unit)
            pool.wait_ge(y_out, C_YO + 16 * total)
            alone(pool, A["passed"])
            for b in range(B):
                if b >= PLACES:
                    pool.wait_ge(o_out[b % PLACES], 16 * (b // PLACES))
                gather(y1[b % PLACES], b, 1, pair_in[b % PLACES])
            with pool.If(tie > 0):
                for k in range(PLACES):
                    pool.wait_ge(o_out[k], 16 * (B // PLACES))
                    alone(pool, A["passed"])
                with pool.Fori(0, B) as b:
                    t_in, t_st = 16 * E * b + 16 * B * (E - 1), (3 * (E - 2) + 1) * b + B
                    pool.dma_start(y1[0], A["out"][bass.ds(b, 1)].rearrange("b l d -> (b l) d")).then_inc(tie_in, 16)
                    pool.wait_ge(tie_in, t_in + 16)
                    alone(pool, A["passed"])
                    pool.tensor_copy(tiw[:, :], w_all[:, bass.ds(E * b, E)])
                    pool.tensor_copy(tix[:, :], i_all[:, bass.ds(E * b, E)]).then_inc(tie_step, 1)
                    pool.wait_ge(tie_step, t_st + 1)
                    alone(pool, A["passed"])
                    for k in range(2, E):
                        pool.memset(y1[1], 0.0).then_inc(tie_step, 1)
                        pool.wait_ge(tie_step, t_st + 3 * (k - 2) + 2)
                        alone(pool, A["passed"])
                        pool.indirect_dma_start(y1[1], None, A["slots"], bass.IndirectOffsetOnAxis(ap=tix[:, k:k + 1], axis=0),
                                                bounds_check=E * ROWS - 1, oob_is_err=False).then_inc(tie_in, 16)
                        pool.wait_ge(tie_in, t_in + 16 * k)
                        alone(pool, A["passed"])
                        pool.tensor_scalar(y1[1], y1[1], tiw[:, k:k + 1], None, ALU.mult).then_inc(tie_step, 1)
                        pool.wait_ge(tie_step, t_st + 3 * (k - 2) + 3)
                        alone(pool, A["passed"])
                        pool.tensor_tensor(y1[0], y1[0], y1[1], ALU.add).then_inc(tie_step, 1)
                        pool.wait_ge(tie_step, t_st + 3 * (k - 2) + 4)
                        alone(pool, A["passed"])
                    pool.dma_start(A["out"][bass.ds(b, 1)].rearrange("b l d -> (b l) d"), y1[0]).then_inc(tie_in, 16)
                    pool.wait_ge(tie_in, t_in + 16 * E)
                    alone(pool, A["passed"])
            pool.nop()


def gated_block(nc, A):
    A["slots"] = nc.dram_tensor("expert_slots", [E * ROWS, D], F32, kind="Internal").ap()
    A["x1_d"] = nc.dram_tensor("after_attention", [B, LQ, D], F32, kind="Internal").ap()
    A["xn2_d"] = nc.dram_tensor("normalised", [B, LQ, D], F32, kind="Internal").ap()
    with ExitStack() as ctx:
        A["w_all"] = ctx.enter_context(nc.sbuf_tensor("w_all", [LQ, B * E], F32))
        A["i_all"] = ctx.enter_context(nc.sbuf_tensor("i_all", [LQ, B * E], I32))
        A["table"] = ctx.enter_context(nc.sbuf_tensor("table", [1, T_TOTAL + 1], I32))
        A["zero"] = ctx.enter_context(nc.sbuf_tensor("zero", [P, D], F32))
        A["passed"] = ctx.enter_context(nc.semaphore("passed"))
        attention_phase(nc, A)
        expert_phase(nc, A)


def unit_constants(np):
    sizes = np.array([unit_sizes(c) for c in range(CHUNKS + 1)])
    starts = np.cumsum(sizes, 1) - sizes
    starts[sizes == 0] = 0
    row = np.concatenate([
        np.tile(np.arange(CHUNKS) * P, NU),
        np.tile(np.diff(sizes, axis=0).T.reshape(-1), E),
        np.tile(np.diff(starts, axis=0).T.reshape(-1) * P, E),
        np.add.outer(np.arange(E) * ROWS, np.zeros(ROUNDS)).reshape(-1),
        np.repeat(np.arange(E), ROUNDS)])
    return np.concatenate([np.tile(row, (NU, 1)), np.arange(1, NU + 1)[:, None]], 1).astype(np.float32)


def kernel(x, ctx_1024, mask_Bx1x1xS2_bf0, g_xattn, g_ffn, L0_xattn_W_q, L0_xattn_b_q, L0_xattn_W_k, L0_xattn_b_k,
           L0_xattn_W_v, L0_xattn_b_v, L0_xattn_W_o, L0_xattn_b_o, L0_ffn_W1, L0_ffn_b1, L0_ffn_W2, L0_ffn_b2,
           L0_ffn_Wr, L0_ffn_br):
    import numpy as np
    import concourse.bacc as bacc
    from concourse.bass_utils import run_bass_kernel_spmd

    def rows(a):
        return np.asarray(a).T.reshape(DC, P, -1).transpose(1, 0, 2)

    def columns(a):
        return np.asarray(a).reshape(DC, P).T

    mask = np.pad(np.asarray(mask_Bx1x1xS2_bf0).reshape(B, S), ((0, 0), (0, SP_ - S)), constant_values=True)
    arrays = {
        "x": np.asarray(x),
        "ctx": np.asarray(ctx_1024).transpose(0, 2, 1).reshape(B, DC, P, S).transpose(0, 2, 1, 3),
        "mrow": mask,
        "mkey": mask.reshape(B, NT, KT).transpose(2, 0, 1).reshape(KT, B * NT),
        "gx": np.asarray(g_xattn), "gf": np.asarray(g_ffn),
        "wq": rows(L0_xattn_W_q), "wk": rows(L0_xattn_W_k), "wv": rows(L0_xattn_W_v), "wo": rows(L0_xattn_W_o),
        "bq": columns(L0_xattn_b_q), "bk": columns(L0_xattn_b_k), "bv": columns(L0_xattn_b_v),
        "bo": np.asarray(L0_xattn_b_o),
        "wr": np.asarray(L0_ffn_Wr).reshape(DC, P, E).transpose(1, 0, 2), "br": np.asarray(L0_ffn_br),
        "W1": np.asarray(L0_ffn_W1).reshape(E, DC, P, NJ, P).transpose(0, 2, 3, 1, 4).reshape(E, P, NJ, D),
        "W2": np.asarray(L0_ffn_W2).reshape(E, NJ, P, D).transpose(0, 2, 1, 3),
        "b1": np.asarray(L0_ffn_b1).reshape(E, NJ, P).transpose(0, 2, 1),
        "b2": np.asarray(L0_ffn_b2).reshape(E * D),
        "ident": np.eye(P, dtype=np.float32),
        "tri": np.triu(np.ones((LQ, LQ), np.float32), 1),
        "blockm": np.repeat(np.repeat(np.eye(GH, dtype=np.float32), DK, 0)[:, :, None], LQ, 2),
        "rankc": np.broadcast_to(np.arange(1, E + 1, dtype=np.float32)[None, :, None], (LQ, E, E)),
        "rankv": np.broadcast_to(np.arange(1, E + 1, dtype=np.float32)[None, :], (LQ, E)),
        "rowbase": np.broadcast_to(np.arange(E, dtype=np.float32)[None, :] * ROWS, (LQ, E)),
"units": unit_constants(np),
    }
    nc = bacc.Bacc("TRN2", target_bir_lowering=False, num_devices=1)
    feeds, aps = {}, {}
    for name, a in arrays.items():
        a = np.ascontiguousarray(a)
        feeds[f"in_{name}"] = a
        aps[name] = nc.dram_tensor(f"in_{name}", a.shape, mybir.dt.from_np(a.dtype), kind="ExternalInput").ap()
    aps["out"] = nc.dram_tensor("out", (B, LQ, D), F32, kind="ExternalOutput").ap()
    gated_block(nc, aps)
    result = run_bass_kernel_spmd(nc, [feeds], core_ids=[0])
    return result.results[0]["out"]
```
